# Optimizing a Trainium2 kernel written in Bass

```python
import numpy as np
import jax
import jax.numpy as jnp

def _softmax(x, axis=-1):
    return jax.nn.softmax(x, axis=axis)

def _gelu(x):
    return jax.nn.gelu(x, approximate=True)

def _silu(x):
    return jax.nn.silu(x)

def _sigmoid(x):
    return jax.nn.sigmoid(x)

def _layernorm(x, axis=-1, eps=1e-05):
    m = jnp.mean(x, axis=axis, keepdims=True)
    v = jnp.var(x, axis=axis, keepdims=True)
    return (x - m) / jnp.sqrt(v + eps)

def _scatter_add(tgt, idx, src, axis=0):
    return tgt.at[idx].add(src)

def _segment_sum(src, seg, n):
    return jax.ops.segment_sum(src, seg, n)
kernel_name = 'mk_conv_seq_d2_conv_nchw384_r2_5b8438'

def setup_inputs(seed: int=0):
    np.random.seed(seed)
    _w = jnp.asarray

    def _rec_inputs():
        import jax
        import jax.numpy as jnp
        _gk = jax.random.key(seed)
        x = -0.000357 + 1 * jax.random.normal(jax.random.fold_in(_gk, 1), (16, 192, 56, 56), jnp.float32)
        return x
    x = _rec_inputs()

    def _L0_conv_setup():
        import jax, jax.numpy as jnp
        import numpy as np
        C = 192
        K = 13
        EPS = 1e-05

        def bn(y, g, b, m, v):
            scale = (g / jnp.sqrt(v + EPS)).reshape(1, -1, 1, 1)
            shift = (b - m * g / jnp.sqrt(v + EPS)).reshape(1, -1, 1, 1)
            return y * scale + shift

        def dwconv(x, w):
            p = w.shape[-1] // 2
            return jax.lax.conv_general_dilated(x, w, window_strides=(1, 1), padding=[(p, p), (p, p)], dimension_numbers=('NCHW', 'OIHW', 'NCHW'), feature_group_count=x.shape[1])
        key = jax.random.key(seed)
        ks = jax.random.split(key, 16)
        f32 = jnp.float32
        inp = {'x': jax.random.normal(ks[0], (16, C, 56, 56), dtype=f32), 'pw_w': jax.random.normal(ks[1], (C, C), dtype=f32) * 0.05, 'pw_g': jax.random.uniform(ks[2], (C,), dtype=f32) + 0.5, 'pw_b': jax.random.normal(ks[3], (C,), dtype=f32) * 0.1, 'pw_m': jax.random.normal(ks[4], (C,), dtype=f32) * 0.1, 'pw_v': jax.random.uniform(ks[5], (C,), dtype=f32) + 0.5, 'dwk_w': jax.random.normal(ks[6], (C, 1, K, K), dtype=f32) * 0.05, 'dwk_g': jax.random.uniform(ks[7], (C,), dtype=f32) + 0.5, 'dwk_b': jax.random.normal(ks[8], (C,), dtype=f32) * 0.1, 'dwk_m': jax.random.normal(ks[9], (C,), dtype=f32) * 0.1, 'dwk_v': jax.random.uniform(ks[10], (C,), dtype=f32) + 0.5, 'dw1_w': jax.random.normal(ks[11], (C,), dtype=f32) * 0.5, 'dw1_g': jax.random.uniform(ks[12], (C,), dtype=f32) + 0.5, 'dw1_b': jax.random.normal(ks[13], (C,), dtype=f32) * 0.1, 'dw1_m': jax.random.normal(ks[14], (C,), dtype=f32) * 0.1, 'dw1_v': jax.random.uniform(ks[15], (C,), dtype=f32) + 0.5}
        return inp
    _L0_conv_all = _L0_conv_setup()
    _L0_conv_in = {k: v for k, v in _L0_conv_all.items() if k in ('pw_w', 'pw_g', 'pw_b', 'pw_m', 'pw_v', 'dwk_w', 'dwk_g', 'dwk_b', 'dwk_m', 'dwk_v', 'dw1_w', 'dw1_g', 'dw1_b', 'dw1_m', 'dw1_v')}
    del _L0_conv_all

    def _L1_conv_setup():
        import jax, jax.numpy as jnp
        import numpy as np

        def _ln(x, g, b):
            m = x.mean(-1, keepdims=True)
            v = x.var(-1, keepdims=True)
            return (x - m) / jnp.sqrt(v + 1e-05) * g + b

        def _dw(x, w):
            return jax.lax.conv_general_dilated(x, w, (1, 1), 'SAME', dimension_numbers=('NCHW', 'OIHW', 'NCHW'), feature_group_count=x.shape[1])

        def _omni(x, a, w1, w3, w5):
            return a[0] * x + a[1] * _dw(x, w1) + a[2] * _dw(x, w3) + a[3] * _dw(x, w5)

        def _wkv(w, u, k, v):
            B, T, C = k.shape

            def step(carry, kv_t):
                p, q, o = carry
                kt, vt = kv_t
                no = jnp.maximum(o, u + kt)
                A = jnp.exp(o - no)
                Bc = jnp.exp(u + kt - no)
                y = (A * p + Bc * vt) / (A * q + Bc)
                no2 = jnp.maximum(w + o, kt)
                A2 = jnp.exp(w + o - no2)
                B2 = jnp.exp(kt - no2)
                return ((A2 * p + B2 * vt, A2 * q + B2, no2), y)
            init = (jnp.zeros((B, C), k.dtype), jnp.zeros((B, C), k.dtype), jnp.full((B, C), -1e+30, k.dtype))
            _, ys = jax.lax.scan(step, init, (jnp.swapaxes(k, 0, 1), jnp.swapaxes(v, 0, 1)))
            return jnp.swapaxes(ys, 0, 1)

        def _block(x, ln1_g, ln1_b, ln2_g, ln2_b, gamma1, gamma2, att_alpha, att_w1, att_w3, att_w5, att_wk, att_wv, att_wr, att_wo, sp_decay, sp_first, ffn_alpha, ffn_w1, ffn_w3, ffn_w5, ffn_wk, ffn_wv, ffn_wr):
            B, C, H, W = x.shape
            T = H * W
            tok = x.reshape(B, C, T).transpose(0, 2, 1)
            xs = _ln(tok, ln1_g, ln1_b)
            xi = _omni(xs.transpose(0, 2, 1).reshape(B, C, H, W), att_alpha, att_w1, att_w3, att_w5)
            xs2 = xi.reshape(B, C, T).transpose(0, 2, 1)
            k = xs2 @ att_wk.T
            v = xs2 @ att_wv.T
            sr = jax.nn.sigmoid(xs2 @ att_wr.T)
            v = _wkv(sp_decay[0] / T, sp_first[0] / T, k, v)
            k2 = k.reshape(B, H, W, C).transpose(0, 2, 1, 3).reshape(B, T, C)
            v2 = v.reshape(B, H, W, C).transpose(0, 2, 1, 3).reshape(B, T, C)
            v2 = _wkv(sp_decay[1] / T, sp_first[1] / T, k2, v2)
            v = v2.reshape(B, W, H, C).transpose(0, 2, 1, 3).reshape(B, T, C)
            att_out = sr * v @ att_wo.T
            tok = tok + gamma1 * att_out
            xf = _ln(tok, ln2_g, ln2_b)
            xi = _omni(xf.transpose(0, 2, 1).reshape(B, C, H, W), ffn_alpha, ffn_w1, ffn_w3, ffn_w5)
            xf2 = xi.reshape(B, C, T).transpose(0, 2, 1)
            kk = jnp.square(jax.nn.relu(xf2 @ ffn_wk.T))
            kv = kk @ ffn_wv.T
            ffn_out = jax.nn.sigmoid(xf2 @ ffn_wr.T) * kv
            tok = tok + gamma2 * ffn_out
            return tok.transpose(0, 2, 1).reshape(B, C, H, W)
        key = jax.random.key(seed)
        B, C, H, W = (8, 192, 32, 32)
        hid = 4 * C
        ks = iter(jax.random.split(key, 32))

        def nrm(shape, scale=1.0):
            return jax.random.normal(next(ks), shape, dtype=jnp.float32) * scale
        s = 1.0 / float(np.sqrt(C))
        sh = 1.0 / float(np.sqrt(hid))
        return dict(x=nrm((B, C, H, W)), ln1_g=jnp.ones(C, jnp.float32), ln1_b=jnp.zeros(C, jnp.float32), ln2_g=jnp.ones(C, jnp.float32), ln2_b=jnp.zeros(C, jnp.float32), gamma1=jnp.ones(C, jnp.float32), gamma2=jnp.ones(C, jnp.float32), att_alpha=nrm((4,), 0.5), att_w1=nrm((C, 1, 1, 1), 0.3), att_w3=nrm((C, 1, 3, 3), 0.1), att_w5=nrm((C, 1, 5, 5), 0.05), att_wk=nrm((C, C), s), att_wv=nrm((C, C), s), att_wr=nrm((C, C), s), att_wo=nrm((C, C), s), sp_decay=nrm((2, C)), sp_first=nrm((2, C)), ffn_alpha=nrm((4,), 0.5), ffn_w1=nrm((C, 1, 1, 1), 0.3), ffn_w3=nrm((C, 1, 3, 3), 0.1), ffn_w5=nrm((C, 1, 5, 5), 0.05), ffn_wk=nrm((hid, C), s), ffn_wv=nrm((C, hid), sh), ffn_wr=nrm((C, C), s))
    _L1_conv_all = _L1_conv_setup()
    _L1_conv_in = {k: v for k, v in _L1_conv_all.items() if k in ('ln1_g', 'ln1_b', 'ln2_g', 'ln2_b', 'gamma1', 'gamma2', 'att_alpha', 'att_w1', 'att_w3', 'att_w5', 'att_wk', 'att_wv', 'att_wr', 'att_wo', 'sp_decay', 'sp_first', 'ffn_alpha', 'ffn_w1', 'ffn_w3', 'ffn_w5', 'ffn_wk', 'ffn_wv', 'ffn_wr')}
    del _L1_conv_all
    return {'x': x, 'L0_conv_pw_w': _L0_conv_in['pw_w'], 'L0_conv_pw_g': _L0_conv_in['pw_g'], 'L0_conv_pw_b': _L0_conv_in['pw_b'], 'L0_conv_pw_m': _L0_conv_in['pw_m'], 'L0_conv_pw_v': _L0_conv_in['pw_v'], 'L0_conv_dwk_w': _L0_conv_in['dwk_w'], 'L0_conv_dwk_g': _L0_conv_in['dwk_g'], 'L0_conv_dwk_b': _L0_conv_in['dwk_b'], 'L0_conv_dwk_m': _L0_conv_in['dwk_m'], 'L0_conv_dwk_v': _L0_conv_in['dwk_v'], 'L0_conv_dw1_w': _L0_conv_in['dw1_w'], 'L0_conv_dw1_g': _L0_conv_in['dw1_g'], 'L0_conv_dw1_b': _L0_conv_in['dw1_b'], 'L0_conv_dw1_m': _L0_conv_in['dw1_m'], 'L0_conv_dw1_v': _L0_conv_in['dw1_v'], 'L1_conv_ln1_g': _L1_conv_in['ln1_g'], 'L1_conv_ln1_b': _L1_conv_in['ln1_b'], 'L1_conv_ln2_g': _L1_conv_in['ln2_g'], 'L1_conv_ln2_b': _L1_conv_in['ln2_b'], 'L1_conv_gamma1': _L1_conv_in['gamma1'], 'L1_conv_gamma2': _L1_conv_in['gamma2'], 'L1_conv_att_alpha': _L1_conv_in['att_alpha'], 'L1_conv_att_w1': _L1_conv_in['att_w1'], 'L1_conv_att_w3': _L1_conv_in['att_w3'], 'L1_conv_att_w5': _L1_conv_in['att_w5'], 'L1_conv_att_wk': _L1_conv_in['att_wk'], 'L1_conv_att_wv': _L1_conv_in['att_wv'], 'L1_conv_att_wr': _L1_conv_in['att_wr'], 'L1_conv_att_wo': _L1_conv_in['att_wo'], 'L1_conv_sp_decay': _L1_conv_in['sp_decay'], 'L1_conv_sp_first': _L1_conv_in['sp_first'], 'L1_conv_ffn_alpha': _L1_conv_in['ffn_alpha'], 'L1_conv_ffn_w1': _L1_conv_in['ffn_w1'], 'L1_conv_ffn_w3': _L1_conv_in['ffn_w3'], 'L1_conv_ffn_w5': _L1_conv_in['ffn_w5'], 'L1_conv_ffn_wk': _L1_conv_in['ffn_wk'], 'L1_conv_ffn_wv': _L1_conv_in['ffn_wv'], 'L1_conv_ffn_wr': _L1_conv_in['ffn_wr']}

def reference(x, L0_conv_pw_w, L0_conv_pw_g, L0_conv_pw_b, L0_conv_pw_m, L0_conv_pw_v, L0_conv_dwk_w, L0_conv_dwk_g, L0_conv_dwk_b, L0_conv_dwk_m, L0_conv_dwk_v, L0_conv_dw1_w, L0_conv_dw1_g, L0_conv_dw1_b, L0_conv_dw1_m, L0_conv_dw1_v, L1_conv_ln1_g, L1_conv_ln1_b, L1_conv_ln2_g, L1_conv_ln2_b, L1_conv_gamma1, L1_conv_gamma2, L1_conv_att_alpha, L1_conv_att_w1, L1_conv_att_w3, L1_conv_att_w5, L1_conv_att_wk, L1_conv_att_wv, L1_conv_att_wr, L1_conv_att_wo, L1_conv_sp_decay, L1_conv_sp_first, L1_conv_ffn_alpha, L1_conv_ffn_w1, L1_conv_ffn_w3, L1_conv_ffn_w5, L1_conv_ffn_wk, L1_conv_ffn_wv, L1_conv_ffn_wr):
    import jax
    import jax.numpy as jnp

    def _L0_conv_ref(x, pw_w, pw_g, pw_b, pw_m, pw_v, dwk_w, dwk_g, dwk_b, dwk_m, dwk_v, dw1_w, dw1_g, dw1_b, dw1_m, dw1_v):
        import jax, jax.numpy as jnp
        import numpy as np
        C = 192
        K = 13
        EPS = 1e-05

        def bn(y, g, b, m, v):
            scale = (g / jnp.sqrt(v + EPS)).reshape(1, -1, 1, 1)
            shift = (b - m * g / jnp.sqrt(v + EPS)).reshape(1, -1, 1, 1)
            return y * scale + shift

        def dwconv(x, w):
            p = w.shape[-1] // 2
            return jax.lax.conv_general_dilated(x, w, window_strides=(1, 1), padding=[(p, p), (p, p)], dimension_numbers=('NCHW', 'OIHW', 'NCHW'), feature_group_count=x.shape[1])
        y = jnp.einsum('bchw,oc->bohw', x, pw_w)
        x_pw = bn(y, pw_g, pw_b, pw_m, pw_v) + x
        out = bn(dwconv(x_pw, dwk_w), dwk_g, dwk_b, dwk_m, dwk_v)
        out = out + bn(x_pw * dw1_w.reshape(1, -1, 1, 1), dw1_g, dw1_b, dw1_m, dw1_v)
        return jax.nn.gelu(out, approximate=False)

    def _L1_conv_ref(x, ln1_g, ln1_b, ln2_g, ln2_b, gamma1, gamma2, att_alpha, att_w1, att_w3, att_w5, att_wk, att_wv, att_wr, att_wo, sp_decay, sp_first, ffn_alpha, ffn_w1, ffn_w3, ffn_w5, ffn_wk, ffn_wv, ffn_wr):
        import jax, jax.numpy as jnp
        import numpy as np

        def _ln(x, g, b):
            m = x.mean(-1, keepdims=True)
            v = x.var(-1, keepdims=True)
            return (x - m) / jnp.sqrt(v + 1e-05) * g + b

        def _dw(x, w):
            return jax.lax.conv_general_dilated(x, w, (1, 1), 'SAME', dimension_numbers=('NCHW', 'OIHW', 'NCHW'), feature_group_count=x.shape[1])

        def _omni(x, a, w1, w3, w5):
            return a[0] * x + a[1] * _dw(x, w1) + a[2] * _dw(x, w3) + a[3] * _dw(x, w5)

        def _wkv(w, u, k, v):
            B, T, C = k.shape

            def step(carry, kv_t):
                p, q, o = carry
                kt, vt = kv_t
                no = jnp.maximum(o, u + kt)
                A = jnp.exp(o - no)
                Bc = jnp.exp(u + kt - no)
                y = (A * p + Bc * vt) / (A * q + Bc)
                no2 = jnp.maximum(w + o, kt)
                A2 = jnp.exp(w + o - no2)
                B2 = jnp.exp(kt - no2)
                return ((A2 * p + B2 * vt, A2 * q + B2, no2), y)
            init = (jnp.zeros((B, C), k.dtype), jnp.zeros((B, C), k.dtype), jnp.full((B, C), -1e+30, k.dtype))
            _, ys = jax.lax.scan(step, init, (jnp.swapaxes(k, 0, 1), jnp.swapaxes(v, 0, 1)))
            return jnp.swapaxes(ys, 0, 1)

        def _block(x, ln1_g, ln1_b, ln2_g, ln2_b, gamma1, gamma2, att_alpha, att_w1, att_w3, att_w5, att_wk, att_wv, att_wr, att_wo, sp_decay, sp_first, ffn_alpha, ffn_w1, ffn_w3, ffn_w5, ffn_wk, ffn_wv, ffn_wr):
            B, C, H, W = x.shape
            T = H * W
            tok = x.reshape(B, C, T).transpose(0, 2, 1)
            xs = _ln(tok, ln1_g, ln1_b)
            xi = _omni(xs.transpose(0, 2, 1).reshape(B, C, H, W), att_alpha, att_w1, att_w3, att_w5)
            xs2 = xi.reshape(B, C, T).transpose(0, 2, 1)
            k = xs2 @ att_wk.T
            v = xs2 @ att_wv.T
            sr = jax.nn.sigmoid(xs2 @ att_wr.T)
            v = _wkv(sp_decay[0] / T, sp_first[0] / T, k, v)
            k2 = k.reshape(B, H, W, C).transpose(0, 2, 1, 3).reshape(B, T, C)
            v2 = v.reshape(B, H, W, C).transpose(0, 2, 1, 3).reshape(B, T, C)
            v2 = _wkv(sp_decay[1] / T, sp_first[1] / T, k2, v2)
            v = v2.reshape(B, W, H, C).transpose(0, 2, 1, 3).reshape(B, T, C)
            att_out = sr * v @ att_wo.T
            tok = tok + gamma1 * att_out
            xf = _ln(tok, ln2_g, ln2_b)
            xi = _omni(xf.transpose(0, 2, 1).reshape(B, C, H, W), ffn_alpha, ffn_w1, ffn_w3, ffn_w5)
            xf2 = xi.reshape(B, C, T).transpose(0, 2, 1)
            kk = jnp.square(jax.nn.relu(xf2 @ ffn_wk.T))
            kv = kk @ ffn_wv.T
            ffn_out = jax.nn.sigmoid(xf2 @ ffn_wr.T) * kv
            tok = tok + gamma2 * ffn_out
            return tok.transpose(0, 2, 1).reshape(B, C, H, W)
        return _block(x, ln1_g, ln1_b, ln2_g, ln2_b, gamma1, gamma2, att_alpha, att_w1, att_w3, att_w5, att_wk, att_wv, att_wr, att_wo, sp_decay, sp_first, ffn_alpha, ffn_w1, ffn_w3, ffn_w5, ffn_wk, ffn_wv, ffn_wr)

    def _gn(v, G=32, eps=1e-05):
        B_, C_, H_, W_ = v.shape
        g = v.reshape(B_, G, C_ // G, H_, W_)
        m = jnp.mean(g, axis=(2, 3, 4), keepdims=True)
        s = jnp.var(g, axis=(2, 3, 4), keepdims=True)
        return ((g - m) / jnp.sqrt(s + eps)).reshape(v.shape)

    def _ln_c(v, eps=1e-06):
        m = jnp.mean(v, axis=1, keepdims=True)
        s = jnp.var(v, axis=1, keepdims=True)
        return (v - m) / jnp.sqrt(s + eps)

    def _ln_t(v, eps=1e-05):
        m = jnp.mean(v, axis=-1, keepdims=True)
        s = jnp.var(v, axis=-1, keepdims=True)
        return (v - m) / jnp.sqrt(s + eps)

    def _to_tokens(v):
        B_, C_, H_, W_ = v.shape
        return v.reshape(B_, C_, H_ * W_).transpose(0, 2, 1)

    def _from_tokens(t, like):
        B_, C_, H_, W_ = like.shape
        return t.transpose(0, 2, 1).reshape(B_, C_, H_, W_)
    x = _L0_conv_ref(x, L0_conv_pw_w, L0_conv_pw_g, L0_conv_pw_b, L0_conv_pw_m, L0_conv_pw_v, L0_conv_dwk_w, L0_conv_dwk_g, L0_conv_dwk_b, L0_conv_dwk_m, L0_conv_dwk_v, L0_conv_dw1_w, L0_conv_dw1_g, L0_conv_dw1_b, L0_conv_dw1_m, L0_conv_dw1_v)
    x = _L1_conv_ref(x, L1_conv_ln1_g, L1_conv_ln1_b, L1_conv_ln2_g, L1_conv_ln2_b, L1_conv_gamma1, L1_conv_gamma2, L1_conv_att_alpha, L1_conv_att_w1, L1_conv_att_w3, L1_conv_att_w5, L1_conv_att_wk, L1_conv_att_wv, L1_conv_att_wr, L1_conv_att_wo, L1_conv_sp_decay, L1_conv_sp_first, L1_conv_ffn_alpha, L1_conv_ffn_w1, L1_conv_ffn_w3, L1_conv_ffn_w5, L1_conv_ffn_wk, L1_conv_ffn_wv, L1_conv_ffn_wr)
    return x

_drawn_inputs = setup_inputs


def setup_inputs(seed=0):
    import zlib

    import numpy as np

    out = dict(_drawn_inputs(seed))
    spreads = {'L1_conv_ln1_g': (1.0, 0.2),
     'L1_conv_ln1_b': (0.0, 0.1),
     'L1_conv_ln2_g': (1.0, 0.6),
     'L1_conv_ln2_b': (0.0, 0.8),
     'L1_conv_gamma1': (1.0, 0.2),
     'L1_conv_gamma2': (1.0, 0.6)}
    factors = {'L1_conv_att_w3': 7.208,
     'L1_conv_att_w5': 5.822,
     'L1_conv_sp_decay': 8.0,
     'L1_conv_sp_first': 8.0,
     'L1_conv_ffn_w1': 8.0,
     'L1_conv_ffn_w3': 8.0,
     'L1_conv_ffn_wr': 8.0}
    for name, (base, spread) in spreads.items():
        noise = np.random.default_rng([zlib.crc32(name.encode()), seed]).standard_normal(out[name].shape)
        drawn = base * np.exp(spread * noise) if base else spread * noise
        out[name] = jnp.asarray(drawn.astype(out[name].dtype))
    for name, factor in factors.items():
        out[name] = (out[name] * factor).astype(out[name].dtype)
    return out
```

```python
from contextlib import ExitStack

import concourse.bass as bass
from concourse import mybir

F32 = mybir.dt.float32
ALU = mybir.AluOpType
ACT = mybir.ActivationFunctionType
AX_X = mybir.AxisListType.X

C = 192
W = 56
HW = W * W
CT = 96
KT = C // CT
HID = 4 * C
HT = HID // 128
G = 8
NG = C // G
PJ = W // 2
K13, K5, K3 = 13, 5, 3
PITCH = 62
PXC = 2 * W
PXP = PITCH + W
JC = 4
NCH = PJ // JC
TC = JC * PXC
HALF = HW // 2
LN_EPS = 1e-5
BN_EPS = 1e-5
NEG = -1e30

VEC = ["pw_v", "dwk_v", "dw1_v", "pw_g", "dwk_g", "dw1_g", "pw_b", "dwk_b", "dw1_b",
       "pw_m", "dwk_m", "dw1_m", "dw1_w", "ln1_g", "ln1_b", "ln2_g", "ln2_b", "gamma1", "gamma2",
       "dec0", "dec1", "first0", "first1"]
NV = len(VEC)
V = {n: i for i, n in enumerate(VEC)}


def band(k):
    dmax = (k // 2 + 1) // 2
    centre = 2 * PITCH * dmax + PXP - 1
    return dmax, centre, 2 * centre + 2, 2 * PITCH * 2 * dmax + PXP


def free(ap, pattern, offset=0):
    return bass.AP(ap.tensor, ap.offset + offset, [list(ap.ap[0])] + pattern)


def dram(t, offset, pattern):
    return bass.AP(t.tensor, offset, pattern)


def taps_view(ap, k, centre):
    return free(ap, [[PITCH, k], [1, k]], centre - (k // 2) * (PITCH + 1))


class Mem:
    def __init__(self, nc, ctx):
        self.nc, self.ctx = nc, ctx

    def sb(self, name, shape, dt=F32):
        return self.ctx.enter_context(self.nc.sbuf_tensor(name, shape, dt))

    def ps(self, name, shape=(128, 512)):
        return self.ctx.enter_context(self.nc.psum_tensor(name, list(shape), F32))

    def sem(self, name):
        return self.ctx.enter_context(self.nc.semaphore(name))


def pair_batch(t, B, b, offset=None):
    row = B * G * PJ
    return dram(t, b * G * PJ if offset is None else offset, [[row, PXC], [PXC * row, NG], [1, G * PJ]])


def pair_group(t, B, g):
    row = B * G * PJ
    return dram(t, g * PXC * row, [[row, PXC], [1, row]])


def copy_pairs(eng, to, of, signal):
    for r in range(2):
        tile, rest = slice(r * PITCH, r * PITCH + W), r * W
        part = []
        for ap in (to, of):
            dims = [list(d) for d in ap.ap]
            if dims[0][1] == PXP:
                part.append(ap[tile])
            else:
                part.append(bass.AP(ap.tensor, ap.offset + rest * dims[0][0], [[dims[0][0], W]] + dims[1:]))
        eng.dma_start(part[0], part[1]).then_inc(signal, 16)


def by_group(t):
    return t[:, :, :].rearrange("p (g c) j -> p g (c j)", g=NG)


def prepare(nc, ins, keep, f13_d, f5a_d, f5f_d, bias_d):
    with ExitStack() as ctx:
        m = Mem(nc, ctx)
        bcv = m.sb("bcv", [128, NV, C])
        colv = m.sb("colv", [CT, KT, NV])
        alph = m.sb("alph", [CT, 8])
        dwk = m.sb("dwk", [CT, KT, K13 * K13])
        w5 = m.sb("w5", [CT, 2, KT, K5 * K5])
        w3 = m.sb("w3", [CT, 2, KT, K3 * K3])
        w1 = m.sb("w1", [CT, 2, KT])
        _, c13, l13, _ = band(K13)
        _, c5, l5, _ = band(K5)
        f13 = m.sb("f13", [CT, KT, l13])
        f5 = m.sb("f5", [CT, 2, KT, l5])
        sd = m.sb("sd", [128, 3, C])
        sc = m.sb("sc", [128, 3, C])
        sh = m.sb("sh", [128, 3, C])
        cd = m.sb("cd", [CT, KT, 3])
        cs = m.sb("cs", [CT, KT, 3])
        c1 = m.sb("c1", [CT, KT])
        uw = m.sb("uw", [CT, KT, 2])
        loads = m.sem("prep_loaded")
        var_ready = m.sem("prep_variances")
        root = m.sem("prep_roots")
        step = m.sem("prep_steps")
        expo = m.sem("prep_exponentials")
        stored = m.sem("prep_stored")
        block = ctx.enter_context(nc.Block())
        folds = [0]

        @block.sync
        def _(sp):
            n = 0
            vecs = ins["vecs"]
            for dst, src in [
                (bcv[:, :, :], dram(vecs, 0, [[0, 128], [1, NV * C]])),
                (colv[:, :, :], ins["vec_cols"]),
                (alph[:, :], dram(ins["alphas"], 0, [[0, CT], [1, 8]])),
                (keep.ident[:, :], ins["ident"]),
                (keep.wpw[:, :, :], ins["pw_wt"].rearrange("(k p) n -> p k n", p=CT)),
                *[(keep.wkvr[:, :, o, :], ins["att_wt"][o].rearrange("(k p) n -> p k n", p=CT))
                  for o in range(3)],
                (keep.wo[:, :, :], ins["att_wot"].rearrange("(k p) n -> p k n", p=CT)),
                (dwk[:, :, :], ins["dwk_w"].rearrange("(k p) n -> p k n", p=CT)),
                (w5[:, 0], ins["att_w5"].rearrange("(k p) n -> p k n", p=CT)),
                (w5[:, 1], ins["ffn_w5"].rearrange("(k p) n -> p k n", p=CT)),
                (w3[:, 0], ins["att_w3"].rearrange("(k p) n -> p k n", p=CT)),
                (w3[:, 1], ins["ffn_w3"].rearrange("(k p) n -> p k n", p=CT)),
                (w1[:, 0], ins["att_w1"]),
                (w1[:, 1], ins["ffn_w1"]),
            ]:
                sp.dma_start(dst, src).then_inc(loads, 16)
                n += 16
            folds[0] = n

        @block.vector
        def _(dve):
            done = [0]

            def link(ins_):
                done[0] += 1
                ins_.then_inc(step, 1)
                dve.wait_ge(step, done[0])

            link(dve.memset(f13[:, :, :], 0.0))
            link(dve.memset(f5[:, :, :, :], 0.0))
            dve.wait_ge(loads, folds[0])
            dve.tensor_scalar_add(sd[:, :, :], bcv[:, 0:3, :], BN_EPS).then_inc(var_ready, 1)
            dve.tensor_scalar_add(cd[:, :, :], colv[:, :, 0:3], BN_EPS).then_inc(var_ready, 1)
            link(dve.tensor_scalar_mul(keep.decay[:, :, :], colv[:, :, V["dec0"]:V["dec0"] + 2], 1.0 / HW))
            dve.scalar_tensor_tensor(uw[:, :, :], colv[:, :, V["first0"]:V["first0"] + 2], 1.0 / HW,
                                     keep.decay[:, :, :], ALU.mult, ALU.add).then_inc(var_ready, 1)
            dve.wait_ge(root, 2)
            link(dve.reciprocal(sd[:, :, :], sd[:, :, :]))
            link(dve.tensor_mul(sc[:, :, :], bcv[:, 3:6, :], sd[:, :, :]))
            link(dve.tensor_mul(sh[:, :, :], bcv[:, 9:12, :], sc[:, :, :]))
            link(dve.tensor_sub(sh[:, :, :], bcv[:, 6:9, :], sh[:, :, :]))
            link(dve.tensor_copy(keep.shift_pw[:, :], sh[:, 0, :]))
            link(dve.tensor_add(sd[:, 0, :], sh[:, 1, :], sh[:, 2, :]))
            for k in range(KT):
                link(dve.tensor_mul(keep.wpw[:, k, :], keep.wpw[:, k, :], sc[0:CT, 0, :]))
                own = keep.wpw[:, k, k * CT:(k + 1) * CT]
                link(dve.tensor_add(own, own, keep.ident[0:CT, 0:CT]))
                link(dve.tensor_mul(keep.wo[:, k, :], keep.wo[:, k, :], bcv[0:CT, V["gamma1"], :]))
            link(dve.reciprocal(cd[:, :, :], cd[:, :, :]))
            link(dve.tensor_mul(cs[:, :, :], colv[:, :, 3:6], cd[:, :, :]))
            link(dve.tensor_mul(c1[:, :], colv[:, :, V["dw1_w"]], cs[:, :, 2]))
            for k in range(KT):
                link(dve.tensor_scalar(taps_view(f13[:, k, :], K13, c13),
                                       dwk[:, k, :].rearrange("p (a b) -> p a b", a=K13),
                                       cs[:, k, 1:2], None, ALU.mult))
                mid = f13[:, k, c13:c13 + 1]
                link(dve.tensor_add(mid, mid, c1[:, k:k + 1]))
            for s in range(2):
                a = [alph[:, 4 * s + n:4 * s + n + 1] for n in range(4)]
                for k in range(KT):
                    link(dve.tensor_scalar(taps_view(f5[:, s, k, :], K5, c5),
                                           w5[:, s, k, :].rearrange("p (a b) -> p a b", a=K5),
                                           a[3], None, ALU.mult))
                    inner = taps_view(f5[:, s, k, :], K3, c5)
                    link(dve.scalar_tensor_tensor(inner, w3[:, s, k, :].rearrange("p (a b) -> p a b", a=K3),
                                                  a[2], inner, ALU.mult, ALU.add))
                    mid = f5[:, s, k, c5:c5 + 1]
                    link(dve.scalar_tensor_tensor(mid, w1[:, s, k:k + 1], a[1], mid, ALU.mult, ALU.add))
                    link(dve.tensor_add(mid, mid, a[0]))
            dve.wait_ge(expo, 1)
            link(dve.tensor_scalar_add(keep.bonus[:, :, :], keep.bonus[:, :, :], -1.0))
            folds[0] = done[0]

        @block.scalar
        def _(act):
            act.wait_ge(var_ready, 2)
            act.activation(sd[:, :, :], sd[:, :, :], ACT.Sqrt).then_inc(root, 1)
            act.activation(cd[:, :, :], cd[:, :, :], ACT.Sqrt).then_inc(root, 1)
            act.wait_ge(var_ready, 3)
            act.activation(keep.bonus[:, :, :], uw[:, :, :], ACT.Exp).then_inc(expo, 1)
            act.wait_ge(step, folds[0])
            act.dma_start(f13_d.rearrange("(k p) n -> p k n", p=CT), f13[:, :, :]).then_inc(stored, 16)
            act.dma_start(f5a_d.rearrange("(k p) n -> p k n", p=CT), f5[:, 0]).then_inc(stored, 16)
            act.dma_start(f5f_d.rearrange("(k p) n -> p k n", p=CT), f5[:, 1]).then_inc(stored, 16)
            act.dma_start(bias_d, sd[0:1, 0, :]).then_inc(stored, 16)
            act.wait_ge(stored, 64)


def pointwise(nc, B, x, keep, xpw_d):
    with ExitStack() as ctx:
        m = Mem(nc, ctx)
        xin = [m.sb(f"xin{u}", [CT, KT, HW]) for u in range(2)]
        xp = [m.sb(f"xp{u}", [PXC, C, PJ]) for u in range(2)]
        NB = 7
        ps = [m.ps(f"pw_ps{i}") for i in range(NB)]
        loaded = [m.sem(f"x_loaded{u}") for u in range(2)]
        ps_ready = m.sem("pw_product_ready")
        ps_free = m.sem("pw_bank_free")
        stored = [m.sem(f"xpw_stored{u}") for u in range(2)]
        PAIRS = PJ // 2
        block = ctx.enter_context(nc.Block())

        def load(sp, b, u):
            sp.dma_start(xin[u][:, :, :], dram(x, b * C * HW, [[HW, CT], [CT * HW, KT], [1, HW]])
                         ).then_inc(loaded[u], 16)

        @block.sync
        def _(sp):
            load(sp, 0, 0)
            load(sp, 1, 1)
            with sp.Fori(0, B // 2 - 1) as i:
                for u in range(2):
                    sp.wait_ge(ps_ready, (i * 2 + u + 1) * PAIRS)
                    load(sp, i * 2 + (u + 2), u)

        @block.tensor
        def _(pe):
            with pe.Fori(0, B // 2) as i:
                for u in range(2):
                    pe.wait_ge(loaded[u], i * 16 + 16)
                    for jp in range(PAIRS):
                        pe.wait_ge(ps_free, i * (2 * PAIRS) + (u * PAIRS + jp + 1))
                        bank = ps[jp % NB]
                        for q in range(2):
                            j = 2 * jp + q
                            for k in range(KT):
                                mm = pe.matmul(bank[0:PXC, q * C:(q + 1) * C],
                                               xin[u][:, k, j * PXC:(j + 1) * PXC], keep.wpw[:, k, :],
                                               start=(k == 0), stop=(k == KT - 1))
                        mm.then_inc(ps_ready, 1)

        @block.vector
        def _(dve):
            dve.sem_inc(ps_free, NB)
            with dve.Fori(0, B // 2) as i:
                for u in range(2):
                    dve.wait_ge(stored[u], i * 16 + 16)
                    for jp in range(PAIRS):
                        dve.wait_ge(ps_ready, i * (2 * PAIRS) + (u * PAIRS + jp + 1))
                        dve.tensor_tensor(
                            xp[u][:, :, 2 * jp:2 * jp + 2],
                            ps[jp % NB][0:PXC, 0:2 * C].rearrange("p (q c) -> p c q", q=2),
                            free(keep.shift_pw[0:PXC, :], [[1, C], [0, 2]]), ALU.add).then_inc(ps_free, 1)

        @block.scalar
        def _(act):
            for u in range(2):
                act.sem_inc(stored[u], 16)
            with act.Fori(0, B // 2) as i:
                for u in range(2):
                    act.wait_ge(ps_free, i * (2 * PAIRS) + ((u + 1) * PAIRS + NB))
                    act.dma_start(pair_batch(xpw_d, B, i * 2 + u),
                                  by_group(xp[u])
                                  ).then_inc(stored[u], 16)
            for u in range(2):
                act.wait_ge(stored[u], 16 * (B // 2 + 1))


def depthwise(nc, B, name, src, parts, k, f_d, dst, post, bias_d=None, norm=None, vecs=None,
              stats=None, flipped=False):
    dmax, centre, length, cols = band(k)
    N = B * PJ
    assert N <= 512
    with ExitStack() as ctx:
        m = Mem(nc, ctx)
        wt = [m.sb(f"{name}_band{u}", [PXP, G, cols]) for u in range(2)]
        raw = [m.sb(f"{name}_in{u}", [PXP, B, G, PJ]) for u in range(2)]
        z = [m.sb(f"{name}_norm{u}", [PXP, B, G, PJ]) for u in range(2)] if norm else raw
        out = [m.sb(f"{name}_out{u}", [PXP, B, G, PJ]) for u in range(2)]
        col = [m.sb(f"{name}_cols{u}", [PXP, 2, G]) for u in range(2)]
        ps = [m.ps(f"{name}_ps{i}") for i in range(G)]
        zeroed = m.sem(f"{name}_bands_zeroed")
        w_loaded = [m.sem(f"{name}_band_loaded{u}") for u in range(2)]
        in_loaded = [m.sem(f"{name}_in_loaded{u}") for u in range(2)]
        normed = m.sem(f"{name}_input_scaled")
        centred = m.sem(f"{name}_input_centred")
        z_ready = m.sem(f"{name}_input_ready")
        conv_done = m.sem(f"{name}_channel_convolved")
        ps_free = m.sem(f"{name}_bank_free")
        stored = [m.sem(f"{name}_stored{u}") for u in range(2)]
        out_read = m.sem(f"{name}_output_summed")
        if stats and not norm:
            sq = m.sb(f"{name}_squares", [PXP, B, G, PJ])
            part = [m.sb(f"{name}_part{n}", [PXP, B, PJ]) for n in range(2)]
            reduced = m.sem(f"{name}_group_reduced")
            summed = m.sem(f"{name}_sums_updated")
        block = ctx.enter_context(nc.Block())
        IN = 48 if norm else 32
        BASE = 2 * G if norm else 0
        step_in = PITCH if parts == PXP else W

        @block.sync
        def _(sp):
            def load(g, u):
                whole = raw[u][:, :, :, :].rearrange("p b c j -> p (b c j)")
                if parts == PXC:
                    sp.dma_start(whole[0:PXC], pair_group(src, B, g)).then_inc(in_loaded[u], 16)
                else:
                    copy_pairs(sp, whole, pair_group(src, B, g), in_loaded[u])
                if norm:
                    sp.dma_start(col[u][:, :, :], dram(vecs, V[norm] * C + g * G, [[0, PXP], [C, 2], [1, G]])
                                 ).then_inc(in_loaded[u], 16)
                if bias_d is not None:
                    sp.dma_start(col[u][:, 0, :], dram(bias_d, g * G, [[0, PXP], [1, G]])
                                 ).then_inc(in_loaded[u], 16)
                for r in range(2):
                    sp.dma_start(wt[u][r * step_in:r * step_in + W, :, :],
                                 dram(f_d, g * (G * length) + PITCH * r, [[1, W], [length, G], [1, cols]])
                                 ).then_inc(w_loaded[u], 16)

            sp.wait_ge(zeroed, 4 if parts == PXP else 2)
            load(0, 0)
            load(1, 1)
            with sp.Fori(0, NG // 2 - 1) as i:
                for u in range(2):
                    sp.wait_ge(ps_free, i * (2 * G) + G * (u + 2))
                    load(i * 2 + (u + 2), u)

        @block.tensor
        def _(pe):
            if norm:
                pe.sem_inc(conv_done, 2 * G)
            with pe.Fori(0, NG // 2) as i:
                for u in range(2):
                    pe.wait_ge(w_loaded[u], i * 32 + 32)
                    if norm:
                        pe.wait_ge(z_ready, i * (2 * G) + G * (u + 1))
                    else:
                        pe.wait_ge(in_loaded[u], i * IN + IN)
                    for cc in range(G):
                        pe.wait_ge(ps_free, i * (2 * G) + (u * G + cc + 1))
                        bank = ps[cc][0:PXP, 0:N].rearrange("p (b j) -> p b j", b=B)
                        order = [0] + [s * d for d in range(1, dmax + 1) for s in (1, -1)]
                        for n, d in enumerate(order):
                            lo, hi = max(0, -d), min(PJ, PJ - d)
                            at = 2 * PITCH * (dmax - d if flipped else dmax + d)
                            mm = pe.matmul(bank[:, :, lo:hi],
                                           wt[u][0:parts, cc, at:at + PXP],
                                           z[u][0:parts, :, cc, lo + d:hi + d],
                                           start=(n == 0), stop=(n == len(order) - 1))
                        mm.then_inc(conv_done, 1)

        @block.vector
        def _(dve):
            for u in range(2):
                dve.memset(wt[u][:, :, :], 0.0).then_inc(zeroed, 1)
                if parts == PXP:
                    dve.memset(raw[u][:, :, :, :], 0.0).then_inc(zeroed, 1)
            if norm:
                rs, ms = stats
                wide = lambda t: free(t, [[PJ, B], [0, G], [1, PJ]])
                with dve.Fori(0, NG // 2) as i:
                    for u in range(2):
                        dve.wait_ge(in_loaded[u], i * IN + IN)
                        dve.wait_ge(conv_done, i * (2 * G) + G * (u + 1))
                        dve.tensor_mul(z[u][:, :, :, :], raw[u][:, :, :, :], wide(rs[:, :])).then_inc(normed, 1)
                        dve.wait_ge(normed, i * 2 + (u + 1))
                        dve.tensor_sub(z[u][:, :, :, :], z[u][:, :, :, :], wide(ms[:, :])).then_inc(centred, 1)
                        dve.wait_ge(centred, i * 2 + (u + 1))
                        for cc in range(G):
                            v = z[u][:, :, cc, :]
                            dve.tensor_scalar(v, v, col[u][:, 0, cc:cc + 1], col[u][:, 1, cc:cc + 1],
                                              ALU.mult, ALU.add).then_inc(z_ready, 1)
            elif stats:
                s1, s2 = stats
                dve.memset(s1[:, :], 0.0).then_inc(summed, 1)
                dve.memset(s2[:, :], 0.0).then_inc(summed, 1)
                dve.sem_inc(out_read, 2)
                by_pixel = lambda t: t[:, :, :, :].rearrange("p b c j -> p b j c")
                flat = lambda t: t[:, :, :].rearrange("p b j -> p (b j)")
                with dve.Fori(0, NG // 2) as i:
                    for u in range(2):
                        dve.wait_ge(ps_free, i * (2 * G) + (G * (u + 2)))
                        dve.wait_ge(summed, i * 4 + (2 * u + 2))
                        dve.tensor_reduce(part[0][:, :, :], by_pixel(out[u]), AX_X, ALU.add).then_inc(reduced, 1)
                        dve.wait_ge(reduced, i * 4 + (2 * u + 1))
                        dve.tensor_add(s1[:, :], s1[:, :], flat(part[0])).then_inc(summed, 1)
                        dve.tensor_mul(sq[:, :, :, :], out[u][:, :, :, :], out[u][:, :, :, :]).then_inc(out_read, 1)
                        dve.wait_ge(out_read, i * 2 + (u + 3))
                        dve.tensor_reduce(part[1][:, :, :], by_pixel(sq), AX_X, ALU.add).then_inc(reduced, 1)
                        dve.wait_ge(reduced, i * 4 + (2 * u + 2))
                        dve.tensor_add(s2[:, :], s2[:, :], flat(part[1])).then_inc(summed, 1)

        @block.scalar
        def _(act):
            act.sem_inc(ps_free, G)
            for u in range(2):
                act.sem_inc(stored[u], 32)
            with act.Fori(0, NG // 2) as i:
                for u in range(2):
                    act.wait_ge(stored[u], i * 32 + 32)
                    if stats and not norm:
                        act.wait_ge(out_read, i * 2 + (u + 1))
                    for cc in range(G):
                        act.wait_ge(conv_done, i * (2 * G) + (BASE + u * G + cc + 1))
                        o = out[u][:, :, cc, :]
                        p = ps[cc][0:PXP, 0:N].rearrange("p (b j) -> p b j", b=B)
                        if post == "gelu":
                            act.activation(o, p, ACT.Gelu, bias=col[u][:, 0, cc:cc + 1]).then_inc(ps_free, 1)
                        else:
                            act.activation(o, p, ACT.Copy).then_inc(ps_free, 1)
                    act.wait_ge(ps_free, i * (2 * G) + (G * (u + 2)))
                    copy_pairs(act, pair_group(dst, B, i * 2 + u),
                               out[u][:, :, :, :].rearrange("p b c j -> p (b c j)"), stored[u])
            for u in range(2):
                act.wait_ge(stored[u], 32 * (NG // 2 + 1))


def norm_scales(nc, name, s1, s2, s1_d=None, s2_d=None):
    with ExitStack() as ctx:
        m = Mem(nc, ctx)
        t = m.sb(f"{name}_mean_squared", list(s1.shape))
        cleared = m.sem(f"{name}_gap_cleared")
        loaded = m.sem(f"{name}_sums_loaded")
        var_ready = m.sem(f"{name}_variance_ready")
        root = m.sem(f"{name}_root_ready")
        step = m.sem(f"{name}_steps")
        block = ctx.enter_context(nc.Block())

        if s1_d is not None:
            @block.sync
            def _(sp):
                sp.wait_ge(cleared, 2)
                copy_pairs(sp, s1[:, :], s1_d, loaded)
                copy_pairs(sp, s2[:, :], s2_d, loaded)

        @block.vector
        def _(dve):
            if s1_d is not None:
                dve.memset(s1[:, :], 0.0).then_inc(cleared, 1)
                dve.memset(s2[:, :], 0.0).then_inc(cleared, 1)
                dve.wait_ge(loaded, 64)
            dve.tensor_scalar_mul(s1[:, :], s1[:, :], 1.0 / C).then_inc(step, 1)
            dve.wait_ge(step, 1)
            dve.tensor_mul(t[:, :], s1[:, :], s1[:, :]).then_inc(step, 1)
            dve.wait_ge(step, 2)
            dve.scalar_tensor_tensor(s2[:, :], s2[:, :], 1.0 / C, t[:, :], ALU.mult, ALU.subtract
                                     ).then_inc(step, 1)
            dve.wait_ge(step, 3)
            dve.tensor_scalar(s2[:, :], s2[:, :], 0.0, LN_EPS, ALU.max, ALU.add).then_inc(var_ready, 1)
            dve.wait_ge(root, 1)
            dve.reciprocal(s2[:, :], s2[:, :]).then_inc(step, 1)
            dve.wait_ge(step, 4)
            dve.tensor_mul(s1[:, :], s1[:, :], s2[:, :]).then_inc(step, 1)

        @block.scalar
        def _(act):
            act.wait_ge(var_ready, 1)
            act.activation(s2[:, :], s2[:, :], ACT.Sqrt).then_inc(root, 1)


def transposed(bank, reverse=False):
    s = -1 if reverse else 1
    return free(bank[0:CT, :], [[PXP, JC], [s * PITCH, 2], [s, W]], PXP - 1 if reverse else 0)


def attention(nc, B, keep, mix_d, y_d, tok_d, s1_d, s2_d):
    with ExitStack() as ctx:
        m = Mem(nc, ctx)
        X = m.sb("mix_pairs", [PXP, C, PJ])
        Y = m.sb("residual_pairs", [PXP, C, PJ])
        xT = [m.sb(f"mixT{u}", [CT, KT, TC]) for u in range(2)]
        kS = m.sb("k_all", [CT, KT, HW])
        vS = m.sb("v_all", [CT, KT, W, PITCH])
        rS = m.sb("r_all", [CT, KT, HW])
        O = [m.sb(f"run_max{c}", [CT, 1 + HALF]) for c in range(KT)]
        A = [m.sb(f"decay_factor{c}", [CT, HALF]) for c in range(KT)]
        E = [m.sb(f"input_factor{c}", [CT, HALF]) for c in range(KT)]
        EV = [m.sb(f"input_times_v{c}", [CT, HALF]) for c in range(KT)]
        P = [m.sb(f"numerator_state{c}", [CT, HALF]) for c in range(KT)]
        qc = [m.sb(f"denominator_carry{c}", [CT, 1]) for c in range(KT)]
        s1 = m.sb("tok_sum", [PXP, PJ])
        s2 = m.sb("tok_square_sum", [PXP, PJ])
        junk = [m.sb(f"tok_squares{n}", [PXP, C]) for n in range(2)]
        z_ps = [m.ps(f"mixT_ps{i}") for i in range(KT)]
        NU = 3
        u_ps = [m.ps(f"proj_ps{i}") for i in range(NU)]
        o_ps = [m.ps(f"out_ps{i}") for i in range(2)]

        x_loaded = m.sem("mix_loaded")
        y_loaded = m.sem("residual_loaded")
        pads = m.sem("v_pads_cleared")
        zt_ready = m.sem("mixT_in_psum")
        xT_ready = m.sem("mixT_in_sbuf")
        un_ready = m.sem("projection_in_psum")
        un_read = m.sem("projection_evacuated")
        kt_done = m.sem("k_by_column")
        carry0 = m.sem("max_carry_ready")
        o_done = m.sem("run_max_done")
        a_arg = m.sem("decay_exponent")
        e_arg = m.sem("input_exponent")
        a_exp = m.sem("decay_factor_ready")
        e_exp = m.sem("input_factor_ready")
        ev_done = m.sem("input_times_v_ready")
        p_done = m.sem("numerator_scan_done")
        q_done = m.sem("denominator_scan_done")
        qc_done = m.sem("denominator_carried")
        n_done = m.sem("numerator_done")
        d_done = m.sem("denominator_done")
        ln_done = m.sem("denominator_logged")
        rec_done = m.sem("denominator_inverted")
        y_done = m.sem("wkv_done")
        sr_done = m.sem("receptance_ready")
        g_done = m.sem("wkv_gated")
        out_ps_ready = m.sem("attention_out_in_psum")
        tok_done = m.sem("tok_done")
        sq_done = m.sem("tok_squared")
        stored = m.sem("tok_stored")
        block = ctx.enter_context(nc.Block())
        UN = 3 * KT
        UNITS = 2 * KT * 2

        def unit(k):
            return k // 4, (k // 2) % 2, k % 2

        def cols(k):
            _, h, _ = unit(k)
            return slice(h * HALF, (h + 1) * HALF)

        def v_view(k):
            s, h, ct = unit(k)
            if s == 0:
                return vS[:, ct, h * (W // 2):(h + 1) * (W // 2), 0:W]
            return vS[:, ct, :, h * (W // 2):(h + 1) * (W // 2)].rearrange("p r w -> p w r")

        def by_column(t, k):
            _, h, ct = unit(k)
            return t[:, ct, :].rearrange("p (r w) -> p w r", r=W)[:, h * (W // 2):(h + 1) * (W // 2), :]

        def grid(t):
            return t[:, 0:HALF].rearrange("p (a b) -> p a b", b=W)

        def k_in(k):
            s, h, ct = unit(k)
            return kS[:, ct, cols(k)] if s == 0 else E[ct][:, :]

        @block.sync
        def _(sp):
            def load_x(b):
                copy_pairs(sp, by_group(X), pair_batch(mix_d, B, b), x_loaded)

            def load_y(b, offset=None):
                copy_pairs(sp, by_group(Y), pair_batch(y_d, B, b, offset), y_loaded)

            def store(b, squares, stores):
                sp.wait_ge(sq_done, squares)
                copy_pairs(sp, pair_batch(tok_d, B, b), by_group(Y), stored)
                for d, t in ((s1_d, s1), (s2_d, s2)):
                    copy_pairs(sp, dram(d, b * PJ, [[B * PJ, PXC], [1, PJ]]), t[:, :], stored)
                sp.wait_ge(stored, stores)

            sp.wait_ge(pads, 3)
            load_x(0)
            load_y(0)
            with sp.Fori(0, B - 1) as i:
                sp.wait_ge(zt_ready, i * (NCH * KT) + NCH * KT)
                load_x(i + 1)
                following = sp.snap((i + 1) * (G * PJ))
                marks = [sp.snap(i * n + m) for n, m in ((PJ, PJ + 2), (96, 96))]
                store(i, *marks)
                load_y(i + 1, following)
            store(B - 1, B * PJ + 2, B * 96)

        @block.tensor
        def _(pe):
            pe.sem_inc(un_ready, UN)
            pe.wait_ge(pads, 3)
            with pe.Fori(0, B) as i:
                def turn(t):
                    for ct in range(KT):
                        pe.wait_ge(xT_ready, i * (NCH * KT) + (KT * t + ct + 1))
                        for jj in range(JC):
                            tr = pe.transpose(z_ps[ct][0:CT, jj * PXP:(jj + 1) * PXP],
                                              X[:, ct * CT:(ct + 1) * CT, JC * t + jj], keep.ident[:, :])
                        tr.then_inc(zt_ready, 1)

                def project(t):
                    pe.wait_ge(xT_ready, i * (NCH * KT) + (KT * (t + 1) + KT))
                    for n in range(UN):
                        o, ct = n // KT, n % KT
                        pe.wait_ge(un_read, i * (NCH * UN) + (UN * t + n + 1))
                        bank = u_ps[(UN * t + n) % NU]
                        for k in range(KT):
                            mm = pe.matmul(bank[0:CT, 0:TC], keep.wkvr[:, k, o, ct * CT:(ct + 1) * CT],
                                           xT[t % 2][:, k, :], start=(k == 0), stop=(k == KT - 1))
                        mm.then_inc(un_ready, 1)

                pe.wait_ge(x_loaded, i * 32 + 32)
                turn(0)
                for t in range(NCH):
                    if t + 1 < NCH:
                        turn(t + 1)
                    project(t)
                pe.wait_ge(g_done, i * 4 + 4)
                for jp in range(PJ // 2):
                    pe.wait_ge(tok_done, i * PJ + (2 * jp + 1))
                    for q in range(2):
                        j = 2 * jp + q
                        for ct in range(KT):
                            mm = pe.matmul(o_ps[jp % 2][0:PXP, q * C:(q + 1) * C],
                                           vS[:, ct, :, :].rearrange("p r w -> p (r w)")[:, 2 * PITCH * j:2 * PITCH * j + PXP],
                                           keep.wo[:, ct, :], start=(ct == 0), stop=(ct == KT - 1))
                    mm.then_inc(out_ps_ready, 1)

        @block.scalar
        def _(act):
            act.sem_inc(xT_ready, KT)
            act.sem_inc(un_read, NU)
            act.sem_inc(sq_done, 2)
            with act.Fori(0, B) as i:
                def mix(t):
                    for ct in range(KT):
                        if ct == 0:
                            act.wait_ge(un_ready, i * (NCH * UN) + UN * max(t, 1))
                        act.wait_ge(zt_ready, i * (NCH * KT) + (KT * t + ct + 1))
                        act.activation(xT[t % 2][:, ct, :].rearrange("p (j r w) -> p j r w", j=JC, r=2),
                                       transposed(z_ps[ct], reverse=True), ACT.Copy).then_inc(xT_ready, 1)

                def evacuate(t):
                    for n in range(UN):
                        o, ct = n // KT, n % KT
                        act.wait_ge(un_ready, i * (NCH * UN) + (UN * (t + 1) + n + 1))
                        bank = u_ps[(UN * t + n) % NU][0:CT, 0:TC]
                        if o == 1:
                            dst = vS[:, ct, 2 * JC * t:2 * JC * (t + 1), 0:W]
                            bank = bank.rearrange("p (r w) -> p r w", w=W)
                        else:
                            dst = (kS if o == 0 else rS)[:, ct, TC * t:TC * (t + 1)]
                        act.activation(dst, bank, ACT.Copy).then_inc(un_read, 1)

                def factors(k):
                    s, h, ct = unit(k)
                    act.wait_ge(a_arg, i * UNITS + (k + 1))
                    act.activation(A[ct][:, :], A[ct][:, :], ACT.Exp, bias=keep.decay[:, ct, s:s + 1]
                                   ).then_inc(a_exp, 1)
                    act.wait_ge(e_arg, i * UNITS + (k + 1))
                    act.activation(E[ct][:, :], E[ct][:, :], ACT.Exp).then_inc(e_exp, 1)

                def invert(k):
                    _, _, ct = unit(k)
                    act.wait_ge(d_done, i * UNITS + (k + 1))
                    act.activation(E[ct][:, :], E[ct][:, :], ACT.Ln).then_inc(ln_done, 1)
                    act.wait_ge(ln_done, i * UNITS + (k + 1))
                    act.activation(E[ct][:, :], E[ct][:, :], ACT.Exp, scale=-1.0).then_inc(rec_done, 1)

                def column_k(k):
                    _, _, ct = unit(k)
                    act.wait_ge(y_done, i * UNITS + (k + 1))
                    act.activation(grid(E[ct]), by_column(kS, k), ACT.Copy).then_inc(kt_done, 1)

                mix(0)
                for t in range(NCH):
                    if t + 1 < NCH:
                        mix(t + 1)
                    evacuate(t)
                    if t == 3:
                        act.preload_act_table_set("natural_log_exp_and_others")
                        factors(0)
                    if t == 4:
                        factors(1)
                        invert(0)
                factors(2)
                invert(1)
                factors(3)
                invert(2)
                act.wait_ge(un_read, i * (NCH * UN) + (NCH * UN + NU))
                act.activation(rS[:, :, :], rS[:, :, :], ACT.Sigmoid).then_inc(sr_done, 1)
                act.preload_act_table_set("natural_log_exp_and_others")
                column_k(4)
                factors(4)
                invert(3)
                for k in range(5, UNITS):
                    column_k(k)
                    factors(k)
                    invert(k - 1)
                invert(UNITS - 1)
                for j in range(PJ):
                    act.wait_ge(tok_done, i * PJ + (j + 4))
                    act.wait_ge(sq_done, i * PJ + (j + 1))
                    act.activation(junk[j % 2][:, :], Y[:, :, j], ACT.Square, accum_out=s2[:, j:j + 1]
                                   ).then_inc(sq_done, 1)

        @block.gpsimd
        def _(pool):
            pool.sem_inc(y_done, 2)
            with pool.Fori(0, B) as i:
                def exponents(k):
                    _, _, ct = unit(k)
                    pool.wait_ge(y_done, i * UNITS + (k + 1))
                    pool.wait_ge(o_done, i * UNITS + (k + 1))
                    pool.tensor_tensor(A[ct][:, :], O[ct][:, 0:HALF], O[ct][:, 1:1 + HALF], ALU.subtract
                                       ).then_inc(a_arg, 1)
                    pool.tensor_tensor(E[ct][:, :], k_in(k), O[ct][:, 1:1 + HALF], ALU.subtract
                                       ).then_inc(e_arg, 1)

                def weigh(k):
                    s, _, ct = unit(k)
                    if s == 0:
                        pool.wait_ge(un_read, i * (NCH * UN) + (UN * (4 if k < 2 else NCH) + NU))
                    if k >= 6:
                        pool.wait_ge(g_done, i * 4 + (k - 5))
                    pool.wait_ge(e_exp, i * UNITS + (k + 1))
                    pool.tensor_tensor(grid(EV[ct]), grid(E[ct]), v_view(k), ALU.mult).then_inc(ev_done, 1)

                def divide(k):
                    s, _, ct = unit(k)
                    pool.wait_ge(rec_done, i * UNITS + (k + 1))
                    dst = v_view(k) if s == 0 else grid(EV[ct])
                    pool.tensor_tensor(dst, grid(EV[ct]), grid(E[ct]), ALU.mult).then_inc(y_done, 1)

                for k in range(UNITS):
                    exponents(k)
                    if k == 4:
                        pool.wait_ge(y_done, i * UNITS + 3 + 2)
                    if k == 5:
                        pool.wait_ge(y_done, i * UNITS + 4 + 2)
                    weigh(k)
                    if k:
                        divide(k - 1)
                divide(UNITS - 1)

        @block.vector
        def _(dve):
            for t in (X, Y):
                dve.memset(t[:, :, :], 0.0).then_inc(pads, 1)
            dve.memset(vS[:, :, :, :], 0.0).then_inc(pads, 1)
            dve.sem_inc(tok_done, 3)
            with dve.Fori(0, B) as i:
                def run_max(k):
                    s, h, ct = unit(k)
                    if s == 0:
                        dve.wait_ge(un_read, i * (NCH * UN) + (UN * (4 if h == 0 else NCH) + NU))
                    else:
                        dve.wait_ge(kt_done, i * 4 + (k - 3))
                    if h == 0:
                        dve.memset(O[ct][:, 0:1], NEG).then_inc(carry0, 1)
                    else:
                        dve.tensor_copy(O[ct][:, 0:1], O[ct][:, HALF:HALF + 1]).then_inc(carry0, 1)
                    dve.wait_ge(carry0, i * UNITS + (k + 1))
                    dve.tensor_tensor_scan(O[ct][:, 1:1 + HALF], free(keep.decay[:, ct, s:s + 1], [[0, HALF]]),
                                           k_in(k), O[ct][:, 0:1], ALU.add, ALU.max).then_inc(o_done, 1)

                def sums(k):
                    _, h, ct = unit(k)
                    dve.wait_ge(a_exp, i * UNITS + (k + 1))
                    dve.wait_ge(ev_done, i * UNITS + (k + 1))
                    dve.tensor_tensor_scan(P[ct][:, :], A[ct][:, :], EV[ct][:, :],
                                           P[ct][:, HALF - 1:HALF] if h else 0.0,
                                           ALU.mult, ALU.add).then_inc(p_done, 1)
                    dve.wait_ge(e_exp, i * UNITS + (k + 1))
                    dve.wait_ge(p_done, i * UNITS + (k + 1))
                    dve.tensor_tensor_scan(A[ct][:, :], A[ct][:, :], E[ct][:, :],
                                           qc[ct][:, :] if h else 0.0, ALU.mult, ALU.add).then_inc(q_done, 1)

                def outputs(k):
                    s, _, ct = unit(k)
                    bonus = keep.bonus[:, ct, s:s + 1]
                    dve.wait_ge(q_done, i * UNITS + (k + 1))
                    dve.tensor_copy(qc[ct][:, :], A[ct][:, HALF - 1:HALF]).then_inc(qc_done, 1)
                    dve.scalar_tensor_tensor(E_V(ct), E_V(ct), bonus, P[ct][:, :], ALU.mult, ALU.add
                                             ).then_inc(n_done, 1)
                    dve.scalar_tensor_tensor(E[ct][:, :], E[ct][:, :], bonus, A[ct][:, :], ALU.mult, ALU.add
                                             ).then_inc(d_done, 1)

                def E_V(ct):
                    return EV[ct][:, :]

                def gate(k):
                    _, _, ct = unit(k)
                    dve.wait_ge(sr_done, i + 1)
                    dve.wait_ge(y_done, i * UNITS + (k + 1 + 2))
                    dve.tensor_tensor(v_view(k), grid(EV[ct]), by_column(rS, k), ALU.mult).then_inc(g_done, 1)

                run_max(0)
                for k in range(UNITS):
                    if k + 1 < 4:
                        run_max(k + 1)
                    sums(k)
                    if 4 <= k + 1 < UNITS:
                        run_max(k + 1)
                    outputs(k)
                    if k - 1 >= 4:
                        gate(k - 1)
                gate(UNITS - 1)
                dve.wait_ge(y_loaded, i * 32 + 32)
                for j in range(PJ):
                    q = j % 2
                    if q == 0:
                        dve.wait_ge(out_ps_ready, i * (PJ // 2) + (j // 2 + 1))
                    dve.scalar_tensor_tensor(Y[:, :, j], o_ps[(j // 2) % 2][0:PXP, q * C:(q + 1) * C], 1.0,
                                             Y[:, :, j], ALU.mult, ALU.add, accum_out=s1[:, j:j + 1]
                                             ).then_inc(tok_done, 1)


def feed_forward(nc, B, ins, keep, mix_d, tok_d, out):
    with ExitStack() as ctx:
        m = Mem(nc, ctx)
        X = [m.sb(f"ffn_mix{u}", [PXP, C, PJ]) for u in range(2)]
        T = [m.sb(f"ffn_tok{u}", [PXP, C, PJ]) for u in range(2)]
        wk = m.sb("ffn_wk", [CT, KT, HID])
        wv = m.sb("ffn_wv", [128, HT, C])
        wr = m.sb("ffn_wr", [CT, KT, C])
        gam = m.sb("gamma2", [128, C])
        xT = [m.sb(f"ffn_mixT{u}", [CT, KT, TC]) for u in range(2)]
        kk = [m.sb(f"hidden{u}", [128, HT, TC]) for u in range(2)]
        sg = [m.sb(f"ffn_gate{u}", [CT, KT, TC]) for u in range(2)]
        gv = m.sb("gated", [CT, KT, TC])
        res = [m.sb(f"result{u}", [CT, KT, TC]) for u in range(2)]
        z_ps = [m.ps(f"f_mixT_ps{i}") for i in range(KT)]
        t_ps = [m.ps(f"f_tokT_ps{i}") for i in range(KT)]
        h_ps = [m.ps(f"f_hid_ps{i}") for i in range(2)]
        v_ps = [m.ps(f"f_out_ps{i}") for i in range(KT)]
        w_loaded = m.sem("ffn_weights_loaded")
        w_folded = m.sem("ffn_gamma_folded")
        gaps = m.sem("ffn_gaps_cleared")
        x_loaded = [m.sem(f"ffn_mix_loaded{u}") for u in range(2)]
        t_loaded = [m.sem(f"ffn_tok_loaded{u}") for u in range(2)]
        zt_ready = m.sem("ffn_mixT_in_psum")
        xT_ready = m.sem("ffn_mixT_in_sbuf")
        r_ready = m.sem("ffn_r_in_psum")
        h_ready = m.sem("ffn_hidden_in_psum")
        g_ready = m.sem("ffn_gate_ready")
        relu_done = m.sem("ffn_hidden_clipped")
        kk_ready = m.sem("ffn_hidden_squared")
        tt_ready = m.sem("ffn_tokT_in_psum")
        v_ready = m.sem("ffn_out_in_psum")
        gv_done = m.sem("ffn_out_gated")
        res_done = m.sem("result_ready")
        stored = [m.sem(f"result_stored{u}") for u in range(2)]
        block = ctx.enter_context(nc.Block())
        CH = 2 * NCH

        @block.tensor
        def _(pe):
            pe.wait_ge(w_loaded, 64)
            pe.wait_ge(w_folded, HT)
            pe.sem_inc(h_ready, 2 * HT)
            pe.sem_inc(v_ready, 2 * KT)
            with pe.Fori(0, B // 2) as i:
                def turn(n, src, banks, free_sem, ready):
                    u, t = n // NCH, n % NCH
                    for ct in range(KT):
                        pe.wait_ge(free_sem, i * (CH * KT) + (KT * n + ct + 1))
                        for jj in range(JC):
                            tr = pe.transpose(banks[ct][0:CT, jj * PXP:(jj + 1) * PXP],
                                              src[u][:, ct * CT:(ct + 1) * CT, JC * t + jj], keep.ident[:, :])
                        tr.then_inc(ready, 1)

                pe.wait_ge(x_loaded[0], i * 32 + 32)
                turn(0, X, z_ps, xT_ready, zt_ready)
                for n in range(CH):
                    pe.wait_ge(xT_ready, i * (CH * KT) + (KT * n + 2 * KT))
                    for a in range(KT + HT):
                        if a < KT:
                            if a == 0:
                                pe.wait_ge(relu_done, i * (CH * HT) + (HT * n + HT - 1 + 2))
                            else:
                                pe.wait_ge(relu_done, i * (CH * HT) + (HT * n + HT + 2))
                            w, M = wr[:, :, a * CT:(a + 1) * CT], CT
                        else:
                            h = a - KT
                            if h < 2:
                                pe.wait_ge(g_ready, i * (CH * KT) + (KT * n + h + 1))
                            else:
                                pe.wait_ge(relu_done, i * (CH * HT) + (HT * (n + 1) + h - 1 + 2))
                            w, M = wk[:, :, h * 128:(h + 1) * 128], 128
                        for k in range(KT):
                            mm = pe.matmul(h_ps[a % 2][0:M, 0:TC], w[:, k, :], xT[n % 2][:, k, :],
                                           start=(k == 0), stop=(k == KT - 1))
                        mm.then_inc(r_ready if a < KT else h_ready, 1)
                    if n + 1 < CH:
                        if n + 1 == NCH:
                            pe.wait_ge(x_loaded[1], i * 32 + 32)
                        turn(n + 1, X, z_ps, xT_ready, zt_ready)
                    if n % NCH == 0:
                        pe.wait_ge(t_loaded[n // NCH], i * 32 + 32)
                    turn(n, T, t_ps, res_done, tt_ready)
                    for ct in range(KT):
                        pe.wait_ge(gv_done, i * (CH * KT) + (KT * n + ct + 1))
                        for h in range(HT):
                            if ct == 0:
                                pe.wait_ge(kk_ready, i * (CH * HT) + (HT * n + h + 1))
                            mm = pe.matmul(v_ps[ct][0:CT, 0:TC], wv[:, h, ct * CT:(ct + 1) * CT],
                                           kk[n % 2][:, h, :], start=(h == 0), stop=(h == HT - 1))
                        mm.then_inc(v_ready, 1)

        @block.scalar
        def _(act):
            act.sem_inc(xT_ready, KT)
            with act.Fori(0, B // 2) as i:
                def mix(n):
                    act.wait_ge(h_ready, i * (CH * HT) + HT * (n + 1))
                    for ct in range(KT):
                        act.wait_ge(zt_ready, i * (CH * KT) + (KT * n + ct + 1))
                        act.activation(xT[n % 2][:, ct, :].rearrange("p (j r w) -> p j r w", j=JC, r=2),
                                       transposed(z_ps[ct], reverse=True), ACT.Copy).then_inc(xT_ready, 1)

                mix(0)
                for n in range(CH):
                    for ct in range(KT):
                        act.wait_ge(gv_done, i * (CH * KT) + (KT * n + 1))
                        act.wait_ge(r_ready, i * (CH * KT) + (KT * n + ct + 1))
                        act.activation(sg[n % 2][:, ct, :], h_ps[ct][0:CT, 0:TC], ACT.Sigmoid
                                       ).then_inc(g_ready, 1)
                    for h in range(HT):
                        act.wait_ge(relu_done, i * (CH * HT) + (HT * (n + 1) + h + 1 + 2))
                        act.activation(kk[n % 2][:, h, :], kk[n % 2][:, h, :], ACT.Square).then_inc(kk_ready, 1)
                    if n + 1 < CH:
                        mix(n + 1)

        @block.vector
        def _(dve):
            for t in (*X, *T):
                dve.memset(t[:, :, :], 0.0).then_inc(gaps, 1)
            dve.wait_ge(w_loaded, 64)
            for h in range(HT):
                dve.tensor_mul(wv[:, h, :], wv[:, h, :], gam[:, :]).then_inc(w_folded, 1)
            dve.sem_inc(relu_done, HT + 2)
            dve.sem_inc(gv_done, KT)
            dve.sem_inc(res_done, KT)
            for u in range(2):
                dve.sem_inc(stored[u], 16)
            with dve.Fori(0, B // 2) as i:
                for n in range(CH):
                    for h in range(HT):
                        if h == 0:
                            dve.wait_ge(v_ready, i * (CH * KT) + KT * (n + 1))
                        dve.wait_ge(h_ready, i * (CH * HT) + (HT * (n + 2) + h + 1))
                        bank = h_ps[h % 2][:, 0:TC]
                        dve.tensor_scalar_max(kk[n % 2][:, h, :], bank, 0.0).then_inc(relu_done, 1)
                    for ct in range(KT):
                        dve.wait_ge(v_ready, i * (CH * KT) + (KT * (n + 2) + ct + 1))
                        dve.wait_ge(g_ready, i * (CH * KT) + (KT * n + ct + 1))
                        dve.tensor_mul(gv[:, ct, :], v_ps[ct][0:CT, 0:TC], sg[n % 2][:, ct, :]
                                       ).then_inc(gv_done, 1)
                    for ct in range(KT):
                        if ct == 0:
                            dve.wait_ge(stored[n % 2], i * (16 * NCH) + 16 * (n // 2 + 1))
                        dve.wait_ge(gv_done, i * (CH * KT) + (KT * (n + 1) + ct + 1))
                        dve.wait_ge(tt_ready, i * (CH * KT) + (KT * n + ct + 1))
                        dve.tensor_tensor(res[n % 2][:, ct, :].rearrange("p (j r w) -> p j r w", j=JC, r=2),
                                          gv[:, ct, :].rearrange("p (j r w) -> p j r w", j=JC, r=2),
                                          transposed(t_ps[ct]), ALU.add).then_inc(res_done, 1)

        @block.sync
        def _(sp):
            for dst, src in [(wk, ins["ffn_wkt"].rearrange("(k p) n -> p k n", p=CT)),
                             (wv, ins["ffn_wvt"].rearrange("(k p) n -> p k n", p=128)),
                             (wr, ins["ffn_wrt"].rearrange("(k p) n -> p k n", p=CT))]:
                sp.dma_start(dst[:, :, :], src).then_inc(w_loaded, 16)
            sp.dma_start(gam[:, :], dram(ins["vecs"], V["gamma2"] * C, [[0, 128], [1, C]])).then_inc(w_loaded, 16)

            def load(b, u):
                copy_pairs(sp, by_group(X[u]), pair_batch(mix_d, B, b), x_loaded[u])
                copy_pairs(sp, by_group(T[u]), pair_batch(tok_d, B, b), t_loaded[u])

            def images(i, reload):
                for n in range(CH):
                    u, t = n // NCH, n % NCH
                    at = i * (2 * C * HW) + (u * C * HW + t * TC)
                    if reload:
                        at = sp.snap(at)
                    sp.wait_ge(res_done, i * (CH * KT) + (KT * (n + 2)))
                    sp.dma_start(dram(out, at, [[HW, CT], [CT * HW, KT], [1, TC]]), res[n % 2][:, :, :]
                                 ).then_inc(stored[n % 2], 16)
                    if t == NCH - 1 and reload:
                        load(i * 2 + (u + 2), u)

            sp.wait_ge(gaps, 4)
            load(0, 0)
            load(1, 1)
            with sp.Fori(0, B // 2 - 1) as i:
                images(i, True)
            images(B // 2 - 1, False)
            for u in range(2):
                sp.wait_ge(stored[u], 16 * (NCH * (B // 2) + 1))


class Kept:

    def __init__(self, m):
        self.ident = m.sb("identity", [PXP, PXP])
        self.wpw = m.sb("pointwise_weights", [CT, KT, C])
        self.wkvr = m.sb("kvr_weights", [CT, KT, 3, C])
        self.wo = m.sb("attention_out_weights", [CT, KT, C])
        self.shift_pw = m.sb("pointwise_shift", [128, C])
        self.decay = m.sb("wkv_decay", [CT, KT, 2])
        self.bonus = m.sb("wkv_bonus", [CT, KT, 2])


def build(nc, B, ins, out, debug=None):
    scratch = lambda name, shape: (debug or {}).get(name) or nc.dram_tensor(name, shape, F32).ap()
    pair_shape = [NG, PXC, B, G * PJ]
    xpw_d = scratch("x_pointwise", pair_shape)
    y_d = scratch("y_gelu", pair_shape)
    mixa_d = scratch("att_mix", pair_shape)
    tok_d = scratch("tok", pair_shape)
    mixf_d = scratch("ffn_mix", pair_shape)
    f13_d = scratch("flat13", [C, band(K13)[2]])
    f5a_d = scratch("flat5_att", [C, band(K5)[2]])
    f5f_d = scratch("flat5_ffn", [C, band(K5)[2]])
    bias_d = scratch("dw_bias", [1, C])
    s1_d = scratch("tok_sums", [PXC, B * PJ])
    s2_d = scratch("tok_square_sums", [PXC, B * PJ])
    with ExitStack() as ctx:
        m = Mem(nc, ctx)
        keep = Kept(m)
        prepare(nc, ins, keep, f13_d, f5a_d, f5f_d, bias_d)
        pointwise(nc, B, ins["x"], keep, xpw_d)
        with ExitStack() as inner:
            mi = Mem(nc, inner)
            s1, s2 = mi.sb("y_sum", [PXP, B * PJ]), mi.sb("y_square_sum", [PXP, B * PJ])
            depthwise(nc, B, "dw13", xpw_d, PXC, K13, f13_d, y_d, "gelu", bias_d=bias_d, stats=(s1, s2),
                      flipped=True)
            norm_scales(nc, "ln1", s1, s2)
            depthwise(nc, B, "omni1", y_d, PXP, K5, f5a_d, mixa_d, "copy", norm="ln1_g",
                      vecs=ins["vecs"], stats=(s2, s1))
        attention(nc, B, keep, mixa_d, y_d, tok_d, s1_d, s2_d)
        with ExitStack() as inner:
            mi = Mem(nc, inner)
            s1, s2 = mi.sb("t_sum", [PXP, B * PJ]), mi.sb("t_square_sum", [PXP, B * PJ])
            norm_scales(nc, "ln2", s1, s2, s1_d, s2_d)
            depthwise(nc, B, "omni2", tok_d, PXP, K5, f5f_d, mixf_d, "copy", norm="ln2_g",
                      vecs=ins["vecs"], stats=(s2, s1))
        feed_forward(nc, B, ins, keep, mixf_d, tok_d, out)


def layout(inputs):
    import numpy as np

    i = {k: np.asarray(v) for k, v in inputs.items()}
    l0, l1 = (lambda n: i["L0_conv_" + n]), (lambda n: i["L1_conv_" + n])
    vec = {n: l0(n) for n in VEC if n.startswith(("pw_", "dwk_", "dw1_"))}
    vec.update({n: l1(n) for n in VEC if n.startswith(("ln", "gamma"))})
    for n in range(2):
        vec[f"dec{n}"], vec[f"first{n}"] = l1("sp_decay")[n], l1("sp_first")[n]
    vecs = np.stack([vec[n] for n in VEC])
    plain = lambda w: np.ascontiguousarray(w[:, 0]).reshape(C, -1)
    flip = lambda w: np.ascontiguousarray(w[:, 0, ::-1, ::-1]).reshape(C, -1)
    x = i["x"]
    pairs = x.reshape(*x.shape[:2], PJ, 2, W)[:, :, :, ::-1, ::-1]
    cols = lambda a: np.ascontiguousarray(a.reshape(KT, CT).T)
    t = lambda a: np.ascontiguousarray(a.T)
    return {
        "x": np.ascontiguousarray(pairs).reshape(x.shape),
        "vecs": vecs,
        "vec_cols": np.ascontiguousarray(vecs.reshape(NV, KT, CT).transpose(2, 1, 0)),
        "alphas": np.concatenate([l1("att_alpha"), l1("ffn_alpha")]),
        "ident": np.eye(PXP, dtype=np.float32),
        "pw_wt": t(l0("pw_w")),
        "dwk_w": flip(l0("dwk_w")),
        "att_w5": plain(l1("att_w5")), "att_w3": plain(l1("att_w3")), "att_w1": cols(l1("att_w1")),
        "ffn_w5": plain(l1("ffn_w5")), "ffn_w3": plain(l1("ffn_w3")), "ffn_w1": cols(l1("ffn_w1")),
        "att_wt": np.stack([t(l1("att_wk")), t(l1("att_wv")), t(l1("att_wr"))]),
        "att_wot": t(l1("att_wo")),
        "ffn_wkt": t(l1("ffn_wk")), "ffn_wvt": t(l1("ffn_wv")), "ffn_wrt": t(l1("ffn_wr")),
    }


def kernel(**inputs):
    import concourse.bacc as bacc
    from concourse.bass_utils import run_bass_kernel_spmd

    arrays = layout(inputs)
    B = arrays["x"].shape[0]
    nc = bacc.Bacc("TRN2", target_bir_lowering=False, num_devices=1)
    ins = {n: nc.dram_tensor(n, a.shape, mybir.dt.from_np(a.dtype), kind="ExternalInput").ap()
           for n, a in arrays.items()}
    out = nc.dram_tensor("out", [B, C, W, W], F32, kind="ExternalOutput").ap()
    build(nc, B, ins, out)
    return run_bass_kernel_spmd(nc, [arrays], core_ids=[0]).results[0]["out"]
```

```python
from contextlib import ExitStack

import concourse.bass as bass
from concourse import mybir

F32 = mybir.dt.float32
ALU = mybir.AluOpType
ACT = mybir.ActivationFunctionType
AX_X = mybir.AxisListType.X

C = 192
W = 56
HW = W * W
CT = 96
KT = C // CT
HID = 4 * C
HT = HID // 128
G = 8
NG = C // G
PJ = W // 2
K13, K5, K3 = 13, 5, 3
PITCH = 62
PXC = 2 * W
PXP = PITCH + W
JC = 4
NCH = PJ // JC
TC = JC * PXC
NQ = NCH
UNITS = 2 * NQ
ROWS_AT = [3, 5, 6, 8, 9, 11, 12]
RESIDUAL_AT = [5, 7, 8, 10, 11, 12, 13]
RING = 4
QT = HW // NQ
QW = W // NQ
LN_EPS = 1e-5
BN_EPS = 1e-5
NEG = -1e30

VEC = ["pw_v", "dwk_v", "dw1_v", "pw_g", "dwk_g", "dw1_g", "pw_b", "dwk_b", "dw1_b",
       "pw_m", "dwk_m", "dw1_m", "dw1_w", "ln1_g", "ln1_b", "ln2_g", "ln2_b", "gamma1", "gamma2",
       "dec0", "dec1", "first0", "first1"]
NV = len(VEC)
V = {n: i for i, n in enumerate(VEC)}


def band(k):
    dmax = (k // 2 + 1) // 2
    centre = 2 * PITCH * dmax + PXP - 1
    return dmax, centre, 2 * centre + 2, 2 * PITCH * 2 * dmax + PXP


def free(ap, pattern, offset=0):
    return bass.AP(ap.tensor, ap.offset + offset, [list(ap.ap[0])] + pattern)


def dram(t, offset, pattern):
    return bass.AP(t.tensor, offset, pattern)


def taps_view(ap, k, centre):
    return free(ap, [[PITCH, k], [1, k]], centre - (k // 2) * (PITCH + 1))


class Mem:
    def __init__(self, nc, ctx):
        self.nc, self.ctx = nc, ctx

    def sb(self, name, shape, dt=F32):
        return self.ctx.enter_context(self.nc.sbuf_tensor(name, shape, dt))

    def ps(self, name, shape=(128, 512)):
        return self.ctx.enter_context(self.nc.psum_tensor(name, list(shape), F32))

    def sem(self, name):
        return self.ctx.enter_context(self.nc.semaphore(name))


def pair_batch(t, B, b, offset=None):
    row = B * G * PJ
    return dram(t, b * G * PJ if offset is None else offset, [[row, PXC], [PXC * row, NG], [1, G * PJ]])


def pair_group(t, B, g):
    row = B * G * PJ
    return dram(t, g * PXC * row, [[row, PXC], [1, row]])


def copy_pairs(eng, to, of, signal):
    for r in range(2):
        tile, rest = slice(r * PITCH, r * PITCH + W), r * W
        part = []
        for ap in (to, of):
            dims = [list(d) for d in ap.ap]
            if dims[0][1] == PXP:
                part.append(ap[tile])
            else:
                part.append(bass.AP(ap.tensor, ap.offset + rest * dims[0][0], [[dims[0][0], W]] + dims[1:]))
        eng.dma_start(part[0], part[1]).then_inc(signal, 16)


def by_group(t):
    return t[:, :, :].rearrange("p (g c) j -> p g (c j)", g=NG)


def prepare(nc, ins, keep, wpw, shift_pw, f13_d, f5a_d, f5f_d, bias_d):
    with ExitStack() as ctx:
        m = Mem(nc, ctx)
        bcv = m.sb("bcv", [128, NV, C])
        colv = m.sb("colv", [CT, KT, NV])
        alph = m.sb("alph", [CT, 8])
        dwk = m.sb("dwk", [CT, KT, K13 * K13])
        w5 = m.sb("w5", [CT, 2, KT, K5 * K5])
        w3 = m.sb("w3", [CT, 2, KT, K3 * K3])
        w1 = m.sb("w1", [CT, 2, KT])
        _, c13, l13, _ = band(K13)
        _, c5, l5, _ = band(K5)
        f13 = m.sb("f13", [CT, KT, l13])
        f5 = m.sb("f5", [CT, 2, KT, l5])
        sd = m.sb("sd", [128, 3, C])
        sc = m.sb("sc", [128, 3, C])
        sh = m.sb("sh", [128, 3, C])
        cd = m.sb("cd", [CT, KT, 3])
        cs = m.sb("cs", [CT, KT, 3])
        c1 = m.sb("c1", [CT, KT])
        uw = m.sb("uw", [CT, KT, 2])
        loads = m.sem("prep_loaded")
        var_ready = m.sem("prep_variances")
        root = m.sem("prep_roots")
        step = m.sem("prep_steps")
        expo = m.sem("prep_exponentials")
        stored = m.sem("prep_stored")
        block = ctx.enter_context(nc.Block())
        folds = [0]

        @block.sync
        def _(sp):
            n = 0
            vecs = ins["vecs"]
            for dst, src in [
                (bcv[:, :, :], dram(vecs, 0, [[0, 128], [1, NV * C]])),
                (colv[:, :, :], ins["vec_cols"]),
                (alph[:, :], dram(ins["alphas"], 0, [[0, CT], [1, 8]])),
                (keep.ident[:, :], ins["ident"]),
                (wpw[:, :, :], ins["pw_wt"].rearrange("(k p) n -> p k n", p=CT)),
                *[(keep.wkvr[:, :, o, :], ins["att_wt"][o].rearrange("(k p) n -> p k n", p=CT))
                  for o in range(3)],
                (keep.wo[:, :, :], ins["att_wot"].rearrange("(k p) n -> p k n", p=CT)),
                (dwk[:, :, :], ins["dwk_w"].rearrange("(k p) n -> p k n", p=CT)),
                (w5[:, 0], ins["att_w5"].rearrange("(k p) n -> p k n", p=CT)),
                (w5[:, 1], ins["ffn_w5"].rearrange("(k p) n -> p k n", p=CT)),
                (w3[:, 0], ins["att_w3"].rearrange("(k p) n -> p k n", p=CT)),
                (w3[:, 1], ins["ffn_w3"].rearrange("(k p) n -> p k n", p=CT)),
                (w1[:, 0], ins["att_w1"]),
                (w1[:, 1], ins["ffn_w1"]),
            ]:
                sp.dma_start(dst, src).then_inc(loads, 16)
                n += 16
            folds[0] = n

        @block.vector
        def _(dve):
            done = [0]

            def link(ins_):
                done[0] += 1
                ins_.then_inc(step, 1)
                dve.wait_ge(step, done[0])

            link(dve.memset(f13[:, :, :], 0.0))
            link(dve.memset(f5[:, :, :, :], 0.0))
            dve.wait_ge(loads, folds[0])
            dve.tensor_scalar_add(sd[:, :, :], bcv[:, 0:3, :], BN_EPS).then_inc(var_ready, 1)
            dve.tensor_scalar_add(cd[:, :, :], colv[:, :, 0:3], BN_EPS).then_inc(var_ready, 1)
            link(dve.tensor_scalar_mul(keep.decay[:, :, :], colv[:, :, V["dec0"]:V["dec0"] + 2], 1.0 / HW))
            dve.scalar_tensor_tensor(uw[:, :, :], colv[:, :, V["first0"]:V["first0"] + 2], 1.0 / HW,
                                     keep.decay[:, :, :], ALU.mult, ALU.add).then_inc(var_ready, 1)
            dve.wait_ge(root, 2)
            link(dve.reciprocal(sd[:, :, :], sd[:, :, :]))
            link(dve.tensor_mul(sc[:, :, :], bcv[:, 3:6, :], sd[:, :, :]))
            link(dve.tensor_mul(sh[:, :, :], bcv[:, 9:12, :], sc[:, :, :]))
            link(dve.tensor_sub(sh[:, :, :], bcv[:, 6:9, :], sh[:, :, :]))
            link(dve.tensor_copy(shift_pw[:, :], sh[:, 0, :]))
            link(dve.tensor_add(sd[:, 0, :], sh[:, 1, :], sh[:, 2, :]))
            for k in range(KT):
                link(dve.tensor_mul(wpw[:, k, :], wpw[:, k, :], sc[0:CT, 0, :]))
                own = wpw[:, k, k * CT:(k + 1) * CT]
                link(dve.tensor_add(own, own, keep.ident[0:CT, 0:CT]))
                link(dve.tensor_mul(keep.wo[:, k, :], keep.wo[:, k, :], bcv[0:CT, V["gamma1"], :]))
            link(dve.reciprocal(cd[:, :, :], cd[:, :, :]))
            link(dve.tensor_mul(cs[:, :, :], colv[:, :, 3:6], cd[:, :, :]))
            link(dve.tensor_mul(c1[:, :], colv[:, :, V["dw1_w"]], cs[:, :, 2]))
            for k in range(KT):
                link(dve.tensor_scalar(taps_view(f13[:, k, :], K13, c13),
                                       dwk[:, k, :].rearrange("p (a b) -> p a b", a=K13),
                                       cs[:, k, 1:2], None, ALU.mult))
                mid = f13[:, k, c13:c13 + 1]
                link(dve.tensor_add(mid, mid, c1[:, k:k + 1]))
            for s in range(2):
                a = [alph[:, 4 * s + n:4 * s + n + 1] for n in range(4)]
                for k in range(KT):
                    link(dve.tensor_scalar(taps_view(f5[:, s, k, :], K5, c5),
                                           w5[:, s, k, :].rearrange("p (a b) -> p a b", a=K5),
                                           a[3], None, ALU.mult))
                    inner = taps_view(f5[:, s, k, :], K3, c5)
                    link(dve.scalar_tensor_tensor(inner, w3[:, s, k, :].rearrange("p (a b) -> p a b", a=K3),
                                                  a[2], inner, ALU.mult, ALU.add))
                    mid = f5[:, s, k, c5:c5 + 1]
                    link(dve.scalar_tensor_tensor(mid, w1[:, s, k:k + 1], a[1], mid, ALU.mult, ALU.add))
                    link(dve.tensor_add(mid, mid, a[0]))
            dve.wait_ge(expo, 1)
            link(dve.tensor_scalar_add(keep.bonus[:, :, :], keep.bonus[:, :, :], -1.0))
            folds[0] = done[0]

        @block.scalar
        def _(act):
            act.wait_ge(var_ready, 2)
            act.activation(sd[:, :, :], sd[:, :, :], ACT.Sqrt).then_inc(root, 1)
            act.activation(cd[:, :, :], cd[:, :, :], ACT.Sqrt).then_inc(root, 1)
            act.wait_ge(var_ready, 3)
            act.activation(keep.bonus[:, :, :], uw[:, :, :], ACT.Exp).then_inc(expo, 1)
            act.wait_ge(step, folds[0])
            act.dma_start(f13_d.rearrange("(k p) n -> p k n", p=CT), f13[:, :, :]).then_inc(stored, 16)
            act.dma_start(f5a_d.rearrange("(k p) n -> p k n", p=CT), f5[:, 0]).then_inc(stored, 16)
            act.dma_start(f5f_d.rearrange("(k p) n -> p k n", p=CT), f5[:, 1]).then_inc(stored, 16)
            act.dma_start(bias_d, sd[0:1, 0, :]).then_inc(stored, 16)
            act.wait_ge(stored, 64)


def pointwise(nc, B, x, wpw, shift_pw, xpw_d):
    with ExitStack() as ctx:
        m = Mem(nc, ctx)
        xin = [m.sb(f"xin{u}", [CT, KT, HW]) for u in range(2)]
        xp = [m.sb(f"xp{u}", [PXC, C, PJ]) for u in range(2)]
        NB = 7
        ps = [m.ps(f"pw_ps{i}") for i in range(NB)]
        loaded = [m.sem(f"x_loaded{u}") for u in range(2)]
        ps_ready = m.sem("pw_product_ready")
        ps_free = m.sem("pw_bank_free")
        stored = [m.sem(f"xpw_stored{u}") for u in range(2)]
        PAIRS = PJ // 2
        block = ctx.enter_context(nc.Block())

        def load(sp, b, u):
            sp.dma_start(xin[u][:, :, :], dram(x, b * C * HW, [[HW, CT], [CT * HW, KT], [1, HW]])
                         ).then_inc(loaded[u], 16)

        @block.sync
        def _(sp):
            load(sp, 0, 0)
            load(sp, 1, 1)
            with sp.Fori(0, B // 2 - 1) as i:
                for u in range(2):
                    sp.wait_ge(ps_ready, (i * 2 + u + 1) * PAIRS)
                    load(sp, i * 2 + (u + 2), u)

        @block.tensor
        def _(pe):
            with pe.Fori(0, B // 2) as i:
                for u in range(2):
                    pe.wait_ge(loaded[u], i * 16 + 16)
                    for jp in range(PAIRS):
                        pe.wait_ge(ps_free, i * (2 * PAIRS) + (u * PAIRS + jp + 1))
                        bank = ps[jp % NB]
                        for q in range(2):
                            j = 2 * jp + q
                            for k in range(KT):
                                mm = pe.matmul(bank[0:PXC, q * C:(q + 1) * C],
                                               xin[u][:, k, j * PXC:(j + 1) * PXC], wpw[:, k, :],
                                               start=(k == 0), stop=(k == KT - 1))
                        mm.then_inc(ps_ready, 1)

        @block.vector
        def _(dve):
            dve.sem_inc(ps_free, NB)
            with dve.Fori(0, B // 2) as i:
                for u in range(2):
                    dve.wait_ge(stored[u], i * 16 + 16)
                    for jp in range(PAIRS):
                        dve.wait_ge(ps_ready, i * (2 * PAIRS) + (u * PAIRS + jp + 1))
                        dve.tensor_tensor(
                            xp[u][:, :, 2 * jp:2 * jp + 2],
                            ps[jp % NB][0:PXC, 0:2 * C].rearrange("p (q c) -> p c q", q=2),
                            free(shift_pw[0:PXC, :], [[1, C], [0, 2]]), ALU.add).then_inc(ps_free, 1)

        @block.scalar
        def _(act):
            for u in range(2):
                act.sem_inc(stored[u], 16)
            with act.Fori(0, B // 2) as i:
                for u in range(2):
                    act.wait_ge(ps_free, i * (2 * PAIRS) + ((u + 1) * PAIRS + NB))
                    act.dma_start(pair_batch(xpw_d, B, i * 2 + u),
                                  by_group(xp[u])
                                  ).then_inc(stored[u], 16)
            for u in range(2):
                act.wait_ge(stored[u], 16 * (B // 2 + 1))


def depthwise(nc, B, name, src, parts, k, f_d, dst, post, bias_d=None, norm=None, vecs=None,
              stats=None, flipped=False):
    dmax, centre, length, cols = band(k)
    N = B * PJ
    assert N <= 512
    with ExitStack() as ctx:
        m = Mem(nc, ctx)
        wt = [m.sb(f"{name}_band{u}", [PXP, G, cols]) for u in range(2)]
        raw = [m.sb(f"{name}_in{u}", [PXP, B, G, PJ]) for u in range(2)]
        z = [m.sb(f"{name}_norm{u}", [PXP, B, G, PJ]) for u in range(2)] if norm else raw
        out = [m.sb(f"{name}_out{u}", [PXP, B, G, PJ]) for u in range(2)]
        col = [m.sb(f"{name}_cols{u}", [PXP, 2, G]) for u in range(2)]
        ps = [m.ps(f"{name}_ps{i}") for i in range(G)]
        zeroed = m.sem(f"{name}_bands_zeroed")
        w_loaded = [m.sem(f"{name}_band_loaded{u}") for u in range(2)]
        in_loaded = [m.sem(f"{name}_in_loaded{u}") for u in range(2)]
        normed = m.sem(f"{name}_input_scaled")
        centred = m.sem(f"{name}_input_centred")
        z_ready = m.sem(f"{name}_input_ready")
        conv_done = m.sem(f"{name}_channel_convolved")
        ps_free = m.sem(f"{name}_bank_free")
        stored = [m.sem(f"{name}_stored{u}") for u in range(2)]
        out_read = m.sem(f"{name}_output_summed")
        if stats and not norm:
            sq = m.sb(f"{name}_squares", [PXP, B, G, PJ])
            part = [m.sb(f"{name}_part{n}", [PXP, B, PJ]) for n in range(2)]
            reduced = m.sem(f"{name}_group_reduced")
            summed = m.sem(f"{name}_sums_updated")
        block = ctx.enter_context(nc.Block())
        IN = 48 if norm else 32
        BASE = 2 * G if norm else 0
        step_in = PITCH if parts == PXP else W

        @block.sync
        def _(sp):
            def load(g, u):
                whole = raw[u][:, :, :, :].rearrange("p b c j -> p (b c j)")
                if parts == PXC:
                    sp.dma_start(whole[0:PXC], pair_group(src, B, g)).then_inc(in_loaded[u], 16)
                else:
                    copy_pairs(sp, whole, pair_group(src, B, g), in_loaded[u])
                if norm:
                    sp.dma_start(col[u][:, :, :], dram(vecs, V[norm] * C + g * G, [[0, PXP], [C, 2], [1, G]])
                                 ).then_inc(in_loaded[u], 16)
                if bias_d is not None:
                    sp.dma_start(col[u][:, 0, :], dram(bias_d, g * G, [[0, PXP], [1, G]])
                                 ).then_inc(in_loaded[u], 16)
                for r in range(2):
                    sp.dma_start(wt[u][r * step_in:r * step_in + W, :, :],
                                 dram(f_d, g * (G * length) + PITCH * r, [[1, W], [length, G], [1, cols]])
                                 ).then_inc(w_loaded[u], 16)

            sp.wait_ge(zeroed, 4 if parts == PXP else 2)
            load(0, 0)
            load(1, 1)
            with sp.Fori(0, NG // 2 - 1) as i:
                for u in range(2):
                    sp.wait_ge(ps_free, i * (2 * G) + G * (u + 2))
                    load(i * 2 + (u + 2), u)

        @block.tensor
        def _(pe):
            if norm:
                pe.sem_inc(conv_done, 2 * G)
            with pe.Fori(0, NG // 2) as i:
                for u in range(2):
                    pe.wait_ge(w_loaded[u], i * 32 + 32)
                    if norm:
                        pe.wait_ge(z_ready, i * (2 * G) + G * (u + 1))
                    else:
                        pe.wait_ge(in_loaded[u], i * IN + IN)
                    for cc in range(G):
                        pe.wait_ge(ps_free, i * (2 * G) + (u * G + cc + 1))
                        bank = ps[cc][0:PXP, 0:N].rearrange("p (b j) -> p b j", b=B)
                        order = [0] + [s * d for d in range(1, dmax + 1) for s in (1, -1)]
                        for n, d in enumerate(order):
                            lo, hi = max(0, -d), min(PJ, PJ - d)
                            at = 2 * PITCH * (dmax - d if flipped else dmax + d)
                            mm = pe.matmul(bank[:, :, lo:hi],
                                           wt[u][0:parts, cc, at:at + PXP],
                                           z[u][0:parts, :, cc, lo + d:hi + d],
                                           start=(n == 0), stop=(n == len(order) - 1))
                        mm.then_inc(conv_done, 1)

        @block.vector
        def _(dve):
            for u in range(2):
                dve.memset(wt[u][:, :, :], 0.0).then_inc(zeroed, 1)
                if parts == PXP:
                    dve.memset(raw[u][:, :, :, :], 0.0).then_inc(zeroed, 1)
            if norm:
                rs, ms = stats
                wide = lambda t: free(t, [[PJ, B], [0, G], [1, PJ]])
                with dve.Fori(0, NG // 2) as i:
                    for u in range(2):
                        dve.wait_ge(in_loaded[u], i * IN + IN)
                        dve.wait_ge(conv_done, i * (2 * G) + G * (u + 1))
                        dve.tensor_mul(z[u][:, :, :, :], raw[u][:, :, :, :], wide(rs[:, :])).then_inc(normed, 1)
                        dve.wait_ge(normed, i * 2 + (u + 1))
                        dve.tensor_sub(z[u][:, :, :, :], z[u][:, :, :, :], wide(ms[:, :])).then_inc(centred, 1)
                        dve.wait_ge(centred, i * 2 + (u + 1))
                        for cc in range(G):
                            v = z[u][:, :, cc, :]
                            dve.tensor_scalar(v, v, col[u][:, 0, cc:cc + 1], col[u][:, 1, cc:cc + 1],
                                              ALU.mult, ALU.add).then_inc(z_ready, 1)
            elif stats:
                s1, s2 = stats
                dve.memset(s1[:, :], 0.0).then_inc(summed, 1)
                dve.memset(s2[:, :], 0.0).then_inc(summed, 1)
                dve.sem_inc(out_read, 2)
                by_pixel = lambda t: t[:, :, :, :].rearrange("p b c j -> p b j c")
                flat = lambda t: t[:, :, :].rearrange("p b j -> p (b j)")
                with dve.Fori(0, NG // 2) as i:
                    for u in range(2):
                        dve.wait_ge(ps_free, i * (2 * G) + (G * (u + 2)))
                        dve.wait_ge(summed, i * 4 + (2 * u + 2))
                        dve.tensor_reduce(part[0][:, :, :], by_pixel(out[u]), AX_X, ALU.add).then_inc(reduced, 1)
                        dve.wait_ge(reduced, i * 4 + (2 * u + 1))
                        dve.tensor_add(s1[:, :], s1[:, :], flat(part[0])).then_inc(summed, 1)
                        dve.tensor_mul(sq[:, :, :, :], out[u][:, :, :, :], out[u][:, :, :, :]).then_inc(out_read, 1)
                        dve.wait_ge(out_read, i * 2 + (u + 3))
                        dve.tensor_reduce(part[1][:, :, :], by_pixel(sq), AX_X, ALU.add).then_inc(reduced, 1)
                        dve.wait_ge(reduced, i * 4 + (2 * u + 2))
                        dve.tensor_add(s2[:, :], s2[:, :], flat(part[1])).then_inc(summed, 1)

        @block.scalar
        def _(act):
            act.sem_inc(ps_free, G)
            for u in range(2):
                act.sem_inc(stored[u], 32)
            with act.Fori(0, NG // 2) as i:
                for u in range(2):
                    act.wait_ge(stored[u], i * 32 + 32)
                    if stats and not norm:
                        act.wait_ge(out_read, i * 2 + (u + 1))
                    for cc in range(G):
                        act.wait_ge(conv_done, i * (2 * G) + (BASE + u * G + cc + 1))
                        o = out[u][:, :, cc, :]
                        p = ps[cc][0:PXP, 0:N].rearrange("p (b j) -> p b j", b=B)
                        if post == "gelu":
                            act.activation(o, p, ACT.Gelu, bias=col[u][:, 0, cc:cc + 1]).then_inc(ps_free, 1)
                        else:
                            act.activation(o, p, ACT.Copy).then_inc(ps_free, 1)
                    act.wait_ge(ps_free, i * (2 * G) + (G * (u + 2)))
                    copy_pairs(act, pair_group(dst, B, i * 2 + u),
                               out[u][:, :, :, :].rearrange("p b c j -> p (b c j)"), stored[u])
            for u in range(2):
                act.wait_ge(stored[u], 32 * (NG // 2 + 1))


def norm_scales(nc, name, s1, s2, s1_d=None, s2_d=None):
    with ExitStack() as ctx:
        m = Mem(nc, ctx)
        t = m.sb(f"{name}_mean_squared", list(s1.shape))
        cleared = m.sem(f"{name}_gap_cleared")
        loaded = m.sem(f"{name}_sums_loaded")
        var_ready = m.sem(f"{name}_variance_ready")
        root = m.sem(f"{name}_root_ready")
        step = m.sem(f"{name}_steps")
        block = ctx.enter_context(nc.Block())

        if s1_d is not None:
            @block.sync
            def _(sp):
                sp.wait_ge(cleared, 2)
                copy_pairs(sp, s1[:, :], s1_d, loaded)
                copy_pairs(sp, s2[:, :], s2_d, loaded)

        @block.vector
        def _(dve):
            if s1_d is not None:
                dve.memset(s1[:, :], 0.0).then_inc(cleared, 1)
                dve.memset(s2[:, :], 0.0).then_inc(cleared, 1)
                dve.wait_ge(loaded, 64)
            dve.tensor_scalar_mul(s1[:, :], s1[:, :], 1.0 / C).then_inc(step, 1)
            dve.wait_ge(step, 1)
            dve.tensor_mul(t[:, :], s1[:, :], s1[:, :]).then_inc(step, 1)
            dve.wait_ge(step, 2)
            dve.scalar_tensor_tensor(s2[:, :], s2[:, :], 1.0 / C, t[:, :], ALU.mult, ALU.subtract
                                     ).then_inc(step, 1)
            dve.wait_ge(step, 3)
            dve.tensor_scalar(s2[:, :], s2[:, :], 0.0, LN_EPS, ALU.max, ALU.add).then_inc(var_ready, 1)
            dve.wait_ge(root, 1)
            dve.reciprocal(s2[:, :], s2[:, :]).then_inc(step, 1)
            dve.wait_ge(step, 4)
            dve.tensor_mul(s1[:, :], s1[:, :], s2[:, :]).then_inc(step, 1)

        @block.scalar
        def _(act):
            act.wait_ge(var_ready, 1)
            act.activation(s2[:, :], s2[:, :], ACT.Sqrt).then_inc(root, 1)


def transposed(bank, reverse=False):
    s = -1 if reverse else 1
    return free(bank[0:CT, :], [[PXP, JC], [s * PITCH, 2], [s, W]], PXP - 1 if reverse else 0)


def attention(nc, B, keep, mix_d, y_d, tok_d, s1_d, s2_d):
    with ExitStack() as ctx:
        m = Mem(nc, ctx)
        X = m.sb("mix_pairs", [PXP, C, PJ])
        Y = m.sb("residual_pairs", [PXC, C, PJ])
        xT = m.sb("mixT", [CT, KT, HW])
        kS = m.sb("k_all", [CT, KT, HW])
        vS = m.sb("v_all", [CT, KT, HW])
        rS = m.sb("r_all", [CT, KT, HW])
        att = m.sb("gated_wkv", [CT, KT, HW])
        s1 = m.sb("tok_sum", [PXC, PJ])
        s2 = m.sb("tok_square_sum", [PXC, PJ])
        junk = m.sb("tok_squares", [PXC, C])
        z_ps = [m.ps(f"mixT_ps{i}") for i in range(KT)]
        u_ps = [m.ps(f"proj_ps{i}") for i in range(3)]
        o_ps = [m.ps(f"out_ps{i}") for i in range(2)]

        x_loaded = m.sem("mix_loaded")
        y_loaded = m.sem("residual_loaded")
        pads = m.sem("gaps_cleared")
        zt_ready = m.sem("mixT_in_psum")
        xT_ready = m.sem("mixT_in_sbuf")
        un_ready = m.sem("projection_in_psum")
        un_read = m.sem("projection_evacuated")
        kt_done = m.sem("k_by_column_done")
        sr_done = m.sem("receptance_ready")
        g_done = m.sem("wkv_gated")
        out_ps_ready = m.sem("attention_out_in_psum")
        tok_done = m.sem("tok_done")
        sq_done = m.sem("tok_squared")
        stored = m.sem("tok_stored")

        O = [m.sb(f"run_max{u}", [CT, 1 + QT]) for u in range(RING)]
        A = [m.sb(f"decay_factor{u}", [CT, QT]) for u in range(2)]
        E = [m.sb(f"input_factor{u}", [CT, QT]) for u in range(RING)]
        EV = [m.sb(f"input_times_v{u}", [CT, QT]) for u in range(2)]
        P = [m.sb(f"numerator_state{u}", [CT, QT]) for u in range(RING)]
        Q = [m.sb(f"denominator_state{u}", [CT, QT]) for u in range(RING)]
        carry_done = m.sem("run_max_carried")
        o_done = m.sem("run_max_done")
        a_arg = m.sem("decay_exponent_done")
        e_arg = m.sem("input_exponent_done")
        a_exp = m.sem("decay_factor_ready")
        e_exp = m.sem("input_factor_ready")
        ev_done = m.sem("input_times_v_done")
        p_done = m.sem("numerator_scan_done")
        q_done = m.sem("denominator_scan_done")
        n_done = m.sem("numerator_done")
        d_done = m.sem("denominator_done")
        ln_done = m.sem("denominator_logged")
        rec_done = m.sem("denominator_inverted")
        wkv_done = m.sem("wkv_divided")
        block = ctx.enter_context(nc.Block())
        UC = 3
        UT = UC * NCH
        ZT = KT * NCH

        class Tile:

            def __init__(self, i, m_):
                self.i, self.m, self.ct = i, m_, m_ % 2

            def at(self, per, offset=0):
                return self.i * (2 * per) + (self.m * per + offset)

            def image(self, per, offset=0):
                return self.i * per + (self.m // 2 * per + offset)

        class Image:
            def __init__(self, i):
                self.i = i

            def at(self, per, offset):
                return self.i * per + offset

        def need(eng, sem, value):
            if not isinstance(value, int) or value > 0:
                eng.wait_ge(sem, value)

        def at_superstep(i, m_, of):
            return isinstance(i, int) and (i, m_) == of

        FIRST, SECOND, LAST = (0, 0), (0, 1), (B - 1, 2)
        columns_at = [p for p in range(UNITS) if p not in ROWS_AT]

        class Unit:

            def __init__(self, i, m_, rows, q, position):
                self.i, self.m, self.rows, self.q, self.position = i, m_, rows, q, position
                self.tile = Tile(i, m_ if rows else m_ - 1)
                self.ct, self.way = self.tile.ct, 0 if rows else 1
                self.slot = (UNITS * (m_ % 2) + position) % RING
                self.bonus = keep.bonus[:, self.ct, self.way:self.way + 1]
                self.decay = keep.decay[:, self.ct, self.way:self.way + 1]

            def count(self, before=0):
                return self.i * (2 * UNITS) + (self.m * UNITS + self.position + 1 - before)

        def units_of(i, m_):
            if at_superstep(i, m_, FIRST):
                return [Unit(i, m_, True, q, NQ + q) for q in range(NQ)]
            if at_superstep(i, m_, LAST):
                return [Unit(i, m_, False, q, q) for q in range(NQ)]
            return [Unit(i, m_, True, ROWS_AT.index(p), p) if p in ROWS_AT
                    else Unit(i, m_, False, columns_at.index(p), p) for p in range(UNITS)]

        def stepped(i, m_):
            now = units_of(i, m_)
            old = [None] if at_superstep(i, m_, FIRST) else units_of(i, m_ - 1)[-1:]
            new = [None, None] if at_superstep(i, m_, LAST) else units_of(i, m_ + 1)[:2]
            line = old + now + new
            return [(line[n + 1], line[n], line[n + 2], line[n + 3]) for n in range(len(now))]

        def former(unit):
            if at_superstep(unit.i, unit.m, FIRST) or at_superstep(unit.i, unit.m, LAST):
                back = 1
            else:
                back = unit.position - (ROWS_AT if unit.rows else columns_at)[unit.q - 1]
            return (unit.slot - back) % RING, unit.count(back)

        def supersteps(eng, step):
            step(0, 0)
            step(0, 1)
            with eng.Fori(0, B - 1) as i:
                step(i, 2)
                step(i, 3, done=Image(i))
            step(B - 1, 2)

        def part_of(t, unit):
            if unit.rows:
                return t[:, unit.ct, unit.q * QT:(unit.q + 1) * QT].rearrange("p (a b) -> p a b", b=W)
            by_column = t[:, unit.ct, :].rearrange("p (r w) -> p w r", r=W)
            return by_column[:, unit.q * QW:(unit.q + 1) * QW, :]

        def grid(t):
            return t[:, 0:QT].rearrange("p (a b) -> p a b", b=W)

        @block.sync
        def _(sp):
            def load_x(b):
                copy_pairs(sp, by_group(X), pair_batch(mix_d, B, b), x_loaded)

            def load_y(b, offset=None):
                sp.dma_start(by_group(Y), pair_batch(y_d, B, b, offset)).then_inc(y_loaded, 16)

            def store(b, squares, stores):
                sp.wait_ge(sq_done, squares)
                sp.dma_start(pair_batch(tok_d, B, b), by_group(Y)).then_inc(stored, 16)
                for d, t in ((s1_d, s1), (s2_d, s2)):
                    sp.dma_start(dram(d, b * PJ, [[B * PJ, PXC], [1, PJ]]), t[:, :]).then_inc(stored, 16)
                sp.wait_ge(stored, stores)

            sp.wait_ge(pads, 1)
            load_x(0)
            load_y(0)
            sp.wait_ge(zt_ready, ZT)
            load_x(1)
            with sp.Fori(0, B - 2) as i:
                sp.wait_ge(zt_ready, i * ZT + 2 * ZT)
                load_x(i + 2)
                next_y = sp.snap((i + 1) * (G * PJ))
                marks = [sp.snap(i * n + a) for n, a in ((PJ, PJ + 1), (48, 48))]
                store(i, *marks)
                load_y(i + 1, next_y)
            store(B - 2, (B - 1) * PJ + 1, (B - 1) * 48)
            load_y(B - 1)
            store(B - 1, B * PJ + 1, B * 48)

        @block.tensor
        def _(pe):
            pe.wait_ge(pads, 1)

            def turn(r, t):
                for ct in range(KT):
                    pe.wait_ge(xT_ready, r.image(ZT, KT * t + ct + 1))
                    for jj in range(JC):
                        tr = pe.transpose(z_ps[ct][0:CT, jj * PXP:(jj + 1) * PXP],
                                          X[:, ct * CT:(ct + 1) * CT, JC * t + jj], keep.ident[:, :])
                    tr.then_inc(zt_ready, 1)

            def project(r, t):
                if r.ct == 0:
                    pe.wait_ge(xT_ready, r.image(ZT, KT * (t + 1) + KT))
                for o in range(UC):
                    pe.wait_ge(un_read, r.at(UT, UC * t + o + 1))
                    for k in range(KT):
                        mm = pe.matmul(u_ps[o][0:CT, 0:TC], keep.wkvr[:, k, o, r.ct * CT:(r.ct + 1) * CT],
                                       xT[:, k, t * TC:(t + 1) * TC], start=(k == 0), stop=(k == KT - 1))
                    mm.then_inc(un_ready, 1)

            def project_out(image, group):
                if group == 0:
                    pe.wait_ge(g_done, image.at(2, 3))
                for jp in (2 * group, 2 * group + 1):
                    pe.wait_ge(tok_done, image.at(PJ, 2 * jp + 1))
                    for q in range(2):
                        j = 2 * jp + q
                        for ct in range(KT):
                            mm = pe.matmul(o_ps[jp % 2][0:PXC, q * C:(q + 1) * C],
                                           att[:, ct, PXC * j:PXC * (j + 1)],
                                           keep.wo[:, ct, :], start=(ct == 0), stop=(ct == KT - 1))
                    mm.then_inc(out_ps_ready, 1)

            def step(i, m_, done=None):
                if not any(unit.rows for unit in units_of(i, m_)):
                    return
                r = Tile(i, m_)
                if r.ct == 0:
                    pe.wait_ge(x_loaded, r.image(32, 32))
                    turn(r, 0)
                for t in range(NCH):
                    if t + 1 < NCH and r.ct == 0:
                        turn(r, t + 1)
                    project(r, t)
                    if t > 1 and done is not None:
                        project_out(done, t - 2)
                if done is not None:
                    project_out(done, NCH - 2)
                    project_out(done, NCH - 1)

            supersteps(pe, step)
            for group in range(NCH):
                project_out(Image(B - 1), group)

        @block.scalar
        def _(act):
            act.sem_inc(xT_ready, KT)
            act.sem_inc(un_read, UC)
            act.sem_inc(sq_done, 1)
            for sem in (a_exp, e_exp, ln_done, rec_done):
                act.sem_inc(sem, NQ)

            def mix(r, t):
                if r.ct or t >= NCH:
                    return
                need(act, un_ready, r.at(UT, UC * (t + 1) - UT))
                for ct in range(KT):
                    act.wait_ge(zt_ready, r.image(ZT, KT * t + ct + 1))
                    act.activation(xT[:, ct, t * TC:(t + 1) * TC].rearrange("p (j r w) -> p j r w", j=JC, r=2),
                                   transposed(z_ps[ct], reverse=True), ACT.Copy).then_inc(xT_ready, 1)

            def evacuate(r, t):
                if t == 0:
                    need(act, g_done, r.at(1))
                for o, dst in enumerate((kS, vS, rS)):
                    act.wait_ge(un_ready, r.at(UT, UC * t + o + 1))
                    act.activation(dst[:, r.ct, TC * t:TC * (t + 1)], u_ps[o][0:CT, 0:TC], ACT.Copy
                                   ).then_inc(un_read, 1)

            def receptance(r):
                act.wait_ge(un_read, r.at(UT, UT + UC))
                act.activation(rS[:, r.ct, :], rS[:, r.ct, :], ACT.Sigmoid).then_inc(sr_done, 1)
                act.preload_act_table_set("natural_log_exp_and_others")

            def factors(unit):
                act.wait_ge(e_arg, unit.count())
                act.activation(E[unit.slot][:, :], E[unit.slot][:, :], ACT.Exp).then_inc(e_exp, 1)
                act.wait_ge(a_arg, unit.count())
                act.activation(A[unit.slot % 2][:, :], A[unit.slot % 2][:, :], ACT.Exp, bias=unit.decay
                               ).then_inc(a_exp, 1)

            def invert(unit):
                e = E[unit.slot][:, :]
                act.wait_ge(d_done, unit.count())
                act.activation(e, e, ACT.Ln).then_inc(ln_done, 1)
                act.wait_ge(ln_done, unit.count())
                act.activation(e, e, ACT.Exp, scale=-1.0).then_inc(rec_done, 1)

            def column_k(unit):
                if unit is None or unit.rows:
                    return
                if unit.q == 0:
                    act.wait_ge(un_read, unit.tile.at(UT, UT + UC))
                act.wait_ge(wkv_done, unit.count(RING))
                act.activation(grid(E[unit.slot]), part_of(kS, unit), ACT.Copy).then_inc(kt_done, 1)

            def squares(image, group):
                for j in range(JC * group, JC * (group + 1)):
                    act.wait_ge(tok_done, image.at(PJ, j + 4))
                    act.wait_ge(sq_done, image.at(PJ, j + 1))
                    act.activation(junk[:, :], Y[:, :, j], ACT.Square, accum_out=s2[:, j:j + 1]
                                   ).then_inc(sq_done, 1)

            def step(i, m_, done=None):
                steps = stepped(i, m_)
                rows = any(unit.rows for unit in units_of(i, m_))
                r = Tile(i, m_)
                if rows:
                    mix(r, 0)
                if steps[0][1] is None:
                    mix(r, 1)
                    for t in range(NCH):
                        evacuate(r, t)
                        mix(r, t + 2)
                    factors(steps[0][0])
                for unit, before, after, second in steps:
                    column_k(second)
                    if after is not None:
                        factors(after)
                    if rows and steps[0][1] is not None and unit.position + 2 in ROWS_AT:
                        t = ROWS_AT.index(unit.position + 2)
                        evacuate(r, t)
                        mix(r, t + 2)
                    invert(unit)
                    if rows and steps[0][1] is not None and unit.position == 0:
                        mix(r, 1)
                    if rows and unit.position == UNITS - 3:
                        receptance(r)
                    if done is not None and unit.position - 1 in RESIDUAL_AT:
                        squares(done, RESIDUAL_AT.index(unit.position - 1))
                if done is not None:
                    squares(done, NCH - 1)

            supersteps(act, step)
            for group in range(NCH):
                squares(Image(B - 1), group)

        @block.gpsimd
        def _(pool):
            for sem in (wkv_done, a_arg, e_arg, ev_done):
                pool.sem_inc(sem, NQ)

            def exponents(unit):
                pool.wait_ge(wkv_done, unit.count(RING))
                pool.wait_ge(q_done, unit.count(2))
                pool.wait_ge(carry_done, unit.count())
                pool.wait_ge(o_done, unit.count())
                o, e = O[unit.slot], E[unit.slot]
                k = kS[:, unit.ct, unit.q * QT:(unit.q + 1) * QT] if unit.rows else e[:, :]
                pool.tensor_tensor(e[:, :], k, o[:, 1:1 + QT], ALU.subtract).then_inc(e_arg, 1)
                pool.tensor_tensor(A[unit.slot % 2][:, :], o[:, 0:QT], o[:, 1:1 + QT], ALU.subtract
                                   ).then_inc(a_arg, 1)

            def weigh(unit):
                if unit.rows:
                    pool.wait_ge(un_read, unit.tile.at(UT, UC * unit.q + UC + 2))
                pool.wait_ge(wkv_done, unit.count(
                    1 if at_superstep(unit.i, unit.m, SECOND) and unit.position == 0 else 2))
                pool.wait_ge(e_exp, unit.count())
                pool.tensor_tensor(grid(EV[unit.slot % 2]), grid(E[unit.slot]), part_of(vS, unit), ALU.mult
                                   ).then_inc(ev_done, 1)

            def divide(unit):
                pool.wait_ge(n_done, unit.count())
                pool.wait_ge(rec_done, unit.count())
                pool.tensor_tensor(part_of(vS, unit), grid(EV[unit.slot % 2]), grid(E[unit.slot]), ALU.mult
                                   ).then_inc(wkv_done, 1)

            def step(i, m_, done=None):
                steps = stepped(i, m_)
                if steps[0][1] is None:
                    exponents(steps[0][0])
                for unit, before, after, _ in steps:
                    at_once = at_superstep(i, m_, SECOND) and unit.position == 0
                    if at_once:
                        divide(before)
                    weigh(unit)
                    if after is not None:
                        exponents(after)
                    if before is not None and not at_once:
                        divide(before)
                if after is None:
                    divide(unit)

            supersteps(pool, step)

        @block.vector
        def _(dve):
            dve.memset(X[:, :, :], 0.0).then_inc(pads, 1)
            dve.sem_inc(tok_done, 3)
            dve.sem_inc(g_done, 1)

            for sem in (carry_done, o_done, p_done, q_done, n_done, d_done):
                dve.sem_inc(sem, NQ)

            def run_max(unit):
                if unit.rows:
                    dve.wait_ge(un_read, unit.tile.at(UT, UC * unit.q + UC + 1))
                    k = kS[:, unit.ct, unit.q * QT:(unit.q + 1) * QT]
                else:
                    dve.wait_ge(kt_done, unit.tile.at(NQ, unit.q + 1))
                    k = E[unit.slot][:, :]
                o = O[unit.slot]
                if unit.q == 0:
                    dve.memset(o[:, 0:1], NEG).then_inc(carry_done, 1)
                    start = NEG
                else:
                    slot, count = former(unit)
                    dve.wait_ge(o_done, count)
                    start = O[slot][:, QT:QT + 1]
                    dve.tensor_copy(o[:, 0:1], start).then_inc(carry_done, 1)
                dve.tensor_tensor_scan(o[:, 1:1 + QT], free(unit.decay, [[0, QT]]), k, start,
                                       ALU.add, ALU.max).then_inc(o_done, 1)

            def scan(unit, state, factor, added):
                start = state[former(unit)[0]][:, QT - 1:QT] if unit.q else 0.0
                return dve.tensor_tensor_scan(state[unit.slot][:, :], factor[:, :], added[:, :], start,
                                              ALU.mult, ALU.add)

            def sums(unit):
                a = A[unit.slot % 2]
                dve.wait_ge(e_exp, unit.count())
                dve.wait_ge(a_exp, unit.count())
                dve.wait_ge(d_done, unit.count(RING))
                scan(unit, Q, a, E[unit.slot]).then_inc(q_done, 1)
                dve.wait_ge(ev_done, unit.count())
                dve.wait_ge(n_done, unit.count(RING))
                scan(unit, P, a, EV[unit.slot % 2]).then_inc(p_done, 1)

            def outputs(unit):
                e, ev = E[unit.slot][:, :], EV[unit.slot % 2][:, :]
                dve.wait_ge(q_done, unit.count())
                dve.scalar_tensor_tensor(e, e, unit.bonus, Q[unit.slot][:, :], ALU.mult, ALU.add
                                         ).then_inc(d_done, 1)
                dve.wait_ge(p_done, unit.count())
                dve.scalar_tensor_tensor(ev, ev, unit.bonus, P[unit.slot][:, :], ALU.mult, ALU.add
                                         ).then_inc(n_done, 1)

            def gate(tile):
                dve.wait_ge(sr_done, tile.at(1, 1))
                dve.wait_ge(wkv_done, tile.at(UNITS, UNITS + NQ if at_superstep(tile.i, tile.m + 1, LAST)
                                              else 2 * UNITS))
                dve.tensor_tensor(att[:, tile.ct, :], vS[:, tile.ct, :], rS[:, tile.ct, :], ALU.mult
                                  ).then_inc(g_done, 1)

            def add_residual(image, group):
                if group == 0:
                    dve.wait_ge(y_loaded, image.at(16, 16))
                for j in range(JC * group, JC * (group + 1)):
                    q = j % 2
                    if q == 0:
                        dve.wait_ge(out_ps_ready, image.at(PJ // 2, j // 2 + 1))
                    dve.scalar_tensor_tensor(Y[:, :, j], o_ps[(j // 2) % 2][0:PXC, q * C:(q + 1) * C], 1.0,
                                             Y[:, :, j], ALU.mult, ALU.add, accum_out=s1[:, j:j + 1]
                                             ).then_inc(tok_done, 1)

            def step(i, m_, done=None):
                steps = stepped(i, m_)
                if steps[0][1] is None:
                    run_max(steps[0][0])
                    run_max(steps[1][0])
                for unit, before, after, second in steps:
                    if unit.position == 1 and m_ > 1:
                        gate(Tile(i, m_ - 2))
                    sums(unit)
                    outputs(unit)
                    if second is not None:
                        run_max(second)
                    if done is not None and unit.position in RESIDUAL_AT:
                        add_residual(done, RESIDUAL_AT.index(unit.position))

            supersteps(dve, step)
            gate(Tile(B - 1, 1))
            for group in range(NCH):
                add_residual(Image(B - 1), group)


def feed_forward(nc, B, ins, keep, mix_d, tok_d, out):
    with ExitStack() as ctx:
        m = Mem(nc, ctx)
        X = [m.sb(f"ffn_mix{u}", [PXP, C, PJ]) for u in range(2)]
        T = [m.sb(f"ffn_tok{u}", [PXP, C, PJ]) for u in range(2)]
        wk = m.sb("ffn_wk", [CT, KT, HID])
        wv = m.sb("ffn_wv", [128, HT, C])
        wr = m.sb("ffn_wr", [CT, KT, C])
        gam = m.sb("gamma2", [128, C])
        xT = [m.sb(f"ffn_mixT{u}", [CT, KT, TC]) for u in range(2)]
        kk = [m.sb(f"hidden{u}", [128, HT, TC]) for u in range(2)]
        sg = [m.sb(f"ffn_gate{u}", [CT, KT, TC]) for u in range(2)]
        gv = m.sb("gated", [CT, KT, TC])
        res = [m.sb(f"result{u}", [CT, KT, TC]) for u in range(2)]
        z_ps = [m.ps(f"f_mixT_ps{i}") for i in range(KT)]
        t_ps = [m.ps(f"f_tokT_ps{i}") for i in range(KT)]
        h_ps = [m.ps(f"f_hid_ps{i}") for i in range(2)]
        v_ps = [m.ps(f"f_out_ps{i}") for i in range(KT)]
        w_loaded = m.sem("ffn_weights_loaded")
        w_folded = m.sem("ffn_gamma_folded")
        gaps = m.sem("ffn_gaps_cleared")
        x_loaded = [m.sem(f"ffn_mix_loaded{u}") for u in range(2)]
        t_loaded = [m.sem(f"ffn_tok_loaded{u}") for u in range(2)]
        zt_ready = m.sem("ffn_mixT_in_psum")
        xT_ready = m.sem("ffn_mixT_in_sbuf")
        r_ready = m.sem("ffn_r_in_psum")
        h_ready = m.sem("ffn_hidden_in_psum")
        g_ready = m.sem("ffn_gate_ready")
        relu_done = m.sem("ffn_hidden_clipped")
        kk_ready = m.sem("ffn_hidden_squared")
        tt_ready = m.sem("ffn_tokT_in_psum")
        v_ready = m.sem("ffn_out_in_psum")
        gv_done = m.sem("ffn_out_gated")
        res_done = m.sem("result_ready")
        stored = [m.sem(f"result_stored{u}") for u in range(2)]
        block = ctx.enter_context(nc.Block())
        CH = 2 * NCH

        @block.tensor
        def _(pe):
            pe.wait_ge(w_loaded, 64)
            pe.wait_ge(w_folded, HT)
            pe.sem_inc(h_ready, 2 * HT)
            pe.sem_inc(v_ready, 2 * KT)
            with pe.Fori(0, B // 2) as i:
                def turn(n, src, banks, free_sem, ready):
                    u, t = n // NCH, n % NCH
                    for ct in range(KT):
                        pe.wait_ge(free_sem, i * (CH * KT) + (KT * n + ct + 1))
                        for jj in range(JC):
                            tr = pe.transpose(banks[ct][0:CT, jj * PXP:(jj + 1) * PXP],
                                              src[u][:, ct * CT:(ct + 1) * CT, JC * t + jj], keep.ident[:, :])
                        tr.then_inc(ready, 1)

                pe.wait_ge(x_loaded[0], i * 32 + 32)
                turn(0, X, z_ps, xT_ready, zt_ready)
                for n in range(CH):
                    pe.wait_ge(xT_ready, i * (CH * KT) + (KT * n + 2 * KT))
                    for a in range(KT + HT):
                        if a < KT:
                            if a == 0:
                                pe.wait_ge(relu_done, i * (CH * HT) + (HT * n + HT - 1 + 2))
                            else:
                                pe.wait_ge(relu_done, i * (CH * HT) + (HT * n + HT + 2))
                            w, M = wr[:, :, a * CT:(a + 1) * CT], CT
                        else:
                            h = a - KT
                            if h < 2:
                                pe.wait_ge(g_ready, i * (CH * KT) + (KT * n + h + 1))
                            else:
                                pe.wait_ge(relu_done, i * (CH * HT) + (HT * (n + 1) + h - 1 + 2))
                            w, M = wk[:, :, h * 128:(h + 1) * 128], 128
                        for k in range(KT):
                            mm = pe.matmul(h_ps[a % 2][0:M, 0:TC], w[:, k, :], xT[n % 2][:, k, :],
                                           start=(k == 0), stop=(k == KT - 1))
                        mm.then_inc(r_ready if a < KT else h_ready, 1)
                    if n + 1 < CH:
                        if n + 1 == NCH:
                            pe.wait_ge(x_loaded[1], i * 32 + 32)
                        turn(n + 1, X, z_ps, xT_ready, zt_ready)
                    if n % NCH == 0:
                        pe.wait_ge(t_loaded[n // NCH], i * 32 + 32)
                    turn(n, T, t_ps, res_done, tt_ready)
                    for ct in range(KT):
                        pe.wait_ge(gv_done, i * (CH * KT) + (KT * n + ct + 1))
                        for h in range(HT):
                            if ct == 0:
                                pe.wait_ge(kk_ready, i * (CH * HT) + (HT * n + h + 1))
                            mm = pe.matmul(v_ps[ct][0:CT, 0:TC], wv[:, h, ct * CT:(ct + 1) * CT],
                                           kk[n % 2][:, h, :], start=(h == 0), stop=(h == HT - 1))
                        mm.then_inc(v_ready, 1)

        @block.scalar
        def _(act):
            act.sem_inc(xT_ready, KT)
            with act.Fori(0, B // 2) as i:
                def mix(n):
                    act.wait_ge(h_ready, i * (CH * HT) + HT * (n + 1))
                    for ct in range(KT):
                        act.wait_ge(zt_ready, i * (CH * KT) + (KT * n + ct + 1))
                        act.activation(xT[n % 2][:, ct, :].rearrange("p (j r w) -> p j r w", j=JC, r=2),
                                       transposed(z_ps[ct], reverse=True), ACT.Copy).then_inc(xT_ready, 1)

                mix(0)
                for n in range(CH):
                    for ct in range(KT):
                        act.wait_ge(gv_done, i * (CH * KT) + (KT * n + 1))
                        act.wait_ge(r_ready, i * (CH * KT) + (KT * n + ct + 1))
                        act.activation(sg[n % 2][:, ct, :], h_ps[ct][0:CT, 0:TC], ACT.Sigmoid
                                       ).then_inc(g_ready, 1)
                    for h in range(HT):
                        act.wait_ge(relu_done, i * (CH * HT) + (HT * (n + 1) + h + 1 + 2))
                        act.activation(kk[n % 2][:, h, :], kk[n % 2][:, h, :], ACT.Square).then_inc(kk_ready, 1)
                    if n + 1 < CH:
                        mix(n + 1)

        @block.vector
        def _(dve):
            for t in (*X, *T):
                dve.memset(t[:, :, :], 0.0).then_inc(gaps, 1)
            dve.wait_ge(w_loaded, 64)
            for h in range(HT):
                dve.tensor_mul(wv[:, h, :], wv[:, h, :], gam[:, :]).then_inc(w_folded, 1)
            dve.sem_inc(relu_done, HT + 2)
            dve.sem_inc(gv_done, KT)
            dve.sem_inc(res_done, KT)
            for u in range(2):
                dve.sem_inc(stored[u], 16)
            with dve.Fori(0, B // 2) as i:
                for n in range(CH):
                    for h in range(HT):
                        if h == 0:
                            dve.wait_ge(v_ready, i * (CH * KT) + KT * (n + 1))
                        dve.wait_ge(h_ready, i * (CH * HT) + (HT * (n + 2) + h + 1))
                        bank = h_ps[h % 2][:, 0:TC]
                        dve.tensor_scalar_max(kk[n % 2][:, h, :], bank, 0.0).then_inc(relu_done, 1)
                    for ct in range(KT):
                        dve.wait_ge(v_ready, i * (CH * KT) + (KT * (n + 2) + ct + 1))
                        dve.wait_ge(g_ready, i * (CH * KT) + (KT * n + ct + 1))
                        dve.tensor_mul(gv[:, ct, :], v_ps[ct][0:CT, 0:TC], sg[n % 2][:, ct, :]
                                       ).then_inc(gv_done, 1)
                    for ct in range(KT):
                        if ct == 0:
                            dve.wait_ge(stored[n % 2], i * (16 * NCH) + 16 * (n // 2 + 1))
                        dve.wait_ge(gv_done, i * (CH * KT) + (KT * (n + 1) + ct + 1))
                        dve.wait_ge(tt_ready, i * (CH * KT) + (KT * n + ct + 1))
                        dve.tensor_tensor(res[n % 2][:, ct, :].rearrange("p (j r w) -> p j r w", j=JC, r=2),
                                          gv[:, ct, :].rearrange("p (j r w) -> p j r w", j=JC, r=2),
                                          transposed(t_ps[ct]), ALU.add).then_inc(res_done, 1)

        @block.sync
        def _(sp):
            for dst, src in [(wk, ins["ffn_wkt"].rearrange("(k p) n -> p k n", p=CT)),
                             (wv, ins["ffn_wvt"].rearrange("(k p) n -> p k n", p=128)),
                             (wr, ins["ffn_wrt"].rearrange("(k p) n -> p k n", p=CT))]:
                sp.dma_start(dst[:, :, :], src).then_inc(w_loaded, 16)
            sp.dma_start(gam[:, :], dram(ins["vecs"], V["gamma2"] * C, [[0, 128], [1, C]])).then_inc(w_loaded, 16)

            def load(b, u):
                copy_pairs(sp, by_group(X[u]), pair_batch(mix_d, B, b), x_loaded[u])
                copy_pairs(sp, by_group(T[u]), pair_batch(tok_d, B, b), t_loaded[u])

            def images(i, reload):
                for n in range(CH):
                    u, t = n // NCH, n % NCH
                    at = i * (2 * C * HW) + (u * C * HW + t * TC)
                    if reload:
                        at = sp.snap(at)
                    sp.wait_ge(res_done, i * (CH * KT) + (KT * (n + 2)))
                    sp.dma_start(dram(out, at, [[HW, CT], [CT * HW, KT], [1, TC]]), res[n % 2][:, :, :]
                                 ).then_inc(stored[n % 2], 16)
                    if t == NCH - 1 and reload:
                        load(i * 2 + (u + 2), u)

            sp.wait_ge(gaps, 4)
            load(0, 0)
            load(1, 1)
            with sp.Fori(0, B // 2 - 1) as i:
                images(i, True)
            images(B // 2 - 1, False)
            for u in range(2):
                sp.wait_ge(stored[u], 16 * (NCH * (B // 2) + 1))


class Kept:

    def __init__(self, m):
        self.ident = m.sb("identity", [PXP, PXP])
        self.wkvr = m.sb("kvr_weights", [CT, KT, 3, C])
        self.wo = m.sb("attention_out_weights", [CT, KT, C])
        self.decay = m.sb("wkv_decay", [CT, KT, 2])
        self.bonus = m.sb("wkv_bonus", [CT, KT, 2])


def build(nc, B, ins, out, debug=None):
    scratch = lambda name, shape: (debug or {}).get(name) or nc.dram_tensor(name, shape, F32).ap()
    pair_shape = [NG, PXC, B, G * PJ]
    xpw_d = scratch("x_pointwise", pair_shape)
    y_d = scratch("y_gelu", pair_shape)
    mixa_d = scratch("att_mix", pair_shape)
    tok_d = scratch("tok", pair_shape)
    mixf_d = scratch("ffn_mix", pair_shape)
    f13_d = scratch("flat13", [C, band(K13)[2]])
    f5a_d = scratch("flat5_att", [C, band(K5)[2]])
    f5f_d = scratch("flat5_ffn", [C, band(K5)[2]])
    bias_d = scratch("dw_bias", [1, C])
    s1_d = scratch("tok_sums", [PXC, B * PJ])
    s2_d = scratch("tok_square_sums", [PXC, B * PJ])
    with ExitStack() as ctx:
        m = Mem(nc, ctx)
        keep = Kept(m)
        with ExitStack() as inner:
            mi = Mem(nc, inner)
            wpw, shift_pw = mi.sb("pointwise_weights", [CT, KT, C]), mi.sb("pointwise_shift", [128, C])
            prepare(nc, ins, keep, wpw, shift_pw, f13_d, f5a_d, f5f_d, bias_d)
            pointwise(nc, B, ins["x"], wpw, shift_pw, xpw_d)
        with ExitStack() as inner:
            mi = Mem(nc, inner)
            s1, s2 = mi.sb("y_sum", [PXP, B * PJ]), mi.sb("y_square_sum", [PXP, B * PJ])
            depthwise(nc, B, "dw13", xpw_d, PXC, K13, f13_d, y_d, "gelu", bias_d=bias_d, stats=(s1, s2),
                      flipped=True)
            norm_scales(nc, "ln1", s1, s2)
            depthwise(nc, B, "omni1", y_d, PXP, K5, f5a_d, mixa_d, "copy", norm="ln1_g",
                      vecs=ins["vecs"], stats=(s2, s1))
        attention(nc, B, keep, mixa_d, y_d, tok_d, s1_d, s2_d)
        with ExitStack() as inner:
            mi = Mem(nc, inner)
            s1, s2 = mi.sb("t_sum", [PXP, B * PJ]), mi.sb("t_square_sum", [PXP, B * PJ])
            norm_scales(nc, "ln2", s1, s2, s1_d, s2_d)
            depthwise(nc, B, "omni2", tok_d, PXP, K5, f5f_d, mixf_d, "copy", norm="ln2_g",
                      vecs=ins["vecs"], stats=(s2, s1))
        feed_forward(nc, B, ins, keep, mixf_d, tok_d, out)


def layout(inputs):
    import numpy as np

    i = {k: np.asarray(v) for k, v in inputs.items()}
    l0, l1 = (lambda n: i["L0_conv_" + n]), (lambda n: i["L1_conv_" + n])
    vec = {n: l0(n) for n in VEC if n.startswith(("pw_", "dwk_", "dw1_"))}
    vec.update({n: l1(n) for n in VEC if n.startswith(("ln", "gamma"))})
    for n in range(2):
        vec[f"dec{n}"], vec[f"first{n}"] = l1("sp_decay")[n], l1("sp_first")[n]
    vecs = np.stack([vec[n] for n in VEC])
    plain = lambda w: np.ascontiguousarray(w[:, 0]).reshape(C, -1)
    flip = lambda w: np.ascontiguousarray(w[:, 0, ::-1, ::-1]).reshape(C, -1)
    x = i["x"]
    pairs = x.reshape(*x.shape[:2], PJ, 2, W)[:, :, :, ::-1, ::-1]
    cols = lambda a: np.ascontiguousarray(a.reshape(KT, CT).T)
    t = lambda a: np.ascontiguousarray(a.T)
    return {
        "x": np.ascontiguousarray(pairs).reshape(x.shape),
        "vecs": vecs,
        "vec_cols": np.ascontiguousarray(vecs.reshape(NV, KT, CT).transpose(2, 1, 0)),
        "alphas": np.concatenate([l1("att_alpha"), l1("ffn_alpha")]),
        "ident": np.eye(PXP, dtype=np.float32),
        "pw_wt": t(l0("pw_w")),
        "dwk_w": flip(l0("dwk_w")),
        "att_w5": plain(l1("att_w5")), "att_w3": plain(l1("att_w3")), "att_w1": cols(l1("att_w1")),
        "ffn_w5": plain(l1("ffn_w5")), "ffn_w3": plain(l1("ffn_w3")), "ffn_w1": cols(l1("ffn_w1")),
        "att_wt": np.stack([t(l1("att_wk")), t(l1("att_wv")), t(l1("att_wr"))]),
        "att_wot": t(l1("att_wo")),
        "ffn_wkt": t(l1("ffn_wk")), "ffn_wvt": t(l1("ffn_wv")), "ffn_wrt": t(l1("ffn_wr")),
    }


def kernel(**inputs):
    import concourse.bacc as bacc
    from concourse.bass_utils import run_bass_kernel_spmd

    arrays = layout(inputs)
    B = arrays["x"].shape[0]
    nc = bacc.Bacc("TRN2", target_bir_lowering=False, num_devices=1)
    ins = {n: nc.dram_tensor(n, a.shape, mybir.dt.from_np(a.dtype), kind="ExternalInput").ap()
           for n, a in arrays.items()}
    out = nc.dram_tensor("out", [B, C, W, W], F32, kind="ExternalOutput").ap()
    build(nc, B, ins, out)
    return run_bass_kernel_spmd(nc, [arrays], core_ids=[0]).results[0]["out"]
```

```python
from contextlib import ExitStack

import concourse.bass as bass
from concourse import mybir

F32 = mybir.dt.float32
F32R = mybir.dt.float32r
ALU = mybir.AluOpType
ACT = mybir.ActivationFunctionType
AX_X = mybir.AxisListType.X

C = 192
W = 56
HW = W * W
CT = 96
KT = C // CT
HID = 4 * C
HT = HID // 128
G = 8
NG = C // G
PJ = W // 2
K13, K5, K3 = 13, 5, 3
PITCH = 62
PXC = 2 * W
PXP = PITCH + W
JC = 4
NCH = PJ // JC
TC = JC * PXC
NQ = NCH
UNITS = 2 * NQ
ROWS_AT = [3, 5, 6, 8, 9, 11, 12]
RESIDUAL_AT = [5, 7, 8, 10, 11, 12, 13]
RING = 4
QT = HW // NQ
QW = W // NQ
LN_EPS = 1e-5
BN_EPS = 1e-5
NEG = -1e30

VEC = ["pw_v", "dwk_v", "dw1_v", "pw_g", "dwk_g", "dw1_g", "pw_b", "dwk_b", "dw1_b",
       "pw_m", "dwk_m", "dw1_m", "dw1_w", "ln1_g", "ln1_b", "ln2_g", "ln2_b", "gamma1", "gamma2",
       "dec0", "dec1", "first0", "first1"]
NV = len(VEC)
V = {n: i for i, n in enumerate(VEC)}


def band(k):
    dmax = (k // 2 + 1) // 2
    centre = 2 * PITCH * dmax + PXP - 1
    return dmax, centre, 2 * centre + 2, 2 * PITCH * 2 * dmax + PXP


def free(ap, pattern, offset=0):
    return bass.AP(ap.tensor, ap.offset + offset, [list(ap.ap[0])] + pattern)


def dram(t, offset, pattern):
    return bass.AP(t.tensor, offset, pattern)


def taps_view(ap, k, centre):
    return free(ap, [[PITCH, k], [1, k]], centre - (k // 2) * (PITCH + 1))


def rounded(ap):
    return ap.bitcast(F32R)


def split_matmul(pe, bank, w, x, start, stop):
    (w_hi, w_lo), (x_hi, x_lo) = ([rounded(p) for p in t] for t in (w, x))
    pe.matmul(bank, w_hi, x_hi, start=start, stop=False)
    pe.matmul(bank, w_hi, x_lo, start=False, stop=False)
    return pe.matmul(bank, w_lo, x_hi, start=False, stop=stop)


class Mem:
    def __init__(self, nc, ctx):
        self.nc, self.ctx = nc, ctx

    def sb(self, name, shape, dt=F32):
        return self.ctx.enter_context(self.nc.sbuf_tensor(name, shape, dt))

    def ps(self, name, shape=(128, 512)):
        return self.ctx.enter_context(self.nc.psum_tensor(name, list(shape), F32))

    def sem(self, name):
        return self.ctx.enter_context(self.nc.semaphore(name))


def pair_batch(t, B, b, offset=None):
    row = B * G * PJ
    return dram(t, b * G * PJ if offset is None else offset, [[row, PXC], [PXC * row, NG], [1, G * PJ]])


def pair_group(t, B, g):
    row = B * G * PJ
    return dram(t, g * PXC * row, [[row, PXC], [1, row]])


def copy_pairs(eng, to, of, signal):
    for r in range(2):
        tile, rest = slice(r * PITCH, r * PITCH + W), r * W
        part = []
        for ap in (to, of):
            dims = [list(d) for d in ap.ap]
            if dims[0][1] == PXP:
                part.append(ap[tile])
            else:
                part.append(bass.AP(ap.tensor, ap.offset + rest * dims[0][0], [[dims[0][0], W]] + dims[1:]))
        eng.dma_start(part[0], part[1]).then_inc(signal, 16)


def by_group(t):
    return t[:, :, :].rearrange("p (g c) j -> p g (c j)", g=NG)


def prepare(nc, ins, keep, wpw, shift_pw, f13_d, f5a_d, f5f_d, bias_d):
    with ExitStack() as ctx:
        m = Mem(nc, ctx)
        bcv = m.sb("bcv", [128, NV, C])
        colv = m.sb("colv", [CT, KT, NV])
        alph = m.sb("alph", [CT, 8])
        dwk = m.sb("dwk", [CT, KT, K13 * K13])
        w5 = m.sb("w5", [CT, 2, KT, K5 * K5])
        w3 = m.sb("w3", [CT, 2, KT, K3 * K3])
        w1 = m.sb("w1", [CT, 2, KT])
        _, c13, l13, _ = band(K13)
        _, c5, l5, _ = band(K5)
        f13 = m.sb("f13", [CT, KT, l13])
        f5 = m.sb("f5", [CT, 2, KT, l5])
        sd = m.sb("sd", [128, 3, C])
        sc = m.sb("sc", [128, 3, C])
        sh = m.sb("sh", [128, 3, C])
        cd = m.sb("cd", [CT, KT, 3])
        cs = m.sb("cs", [CT, KT, 3])
        c1 = m.sb("c1", [CT, KT])
        uw = m.sb("uw", [CT, KT, 2])
        loads = m.sem("prep_loaded")
        var_ready = m.sem("prep_variances")
        root = m.sem("prep_roots")
        step = m.sem("prep_steps")
        expo = m.sem("prep_exponentials")
        stored = m.sem("prep_stored")
        block = ctx.enter_context(nc.Block())
        folds = [0]

        @block.sync
        def _(sp):
            n = 0
            vecs = ins["vecs"]
            for dst, src in [
                (bcv[:, :, :], dram(vecs, 0, [[0, 128], [1, NV * C]])),
                (colv[:, :, :], ins["vec_cols"]),
                (alph[:, :], dram(ins["alphas"], 0, [[0, CT], [1, 8]])),
                (keep.ident[:, :], ins["ident"]),
                (wpw[:, :, :], ins["pw_wt"].rearrange("(k p) n -> p k n", p=CT)),
                *[(keep.wkvr[:, :, o, :], ins["att_wt"][o].rearrange("(k p) n -> p k n", p=CT))
                  for o in range(3)],
                (keep.wo[:, :, :], ins["att_wot"].rearrange("(k p) n -> p k n", p=CT)),
                (dwk[:, :, :], ins["dwk_w"].rearrange("(k p) n -> p k n", p=CT)),
                (w5[:, 0], ins["att_w5"].rearrange("(k p) n -> p k n", p=CT)),
                (w5[:, 1], ins["ffn_w5"].rearrange("(k p) n -> p k n", p=CT)),
                (w3[:, 0], ins["att_w3"].rearrange("(k p) n -> p k n", p=CT)),
                (w3[:, 1], ins["ffn_w3"].rearrange("(k p) n -> p k n", p=CT)),
                (w1[:, 0], ins["att_w1"]),
                (w1[:, 1], ins["ffn_w1"]),
            ]:
                sp.dma_start(dst, src).then_inc(loads, 16)
                n += 16
            folds[0] = n

        @block.vector
        def _(dve):
            done = [0]

            def link(ins_):
                done[0] += 1
                ins_.then_inc(step, 1)
                dve.wait_ge(step, done[0])

            link(dve.memset(f13[:, :, :], 0.0))
            link(dve.memset(f5[:, :, :, :], 0.0))
            dve.wait_ge(loads, folds[0])
            dve.tensor_scalar_add(sd[:, :, :], bcv[:, 0:3, :], BN_EPS).then_inc(var_ready, 1)
            dve.tensor_scalar_add(cd[:, :, :], colv[:, :, 0:3], BN_EPS).then_inc(var_ready, 1)
            link(dve.tensor_scalar_mul(keep.decay[:, :, :], colv[:, :, V["dec0"]:V["dec0"] + 2], 1.0 / HW))
            dve.scalar_tensor_tensor(uw[:, :, :], colv[:, :, V["first0"]:V["first0"] + 2], 1.0 / HW,
                                     keep.decay[:, :, :], ALU.mult, ALU.add).then_inc(var_ready, 1)
            dve.wait_ge(root, 2)
            link(dve.reciprocal(sd[:, :, :], sd[:, :, :]))
            link(dve.tensor_mul(sc[:, :, :], bcv[:, 3:6, :], sd[:, :, :]))
            link(dve.tensor_mul(sh[:, :, :], bcv[:, 9:12, :], sc[:, :, :]))
            link(dve.tensor_sub(sh[:, :, :], bcv[:, 6:9, :], sh[:, :, :]))
            link(dve.tensor_copy(shift_pw[:, :], sh[:, 0, :]))
            link(dve.tensor_add(sd[:, 0, :], sh[:, 1, :], sh[:, 2, :]))
            for k in range(KT):
                link(dve.tensor_mul(wpw[:, k, :], wpw[:, k, :], sc[0:CT, 0, :]))
                own = wpw[:, k, k * CT:(k + 1) * CT]
                link(dve.tensor_add(own, own, keep.ident[0:CT, 0:CT]))
                link(dve.tensor_mul(keep.wo[:, k, :], keep.wo[:, k, :], bcv[0:CT, V["gamma1"], :]))
            link(dve.reciprocal(cd[:, :, :], cd[:, :, :]))
            link(dve.tensor_mul(cs[:, :, :], colv[:, :, 3:6], cd[:, :, :]))
            link(dve.tensor_mul(c1[:, :], colv[:, :, V["dw1_w"]], cs[:, :, 2]))
            for k in range(KT):
                link(dve.tensor_scalar(taps_view(f13[:, k, :], K13, c13),
                                       dwk[:, k, :].rearrange("p (a b) -> p a b", a=K13),
                                       cs[:, k, 1:2], None, ALU.mult))
                mid = f13[:, k, c13:c13 + 1]
                link(dve.tensor_add(mid, mid, c1[:, k:k + 1]))
            for s in range(2):
                a = [alph[:, 4 * s + n:4 * s + n + 1] for n in range(4)]
                for k in range(KT):
                    link(dve.tensor_scalar(taps_view(f5[:, s, k, :], K5, c5),
                                           w5[:, s, k, :].rearrange("p (a b) -> p a b", a=K5),
                                           a[3], None, ALU.mult))
                    inner = taps_view(f5[:, s, k, :], K3, c5)
                    link(dve.scalar_tensor_tensor(inner, w3[:, s, k, :].rearrange("p (a b) -> p a b", a=K3),
                                                  a[2], inner, ALU.mult, ALU.add))
                    mid = f5[:, s, k, c5:c5 + 1]
                    link(dve.scalar_tensor_tensor(mid, w1[:, s, k:k + 1], a[1], mid, ALU.mult, ALU.add))
                    link(dve.tensor_add(mid, mid, a[0]))
            dve.wait_ge(expo, 1)
            link(dve.tensor_scalar_add(keep.bonus[:, :, :], keep.bonus[:, :, :], -1.0))
            folds[0] = done[0]

        @block.scalar
        def _(act):
            act.wait_ge(var_ready, 2)
            act.activation(sd[:, :, :], sd[:, :, :], ACT.Sqrt).then_inc(root, 1)
            act.activation(cd[:, :, :], cd[:, :, :], ACT.Sqrt).then_inc(root, 1)
            act.wait_ge(var_ready, 3)
            act.activation(keep.bonus[:, :, :], uw[:, :, :], ACT.Exp).then_inc(expo, 1)
            act.wait_ge(step, folds[0])
            act.dma_start(f13_d.rearrange("(k p) n -> p k n", p=CT), f13[:, :, :]).then_inc(stored, 16)
            act.dma_start(f5a_d.rearrange("(k p) n -> p k n", p=CT), f5[:, 0]).then_inc(stored, 16)
            act.dma_start(f5f_d.rearrange("(k p) n -> p k n", p=CT), f5[:, 1]).then_inc(stored, 16)
            act.dma_start(bias_d, sd[0:1, 0, :]).then_inc(stored, 16)
            act.wait_ge(stored, 64)


def pointwise(nc, B, x, wpw, shift_pw, xpw_d):
    with ExitStack() as ctx:
        m = Mem(nc, ctx)
        xin = [m.sb(f"xin{u}", [CT, KT, HW]) for u in range(2)]
        xp = [m.sb(f"xp{u}", [PXC, C, PJ]) for u in range(2)]
        NB = 7
        ps = [m.ps(f"pw_ps{i}") for i in range(NB)]
        loaded = [m.sem(f"x_loaded{u}") for u in range(2)]
        ps_ready = m.sem("pw_product_ready")
        ps_free = m.sem("pw_bank_free")
        stored = [m.sem(f"xpw_stored{u}") for u in range(2)]
        PAIRS = PJ // 2
        block = ctx.enter_context(nc.Block())

        def load(sp, b, u):
            sp.dma_start(xin[u][:, :, :], dram(x, b * C * HW, [[HW, CT], [CT * HW, KT], [1, HW]])
                         ).then_inc(loaded[u], 16)

        @block.sync
        def _(sp):
            load(sp, 0, 0)
            load(sp, 1, 1)
            with sp.Fori(0, B // 2 - 1) as i:
                for u in range(2):
                    sp.wait_ge(ps_ready, (i * 2 + u + 1) * PAIRS)
                    load(sp, i * 2 + (u + 2), u)

        @block.tensor
        def _(pe):
            with pe.Fori(0, B // 2) as i:
                for u in range(2):
                    pe.wait_ge(loaded[u], i * 16 + 16)
                    for jp in range(PAIRS):
                        pe.wait_ge(ps_free, i * (2 * PAIRS) + (u * PAIRS + jp + 1))
                        bank = ps[jp % NB]
                        for q in range(2):
                            j = 2 * jp + q
                            for k in range(KT):
                                mm = pe.matmul(bank[0:PXC, q * C:(q + 1) * C],
                                               xin[u][:, k, j * PXC:(j + 1) * PXC], wpw[:, k, :],
                                               start=(k == 0), stop=(k == KT - 1))
                        mm.then_inc(ps_ready, 1)

        @block.vector
        def _(dve):
            dve.sem_inc(ps_free, NB)
            with dve.Fori(0, B // 2) as i:
                for u in range(2):
                    dve.wait_ge(stored[u], i * 16 + 16)
                    for jp in range(PAIRS):
                        dve.wait_ge(ps_ready, i * (2 * PAIRS) + (u * PAIRS + jp + 1))
                        dve.tensor_tensor(
                            xp[u][:, :, 2 * jp:2 * jp + 2],
                            ps[jp % NB][0:PXC, 0:2 * C].rearrange("p (q c) -> p c q", q=2),
                            free(shift_pw[0:PXC, :], [[1, C], [0, 2]]), ALU.add).then_inc(ps_free, 1)

        @block.scalar
        def _(act):
            for u in range(2):
                act.sem_inc(stored[u], 16)
            with act.Fori(0, B // 2) as i:
                for u in range(2):
                    act.wait_ge(ps_free, i * (2 * PAIRS) + ((u + 1) * PAIRS + NB))
                    act.dma_start(pair_batch(xpw_d, B, i * 2 + u),
                                  by_group(xp[u])
                                  ).then_inc(stored[u], 16)
            for u in range(2):
                act.wait_ge(stored[u], 16 * (B // 2 + 1))


def depthwise(nc, B, name, src, parts, k, f_d, dst, post, bias_d=None, norm=None, vecs=None,
              stats=None, flipped=False):
    dmax, centre, length, cols = band(k)
    N = B * PJ
    assert N <= 512
    with ExitStack() as ctx:
        m = Mem(nc, ctx)
        wt = [m.sb(f"{name}_band{u}", [PXP, G, cols]) for u in range(2)]
        raw = [m.sb(f"{name}_in{u}", [PXP, B, G, PJ]) for u in range(2)]
        z = [m.sb(f"{name}_norm{u}", [PXP, B, G, PJ]) for u in range(2)] if norm else raw
        out = [m.sb(f"{name}_out{u}", [PXP, B, G, PJ]) for u in range(2)]
        col = [m.sb(f"{name}_cols{u}", [PXP, 2, G]) for u in range(2)]
        SLOTS = 4
        wp = [[m.sb(f"{name}_band{s}_part{n}", [PXP, cols]) for n in range(2)] for s in range(SLOTS)]
        zp = [[m.sb(f"{name}_in{s}_part{n}", [PXP, PJ, B]) for n in range(2)] for s in range(SLOTS)]
        rounded_done = m.sem(f"{name}_parts_rounded")
        band_split = m.sem(f"{name}_band_split")
        in_split = m.sem(f"{name}_in_split")
        ps = [m.ps(f"{name}_ps{i}") for i in range(G)]
        zeroed = m.sem(f"{name}_bands_zeroed")
        w_loaded = [m.sem(f"{name}_band_loaded{u}") for u in range(2)]
        in_loaded = [m.sem(f"{name}_in_loaded{u}") for u in range(2)]
        normed = m.sem(f"{name}_input_scaled")
        centred = m.sem(f"{name}_input_centred")
        z_ready = m.sem(f"{name}_input_ready")
        conv_done = m.sem(f"{name}_channel_convolved")
        ps_free = m.sem(f"{name}_bank_free")
        stored = [m.sem(f"{name}_stored{u}") for u in range(2)]
        out_read = m.sem(f"{name}_output_summed")
        if stats and not norm:
            sq = m.sb(f"{name}_squares", [PXP, B, G, PJ])
            part = [m.sb(f"{name}_part{n}", [PXP, B, PJ]) for n in range(2)]
            reduced = m.sem(f"{name}_group_reduced")
            summed = m.sem(f"{name}_sums_updated")
        block = ctx.enter_context(nc.Block())
        flat = lambda t: t[:, :, :].rearrange("p a b -> p (a b)")
        by_pair = lambda ap: ap.rearrange("p b j -> p j b")
        IN = 48 if norm else 32
        BASE = 2 * G
        step_in = PITCH if parts == PXP else W

        def channel(i, n):
            group = n // G
            return group % 2, n % G, i * (2 * G) + (n + 1), i + (group // 2 + 1)

        def rest_of_band(eng, i, n):
            u, cc, _, _ = channel(i, n)
            p = [q[0:parts, :] for q in wp[n % SLOTS]]
            eng.wait_ge(rounded_done, i * (4 * G) + (2 * n + 1))
            eng.tensor_tensor(rounded(p[1]), wt[u][0:parts, cc, :], p[0], ALU.subtract).then_inc(band_split, 1)

        @block.sync
        def _(sp):
            def place(g):
                return [g * (PXC * B * G * PJ), g * G, g * (G * length)]

            def load_input(at, u):
                whole = raw[u][:, :, :, :].rearrange("p b c j -> p (b c j)")
                group = dram(src, at[0], [[B * G * PJ, PXC], [1, B * G * PJ]])
                if parts == PXC:
                    sp.dma_start(whole[0:PXC], group).then_inc(in_loaded[u], 16)
                else:
                    copy_pairs(sp, whole, group, in_loaded[u])
                if norm:
                    sp.dma_start(col[u][:, :, :], dram(vecs, at[1] + V[norm] * C, [[0, PXP], [C, 2], [1, G]])
                                 ).then_inc(in_loaded[u], 16)
                if bias_d is not None:
                    sp.dma_start(col[u][:, 0, :], dram(bias_d, at[1], [[0, PXP], [1, G]])
                                 ).then_inc(in_loaded[u], 16)

            def load_bands(at, u):
                for r in range(2):
                    sp.dma_start(wt[u][r * step_in:r * step_in + W, :, :],
                                 dram(f_d, at[2] + PITCH * r, [[1, W], [length, G], [1, cols]])
                                 ).then_inc(w_loaded[u], 16)

            sp.wait_ge(zeroed, 4 if parts == PXP else 2)
            for u in range(2):
                load_input(place(u), u)
                load_bands(place(u), u)
            with sp.Fori(0, NG // 2 - 1) as i:
                for u in range(2):
                    at = [sp.snap(a) for a in place(i * 2 + (u + 2))]
                    if norm:
                        through = sp.snap(i * (2 * G) + G * (u + 1))
                        sp.wait_ge(z_ready, through)
                        load_input(at, u)
                        sp.wait_ge(band_split, through)
                    else:
                        sp.wait_ge(ps_free, i * (2 * G) + G * (u + 2))
                        load_input(at, u)
                    load_bands(at, u)

        @block.tensor
        def _(pe):
            pe.sem_inc(conv_done, BASE)
            with pe.Fori(0, NG // 2) as i:
                for n in range(2 * G):
                    u, cc, number, _ = channel(i, n)
                    pe.wait_ge(band_split, number)
                    pe.wait_ge(in_split, number)
                    pe.wait_ge(ps_free, number)
                    order = [0] + [s * d for d in range(1, dmax + 1) for s in (1, -1)]
                    for d in order:
                        lo, hi = max(0, -d), min(PJ, PJ - d)
                        at = 2 * PITCH * (dmax - d if flipped else dmax + d)
                        mm = split_matmul(pe, ps[cc][0:PXP, lo * B:hi * B],
                                          [x[0:parts, at:at + PXP] for x in wp[n % SLOTS]],
                                          [flat(x)[0:parts, (lo + d) * B:(hi + d) * B] for x in zp[n % SLOTS]],
                                          d == 0, d == order[-1])
                    mm.then_inc(conv_done, 1)

        @block.gpsimd
        def _(pool):
            with pool.Fori(0, NG // 2) as i:
                for n in range(2 * G):
                    u, cc, _, _ = channel(i, n)
                    if not norm:
                        rest_of_band(pool, i, n)
                    pool.wait_ge(rounded_done, i * (4 * G) + (2 * n + 2))
                    p = zp[n % SLOTS]
                    pool.tensor_tensor(rounded(p[1][0:parts]), by_pair(z[u][0:parts, :, cc, :]), p[0][0:parts],
                                       ALU.subtract).then_inc(in_split, 1)

        @block.vector
        def _(dve):
            for u in range(2):
                dve.memset(wt[u][:, :, :], 0.0).then_inc(zeroed, 1)
                if parts == PXP:
                    dve.memset(raw[u][:, :, :, :], 0.0).then_inc(zeroed, 1)
            if norm:
                rs, ms = stats
                wide = lambda t: free(t, [[PJ, B], [0, G // 2], [1, PJ]])

                H = G // 2

                def scale(i, g, half):
                    u, _, number, loads = channel(i, g * G)
                    part = slice(half * H, (half + 1) * H)
                    if half == 0:
                        dve.wait_ge(in_loaded[u], loads * IN)
                        dve.wait_ge(conv_done, number + (G - 1))
                    dve.tensor_mul(z[u][:, :, part, :], raw[u][:, :, part, :], wide(rs[:, :])).then_inc(normed, 1)

                def subtract_mean(i, g, half):
                    v = z[g % 2][:, :, half * H:(half + 1) * H, :]
                    dve.wait_ge(normed, i * 4 + (2 * g + half + 1))
                    dve.tensor_sub(v, v, wide(ms[:, :])).then_inc(centred, 1)

                def groups(i, last):
                    for n in range(2 * G):
                        u, cc, _, _ = channel(i, n)
                        if cc == 0:
                            dve.wait_ge(centred, i * 4 + 2 * (n // G + 1))
                        v = z[u][:, :, cc, :]
                        dve.tensor_scalar(v, v, col[u][:, 0, cc:cc + 1], col[u][:, 1, cc:cc + 1],
                                          ALU.mult, ALU.add).then_inc(z_ready, 1)
                        rest_of_band(dve, i, n)
                        if cc >= H and (n // G == 0 or not last):
                            (scale, subtract_mean)[(cc - H) // 2](i, n // G + 1, cc % 2)

                for step in (scale, subtract_mean):
                    for half in range(2):
                        step(0, 0, half)
                with dve.Fori(0, NG // 2 - 1) as i:
                    groups(i, False)
                groups(NG // 2 - 1, True)
            elif stats:
                s1, s2 = stats
                dve.memset(s1[:, :], 0.0).then_inc(summed, 1)
                dve.memset(s2[:, :], 0.0).then_inc(summed, 1)
                dve.sem_inc(out_read, 2)
                by_pixel = lambda t: t[:, :, :, :].rearrange("p b c j -> p b j c")
                with dve.Fori(0, NG // 2) as i:
                    for u in range(2):
                        dve.wait_ge(ps_free, i * (2 * G) + (G * (u + 2)))
                        dve.wait_ge(summed, i * 4 + (2 * u + 2))
                        dve.tensor_reduce(part[0][:, :, :], by_pixel(out[u]), AX_X, ALU.add).then_inc(reduced, 1)
                        dve.wait_ge(reduced, i * 4 + (2 * u + 1))
                        dve.tensor_add(s1[:, :], s1[:, :], flat(part[0])).then_inc(summed, 1)
                        dve.tensor_mul(sq[:, :, :, :], out[u][:, :, :, :], out[u][:, :, :, :]).then_inc(out_read, 1)
                        dve.wait_ge(out_read, i * 2 + (u + 3))
                        dve.tensor_reduce(part[1][:, :, :], by_pixel(sq), AX_X, ALU.add).then_inc(reduced, 1)
                        dve.wait_ge(reduced, i * 4 + (2 * u + 2))
                        dve.tensor_add(s2[:, :], s2[:, :], flat(part[1])).then_inc(summed, 1)

        @block.scalar
        def _(act):
            act.sem_inc(ps_free, G)
            for u in range(2):
                act.sem_inc(stored[u], 32)

            def round_parts(i, n):
                u, cc, number, loads = channel(i, n)
                act.wait_ge(conv_done, i * (2 * G) + (n + 1 + BASE - SLOTS))
                if cc == 0:
                    act.wait_ge(w_loaded[u], loads * 32)
                    act.wait_ge(in_loaded[u], loads * IN)
                act.activation(rounded(wp[n % SLOTS][0][0:parts, :]), wt[u][0:parts, cc, :], ACT.Copy
                               ).then_inc(rounded_done, 1)
                if norm:
                    act.wait_ge(z_ready, number)
                act.activation(rounded(zp[n % SLOTS][0][0:parts]), by_pair(z[u][0:parts, :, cc, :]), ACT.Copy
                               ).then_inc(rounded_done, 1)

            def groups(i, last):
                for n in range(2 * G):
                    u, cc, _, _ = channel(i, n)
                    if n + AHEAD < 2 * G or not last:
                        round_parts(i, n + AHEAD)
                    if cc == 0:
                        act.wait_ge(stored[u], i * 32 + 32)
                        if stats and not norm:
                            act.wait_ge(out_read, i * 2 + (u + 1))
                    act.wait_ge(conv_done, i * (2 * G) + (BASE + n + 1))
                    o = out[u][:, :, cc, :]
                    p = ps[cc][0:PXP, 0:N].rearrange("p (j b) -> p b j", b=B)
                    if post == "gelu":
                        act.activation(o, p, ACT.Gelu, bias=col[u][:, 0, cc:cc + 1]).then_inc(ps_free, 1)
                    else:
                        act.activation(o, p, ACT.Copy).then_inc(ps_free, 1)
                    if cc == G - 1:
                        act.wait_ge(ps_free, i * (2 * G) + (G * (u + 2)))
                        copy_pairs(act, pair_group(dst, B, i * 2 + u),
                                   out[u][:, :, :, :].rearrange("p b c j -> p (b c j)"), stored[u])

            AHEAD = 3
            for n in range(AHEAD):
                round_parts(0, n)
            with act.Fori(0, NG // 2 - 1) as i:
                groups(i, False)
            groups(NG // 2 - 1, True)
            for u in range(2):
                act.wait_ge(stored[u], 32 * (NG // 2 + 1))


def norm_scales(nc, name, s1, s2, s1_d=None, s2_d=None):
    with ExitStack() as ctx:
        m = Mem(nc, ctx)
        t = m.sb(f"{name}_mean_squared", list(s1.shape))
        cleared = m.sem(f"{name}_gap_cleared")
        loaded = m.sem(f"{name}_sums_loaded")
        var_ready = m.sem(f"{name}_variance_ready")
        root = m.sem(f"{name}_root_ready")
        step = m.sem(f"{name}_steps")
        block = ctx.enter_context(nc.Block())

        if s1_d is not None:
            @block.sync
            def _(sp):
                sp.wait_ge(cleared, 2)
                copy_pairs(sp, s1[:, :], s1_d, loaded)
                copy_pairs(sp, s2[:, :], s2_d, loaded)

        @block.vector
        def _(dve):
            if s1_d is not None:
                dve.memset(s1[:, :], 0.0).then_inc(cleared, 1)
                dve.memset(s2[:, :], 0.0).then_inc(cleared, 1)
                dve.wait_ge(loaded, 64)
            dve.tensor_scalar_mul(s1[:, :], s1[:, :], 1.0 / C).then_inc(step, 1)
            dve.wait_ge(step, 1)
            dve.tensor_mul(t[:, :], s1[:, :], s1[:, :]).then_inc(step, 1)
            dve.wait_ge(step, 2)
            dve.scalar_tensor_tensor(s2[:, :], s2[:, :], 1.0 / C, t[:, :], ALU.mult, ALU.subtract
                                     ).then_inc(step, 1)
            dve.wait_ge(step, 3)
            dve.tensor_scalar(s2[:, :], s2[:, :], 0.0, LN_EPS, ALU.max, ALU.add).then_inc(var_ready, 1)
            dve.wait_ge(root, 1)
            dve.reciprocal(s2[:, :], s2[:, :]).then_inc(step, 1)
            dve.wait_ge(step, 4)
            dve.tensor_mul(s1[:, :], s1[:, :], s2[:, :]).then_inc(step, 1)

        @block.scalar
        def _(act):
            act.wait_ge(var_ready, 1)
            act.activation(s2[:, :], s2[:, :], ACT.Sqrt).then_inc(root, 1)


def transposed(bank, reverse=False):
    s = -1 if reverse else 1
    return free(bank[0:CT, :], [[PXP, JC], [s * PITCH, 2], [s, W]], PXP - 1 if reverse else 0)


def by_pixel(ap):
    return ap.rearrange("p (j r w) -> p j r w", j=JC, r=2)


def attention(nc, B, keep, mix_d, y_d, tok_d, s1_d, s2_d):
    with ExitStack() as ctx:
        m = Mem(nc, ctx)
        X = m.sb("mix_pairs", [PXP, C, PJ])
        Y = m.sb("residual_pairs", [PXC, C, PJ])
        xT = m.sb("mixT", [CT, KT, HW])
        kS = m.sb("k_all", [CT, KT, HW])
        vS = m.sb("v_all", [CT, KT, HW])
        rS = m.sb("r_all", [CT, KT, HW])
        att = m.sb("gated_wkv", [CT, KT, HW])
        s1 = m.sb("tok_sum", [PXC, PJ])
        s2 = m.sb("tok_square_sum", [PXC, PJ])
        junk = m.sb("tok_squares", [PXC, C])
        z_ps = [m.ps(f"mixT_ps{i}") for i in range(KT)]
        u_ps = [m.ps(f"proj_ps{i}") for i in range(3)]
        o_ps = [m.ps(f"out_ps{i}") for i in range(2)]

        x_loaded = m.sem("mix_loaded")
        y_loaded = m.sem("residual_loaded")
        pads = m.sem("gaps_cleared")
        zt_ready = m.sem("mixT_in_psum")
        xT_ready = m.sem("mixT_in_sbuf")
        un_ready = m.sem("projection_in_psum")
        un_read = m.sem("projection_evacuated")
        kt_done = m.sem("k_by_column_done")
        sr_done = m.sem("receptance_ready")
        g_done = m.sem("wkv_gated")
        out_ps_ready = m.sem("attention_out_in_psum")
        tok_done = m.sem("tok_done")
        sq_done = m.sem("tok_squared")
        stored = m.sem("tok_stored")

        O = [m.sb(f"run_max{u}", [CT, 1 + QT]) for u in range(RING)]
        A = [m.sb(f"decay_factor{u}", [CT, QT]) for u in range(2)]
        E = [m.sb(f"input_factor{u}", [CT, QT]) for u in range(RING)]
        EV = [m.sb(f"input_times_v{u}", [CT, QT]) for u in range(2)]
        P = [m.sb(f"numerator_state{u}", [CT, QT]) for u in range(RING)]
        Q = [m.sb(f"denominator_state{u}", [CT, QT]) for u in range(RING)]
        carry_done = m.sem("run_max_carried")
        o_done = m.sem("run_max_done")
        a_arg = m.sem("decay_exponent_done")
        e_arg = m.sem("input_exponent_done")
        a_exp = m.sem("decay_factor_ready")
        e_exp = m.sem("input_factor_ready")
        ev_done = m.sem("input_times_v_done")
        p_done = m.sem("numerator_scan_done")
        q_done = m.sem("denominator_scan_done")
        n_done = m.sem("numerator_done")
        d_done = m.sem("denominator_done")
        ln_done = m.sem("denominator_logged")
        rec_done = m.sem("denominator_inverted")
        wkv_done = m.sem("wkv_divided")
        block = ctx.enter_context(nc.Block())
        UC = 3
        UT = UC * NCH
        ZT = KT * NCH

        class Tile:

            def __init__(self, i, m_):
                self.i, self.m, self.ct = i, m_, m_ % 2

            def at(self, per, offset=0):
                return self.i * (2 * per) + (self.m * per + offset)

            def image(self, per, offset=0):
                return self.i * per + (self.m // 2 * per + offset)

        class Image:
            def __init__(self, i):
                self.i = i

            def at(self, per, offset):
                return self.i * per + offset

        def need(eng, sem, value):
            if not isinstance(value, int) or value > 0:
                eng.wait_ge(sem, value)

        def at_superstep(i, m_, of):
            return isinstance(i, int) and (i, m_) == of

        FIRST, SECOND, LAST = (0, 0), (0, 1), (B - 1, 2)
        columns_at = [p for p in range(UNITS) if p not in ROWS_AT]

        class Unit:

            def __init__(self, i, m_, rows, q, position):
                self.i, self.m, self.rows, self.q, self.position = i, m_, rows, q, position
                self.tile = Tile(i, m_ if rows else m_ - 1)
                self.ct, self.way = self.tile.ct, 0 if rows else 1
                self.slot = (UNITS * (m_ % 2) + position) % RING
                self.bonus = keep.bonus[:, self.ct, self.way:self.way + 1]
                self.decay = keep.decay[:, self.ct, self.way:self.way + 1]

            def count(self, before=0):
                return self.i * (2 * UNITS) + (self.m * UNITS + self.position + 1 - before)

        def units_of(i, m_):
            if at_superstep(i, m_, FIRST):
                return [Unit(i, m_, True, q, NQ + q) for q in range(NQ)]
            if at_superstep(i, m_, LAST):
                return [Unit(i, m_, False, q, q) for q in range(NQ)]
            return [Unit(i, m_, True, ROWS_AT.index(p), p) if p in ROWS_AT
                    else Unit(i, m_, False, columns_at.index(p), p) for p in range(UNITS)]

        def stepped(i, m_):
            now = units_of(i, m_)
            old = [None] if at_superstep(i, m_, FIRST) else units_of(i, m_ - 1)[-1:]
            new = [None, None] if at_superstep(i, m_, LAST) else units_of(i, m_ + 1)[:2]
            line = old + now + new
            return [(line[n + 1], line[n], line[n + 2], line[n + 3]) for n in range(len(now))]

        def former(unit):
            if at_superstep(unit.i, unit.m, FIRST) or at_superstep(unit.i, unit.m, LAST):
                back = 1
            else:
                back = unit.position - (ROWS_AT if unit.rows else columns_at)[unit.q - 1]
            return (unit.slot - back) % RING, unit.count(back)

        def supersteps(eng, step):
            step(0, 0)
            step(0, 1)
            with eng.Fori(0, B - 1) as i:
                step(i, 2)
                step(i, 3, done=Image(i))
            step(B - 1, 2)

        def part_of(t, unit):
            if unit.rows:
                return t[:, unit.ct, unit.q * QT:(unit.q + 1) * QT].rearrange("p (a b) -> p a b", b=W)
            by_column = t[:, unit.ct, :].rearrange("p (r w) -> p w r", r=W)
            return by_column[:, unit.q * QW:(unit.q + 1) * QW, :]

        def grid(t):
            return t[:, 0:QT].rearrange("p (a b) -> p a b", b=W)

        @block.sync
        def _(sp):
            def load_x(b):
                copy_pairs(sp, by_group(X), pair_batch(mix_d, B, b), x_loaded)

            def load_y(b, offset=None):
                sp.dma_start(by_group(Y), pair_batch(y_d, B, b, offset)).then_inc(y_loaded, 16)

            def store(b, squares, stores):
                sp.wait_ge(sq_done, squares)
                sp.dma_start(pair_batch(tok_d, B, b), by_group(Y)).then_inc(stored, 16)
                for d, t in ((s1_d, s1), (s2_d, s2)):
                    sp.dma_start(dram(d, b * PJ, [[B * PJ, PXC], [1, PJ]]), t[:, :]).then_inc(stored, 16)
                sp.wait_ge(stored, stores)

            sp.wait_ge(pads, 1)
            load_x(0)
            load_y(0)
            sp.wait_ge(zt_ready, ZT)
            load_x(1)
            with sp.Fori(0, B - 2) as i:
                sp.wait_ge(zt_ready, i * ZT + 2 * ZT)
                load_x(i + 2)
                next_y = sp.snap((i + 1) * (G * PJ))
                marks = [sp.snap(i * n + a) for n, a in ((PJ, PJ + 1), (48, 48))]
                store(i, *marks)
                load_y(i + 1, next_y)
            store(B - 2, (B - 1) * PJ + 1, (B - 1) * 48)
            load_y(B - 1)
            store(B - 1, B * PJ + 1, B * 48)

        @block.tensor
        def _(pe):
            pe.wait_ge(pads, 1)

            def turn(r, t):
                for ct in range(KT):
                    pe.wait_ge(xT_ready, r.image(ZT, KT * t + ct + 1))
                    for jj in range(JC):
                        tr = pe.transpose(z_ps[ct][0:CT, jj * PXP:(jj + 1) * PXP],
                                          X[:, ct * CT:(ct + 1) * CT, JC * t + jj], keep.ident[:, :])
                    tr.then_inc(zt_ready, 1)

            def project(r, t):
                if r.ct == 0:
                    pe.wait_ge(xT_ready, r.image(ZT, KT * (t + 1) + KT))
                for o in range(UC):
                    pe.wait_ge(un_read, r.at(UT, UC * t + o + 1))
                    for k in range(KT):
                        mm = pe.matmul(u_ps[o][0:CT, 0:TC], keep.wkvr[:, k, o, r.ct * CT:(r.ct + 1) * CT],
                                       xT[:, k, t * TC:(t + 1) * TC], start=(k == 0), stop=(k == KT - 1))
                    mm.then_inc(un_ready, 1)

            def project_out(image, group):
                if group == 0:
                    pe.wait_ge(g_done, image.at(2, 3))
                for jp in (2 * group, 2 * group + 1):
                    pe.wait_ge(tok_done, image.at(PJ, 2 * jp + 1))
                    for q in range(2):
                        j = 2 * jp + q
                        for ct in range(KT):
                            mm = pe.matmul(o_ps[jp % 2][0:PXC, q * C:(q + 1) * C],
                                           att[:, ct, PXC * j:PXC * (j + 1)],
                                           keep.wo[:, ct, :], start=(ct == 0), stop=(ct == KT - 1))
                    mm.then_inc(out_ps_ready, 1)

            def step(i, m_, done=None):
                if not any(unit.rows for unit in units_of(i, m_)):
                    return
                r = Tile(i, m_)
                if r.ct == 0:
                    pe.wait_ge(x_loaded, r.image(32, 32))
                    turn(r, 0)
                for t in range(NCH):
                    if t + 1 < NCH and r.ct == 0:
                        turn(r, t + 1)
                    project(r, t)
                    if t > 1 and done is not None:
                        project_out(done, t - 2)
                if done is not None:
                    project_out(done, NCH - 2)
                    project_out(done, NCH - 1)

            supersteps(pe, step)
            for group in range(NCH):
                project_out(Image(B - 1), group)

        @block.scalar
        def _(act):
            act.sem_inc(xT_ready, KT)
            act.sem_inc(un_read, UC)
            act.sem_inc(sq_done, 1)
            for sem in (a_exp, e_exp, ln_done, rec_done):
                act.sem_inc(sem, NQ)

            def mix(r, t):
                if r.ct or t >= NCH:
                    return
                need(act, un_ready, r.at(UT, UC * (t + 1) - UT))
                for ct in range(KT):
                    act.wait_ge(zt_ready, r.image(ZT, KT * t + ct + 1))
                    act.activation(xT[:, ct, t * TC:(t + 1) * TC].rearrange("p (j r w) -> p j r w", j=JC, r=2),
                                   transposed(z_ps[ct], reverse=True), ACT.Copy).then_inc(xT_ready, 1)

            def evacuate(r, t):
                if t == 0:
                    need(act, g_done, r.at(1))
                for o, dst in enumerate((kS, vS, rS)):
                    act.wait_ge(un_ready, r.at(UT, UC * t + o + 1))
                    act.activation(dst[:, r.ct, TC * t:TC * (t + 1)], u_ps[o][0:CT, 0:TC], ACT.Copy
                                   ).then_inc(un_read, 1)

            def receptance(r):
                act.wait_ge(un_read, r.at(UT, UT + UC))
                act.activation(rS[:, r.ct, :], rS[:, r.ct, :], ACT.Sigmoid).then_inc(sr_done, 1)
                act.preload_act_table_set("natural_log_exp_and_others")

            def factors(unit):
                act.wait_ge(e_arg, unit.count())
                act.activation(E[unit.slot][:, :], E[unit.slot][:, :], ACT.Exp).then_inc(e_exp, 1)
                act.wait_ge(a_arg, unit.count())
                act.activation(A[unit.slot % 2][:, :], A[unit.slot % 2][:, :], ACT.Exp, bias=unit.decay
                               ).then_inc(a_exp, 1)

            def invert(unit):
                e = E[unit.slot][:, :]
                act.wait_ge(d_done, unit.count())
                act.activation(e, e, ACT.Ln).then_inc(ln_done, 1)
                act.wait_ge(ln_done, unit.count())
                act.activation(e, e, ACT.Exp, scale=-1.0).then_inc(rec_done, 1)

            def column_k(unit):
                if unit is None or unit.rows:
                    return
                if unit.q == 0:
                    act.wait_ge(un_read, unit.tile.at(UT, UT + UC))
                act.wait_ge(wkv_done, unit.count(RING))
                act.activation(grid(E[unit.slot]), part_of(kS, unit), ACT.Copy).then_inc(kt_done, 1)

            def squares(image, group):
                for j in range(JC * group, JC * (group + 1)):
                    act.wait_ge(tok_done, image.at(PJ, j + 4))
                    act.wait_ge(sq_done, image.at(PJ, j + 1))
                    act.activation(junk[:, :], Y[:, :, j], ACT.Square, accum_out=s2[:, j:j + 1]
                                   ).then_inc(sq_done, 1)

            def step(i, m_, done=None):
                steps = stepped(i, m_)
                rows = any(unit.rows for unit in units_of(i, m_))
                r = Tile(i, m_)
                if rows:
                    mix(r, 0)
                if steps[0][1] is None:
                    mix(r, 1)
                    for t in range(NCH):
                        evacuate(r, t)
                        mix(r, t + 2)
                    factors(steps[0][0])
                for unit, before, after, second in steps:
                    column_k(second)
                    if after is not None:
                        factors(after)
                    if rows and steps[0][1] is not None and unit.position + 2 in ROWS_AT:
                        t = ROWS_AT.index(unit.position + 2)
                        evacuate(r, t)
                        mix(r, t + 2)
                    invert(unit)
                    if rows and steps[0][1] is not None and unit.position == 0:
                        mix(r, 1)
                    if rows and unit.position == UNITS - 3:
                        receptance(r)
                    if done is not None and unit.position - 1 in RESIDUAL_AT:
                        squares(done, RESIDUAL_AT.index(unit.position - 1))
                if done is not None:
                    squares(done, NCH - 1)

            supersteps(act, step)
            for group in range(NCH):
                squares(Image(B - 1), group)

        @block.gpsimd
        def _(pool):
            for sem in (wkv_done, e_arg, ev_done):
                pool.sem_inc(sem, NQ)

            def exponents(unit):
                pool.wait_ge(wkv_done, unit.count(RING))
                pool.wait_ge(o_done, unit.count())
                o, e = O[unit.slot], E[unit.slot]
                k = kS[:, unit.ct, unit.q * QT:(unit.q + 1) * QT] if unit.rows else e[:, :]
                pool.tensor_tensor(e[:, :], k, o[:, 1:1 + QT], ALU.subtract).then_inc(e_arg, 1)

            def weigh(unit):
                if unit.rows:
                    pool.wait_ge(un_read, unit.tile.at(UT, UC * unit.q + UC + 2))
                pool.wait_ge(wkv_done, unit.count(
                    1 if at_superstep(unit.i, unit.m, SECOND) and unit.position == 0 else 2))
                pool.wait_ge(e_exp, unit.count())
                pool.tensor_tensor(grid(EV[unit.slot % 2]), grid(E[unit.slot]), part_of(vS, unit), ALU.mult
                                   ).then_inc(ev_done, 1)

            def divide(unit):
                pool.wait_ge(n_done, unit.count())
                pool.wait_ge(rec_done, unit.count())
                pool.tensor_tensor(part_of(vS, unit), grid(EV[unit.slot % 2]), grid(E[unit.slot]), ALU.mult
                                   ).then_inc(wkv_done, 1)

            def step(i, m_, done=None):
                steps = stepped(i, m_)
                if steps[0][1] is None:
                    exponents(steps[0][0])
                for unit, before, after, _ in steps:
                    at_once = at_superstep(i, m_, SECOND) and unit.position == 0
                    if at_once:
                        divide(before)
                    weigh(unit)
                    if after is not None:
                        exponents(after)
                    if before is not None and not at_once:
                        divide(before)
                if after is None:
                    divide(unit)

            supersteps(pool, step)

        @block.vector
        def _(dve):
            dve.memset(X[:, :, :], 0.0).then_inc(pads, 1)
            dve.sem_inc(tok_done, 3)
            dve.sem_inc(g_done, 1)

            for sem in (carry_done, o_done, a_arg, p_done, q_done, n_done, d_done):
                dve.sem_inc(sem, NQ)

            def run_max(unit):
                if unit.rows:
                    dve.wait_ge(un_read, unit.tile.at(UT, UC * unit.q + UC + 1))
                    k = kS[:, unit.ct, unit.q * QT:(unit.q + 1) * QT]
                else:
                    dve.wait_ge(kt_done, unit.tile.at(NQ, unit.q + 1))
                    k = E[unit.slot][:, :]
                o = O[unit.slot]
                if unit.q == 0:
                    dve.memset(o[:, 0:1], NEG).then_inc(carry_done, 1)
                    start = NEG
                else:
                    slot, count = former(unit)
                    dve.wait_ge(o_done, count)
                    start = O[slot][:, QT:QT + 1]
                    dve.tensor_copy(o[:, 0:1], start).then_inc(carry_done, 1)
                dve.tensor_tensor_scan(o[:, 1:1 + QT], free(unit.decay, [[0, QT]]), k, start,
                                       ALU.add, ALU.max).then_inc(o_done, 1)

            def decay_exponent(unit):
                o = O[unit.slot]
                dve.wait_ge(carry_done, unit.count())
                dve.wait_ge(o_done, unit.count())
                dve.tensor_tensor(A[unit.slot % 2][:, :], o[:, 0:QT], o[:, 1:1 + QT], ALU.subtract
                                  ).then_inc(a_arg, 1)

            def scan(unit, state, factor, added):
                start = state[former(unit)[0]][:, QT - 1:QT] if unit.q else 0.0
                return dve.tensor_tensor_scan(state[unit.slot][:, :], factor[:, :], added[:, :], start,
                                              ALU.mult, ALU.add)

            def sums(unit):
                a = A[unit.slot % 2]
                dve.wait_ge(e_exp, unit.count())
                dve.wait_ge(a_exp, unit.count())
                dve.wait_ge(d_done, unit.count(RING))
                scan(unit, Q, a, E[unit.slot]).then_inc(q_done, 1)
                dve.wait_ge(ev_done, unit.count())
                dve.wait_ge(n_done, unit.count(RING))
                scan(unit, P, a, EV[unit.slot % 2]).then_inc(p_done, 1)

            def outputs(unit):
                e, ev = E[unit.slot][:, :], EV[unit.slot % 2][:, :]
                dve.wait_ge(q_done, unit.count())
                dve.scalar_tensor_tensor(e, e, unit.bonus, Q[unit.slot][:, :], ALU.mult, ALU.add
                                         ).then_inc(d_done, 1)
                dve.wait_ge(p_done, unit.count())
                dve.scalar_tensor_tensor(ev, ev, unit.bonus, P[unit.slot][:, :], ALU.mult, ALU.add
                                         ).then_inc(n_done, 1)

            def gate(tile):
                dve.wait_ge(sr_done, tile.at(1, 1))
                dve.wait_ge(wkv_done, tile.at(UNITS, UNITS + NQ if at_superstep(tile.i, tile.m + 1, LAST)
                                              else 2 * UNITS))
                dve.tensor_tensor(att[:, tile.ct, :], vS[:, tile.ct, :], rS[:, tile.ct, :], ALU.mult
                                  ).then_inc(g_done, 1)

            def add_residual(image, group):
                if group == 0:
                    dve.wait_ge(y_loaded, image.at(16, 16))
                for j in range(JC * group, JC * (group + 1)):
                    q = j % 2
                    if q == 0:
                        dve.wait_ge(out_ps_ready, image.at(PJ // 2, j // 2 + 1))
                    dve.scalar_tensor_tensor(Y[:, :, j], o_ps[(j // 2) % 2][0:PXC, q * C:(q + 1) * C], 1.0,
                                             Y[:, :, j], ALU.mult, ALU.add, accum_out=s1[:, j:j + 1]
                                             ).then_inc(tok_done, 1)

            def step(i, m_, done=None):
                steps = stepped(i, m_)
                if steps[0][1] is None:
                    for n in range(2):
                        run_max(steps[n][0])
                        decay_exponent(steps[n][0])
                for unit, before, after, second in steps:
                    if unit.position == 1 and m_ > 1:
                        gate(Tile(i, m_ - 2))
                    sums(unit)
                    outputs(unit)
                    if second is not None:
                        run_max(second)
                    if done is not None and unit.position in RESIDUAL_AT:
                        add_residual(done, RESIDUAL_AT.index(unit.position))
                    if second is not None:
                        decay_exponent(second)

            supersteps(dve, step)
            gate(Tile(B - 1, 1))
            for group in range(NCH):
                add_residual(Image(B - 1), group)


def feed_forward(nc, B, ins, keep, mix_d, tok_d, out):
    with ExitStack() as ctx:
        m = Mem(nc, ctx)
        X = [m.sb(f"ffn_mix{u}", [PXP, C, PJ]) for u in range(2)]
        T = [m.sb(f"ffn_tok{u}", [PXP, C, PJ]) for u in range(2)]
        wk = m.sb("ffn_wk", [CT, KT, HID])
        wv = m.sb("ffn_wv", [128, HT, C])
        wr = m.sb("ffn_wr", [CT, KT, C])
        gam = m.sb("gamma2", [128, C])
        wk_parts = [m.sb(f"ffn_wk_part{n}", [CT, KT, HID]) for n in range(2)]
        wv_parts = [m.sb(f"ffn_wv_part{n}", [128, HT, C]) for n in range(2)]
        wr_parts = [m.sb(f"ffn_wr_part{n}", [CT, KT, C]) for n in range(2)]
        xT = [[m.sb(f"ffn_mixT{u}_part{n}", [CT, KT, TC]) for n in range(2)] for u in range(2)]
        kk = [[m.sb(f"hidden{u}_part{n}", [128, HT, TC]) for n in range(2)] for u in range(2)]
        KW = 3
        whole = [m.sb(f"hidden_whole{u}", [128, TC]) for u in range(KW)]
        sg = [m.sb(f"ffn_gate{u}", [CT, KT, TC]) for u in range(2)]
        gv = m.sb("gated", [CT, KT, TC])
        res = [m.sb(f"result{u}", [CT, KT, TC]) for u in range(2)]
        z_ps = [m.ps(f"f_mixT_ps{i}") for i in range(KT)]
        t_ps = [m.ps(f"f_tokT_ps{i}") for i in range(KT)]
        h_ps = [m.ps(f"f_hid_ps{i}") for i in range(2)]
        v_ps = [m.ps(f"f_out_ps{i}") for i in range(KT)]
        w_loaded = m.sem("ffn_weights_loaded")
        w_folded = m.sem("ffn_gamma_folded")
        w_high = m.sem("ffn_weights_high")
        w_split = m.sem("ffn_weights_split")
        xh_ready = m.sem("ffn_mixT_high")
        xl_ready = m.sem("ffn_mixT_split")
        kh_ready = m.sem("ffn_hidden_high")
        kl_ready = m.sem("ffn_hidden_split")
        gaps = m.sem("ffn_gaps_cleared")
        x_loaded = [m.sem(f"ffn_mix_loaded{u}") for u in range(2)]
        t_loaded = [m.sem(f"ffn_tok_loaded{u}") for u in range(2)]
        zt_ready = m.sem("ffn_mixT_in_psum")
        r_ready = m.sem("ffn_r_in_psum")
        h_ready = m.sem("ffn_hidden_in_psum")
        g_ready = m.sem("ffn_gate_ready")
        relu_done = m.sem("ffn_hidden_clipped")
        kk_ready = m.sem("ffn_hidden_squared")
        tt_ready = m.sem("ffn_tokT_in_psum")
        v_ready = m.sem("ffn_out_in_psum")
        gv_done = m.sem("ffn_out_gated")
        res_done = m.sem("result_ready")
        stored = [m.sem(f"result_stored{u}") for u in range(2)]
        block = ctx.enter_context(nc.Block())
        CH = 2 * NCH

        @block.tensor
        def _(pe):
            pe.wait_ge(w_split, 3)
            pe.wait_ge(gaps, 4)
            pe.sem_inc(h_ready, 2 * HT)
            pe.sem_inc(v_ready, 2 * KT)

            def turn(i, n, src, banks, free_sem, ready):
                u, t = n // NCH % 2, n % NCH
                for ct in range(KT):
                    pe.wait_ge(free_sem, i * (CH * KT) + (KT * n + ct + 1))
                    for jj in range(JC):
                        tr = pe.transpose(banks[ct][0:CT, jj * PXP:(jj + 1) * PXP],
                                          src[u][:, ct * CT:(ct + 1) * CT, JC * t + jj], keep.ident[:, :])
                    tr.then_inc(ready, 1)

            def images(i, last):
                for n in range(CH):
                    pe.wait_ge(xl_ready, i * (CH * KT) + (KT * n + 2 * KT))
                    for a in range(KT + HT):
                        if a < KT:
                            if a == 0:
                                pe.wait_ge(relu_done, i * (CH * HT) + (HT * n + HT - 1 + 2))
                            else:
                                pe.wait_ge(relu_done, i * (CH * HT) + (HT * n + HT + 2))
                            w, part, M = wr_parts, slice(a * CT, (a + 1) * CT), CT
                        else:
                            h = a - KT
                            if h < 2:
                                pe.wait_ge(g_ready, i * (CH * KT) + (KT * n + h + 1))
                            else:
                                pe.wait_ge(relu_done, i * (CH * HT) + (HT * (n + 1) + h - 1 + 2))
                            w, part, M = wk_parts, slice(h * 128, (h + 1) * 128), 128
                        for k in range(KT):
                            mm = split_matmul(pe, h_ps[a % 2][0:M, 0:TC], [x[:, k, part] for x in w],
                                              [x[:, k, :] for x in xT[n % 2]], k == 0, k == KT - 1)
                        mm.then_inc(r_ready if a < KT else h_ready, 1)
                    if n + 1 < CH or not last:
                        if (n + 1) % NCH == 0:
                            pe.wait_ge(x_loaded[(n + 1) // NCH % 2], i * 32 + (32 if n + 1 < CH else 64))
                        turn(i, n + 1, X, z_ps, xl_ready, zt_ready)
                    if n % NCH == 0:
                        pe.wait_ge(t_loaded[n // NCH], i * 32 + 32)
                    turn(i, n, T, t_ps, res_done, tt_ready)
                    for h in range(HT):
                        pe.wait_ge(kl_ready, i * (CH * HT) + (HT * n + h + 1 + KW))
                        for ct in range(KT):
                            if h == 0:
                                pe.wait_ge(gv_done, i * (CH * KT) + (KT * n + ct + 1))
                            mm = split_matmul(pe, v_ps[ct][0:CT, 0:TC],
                                              [x[:, h, ct * CT:(ct + 1) * CT] for x in wv_parts],
                                              [x[:, h, :] for x in kk[n % 2]], h == 0, h == HT - 1)
                            if h == HT - 1:
                                mm.then_inc(v_ready, 1)

            pe.wait_ge(x_loaded[0], 32)
            turn(0, 0, X, z_ps, xl_ready, zt_ready)
            with pe.Fori(0, B // 2 - 1) as i:
                images(i, False)
            images(B // 2 - 1, True)

        @block.scalar
        def _(act):
            act.wait_ge(w_loaded, 64)
            for w, parts in ((wk, wk_parts), (wr, wr_parts), (wv, wv_parts)):
                if w is wv:
                    act.wait_ge(w_folded, HT)
                act.activation(rounded(parts[0][:, :, :]), w[:, :, :], ACT.Copy).then_inc(w_high, 1)

            def mix(i, n):
                act.wait_ge(h_ready, i * (CH * HT) + HT * (n + 1))
                for ct in range(KT):
                    act.wait_ge(zt_ready, i * (CH * KT) + (KT * n + ct + 1))
                    act.activation(rounded(by_pixel(xT[n % 2][0][:, ct, :])),
                                   transposed(z_ps[ct], reverse=True), ACT.Copy).then_inc(xh_ready, 1)

            def high_of_hidden(i, n, h):
                act.wait_ge(kk_ready, i * (CH * HT) + (HT * n + h + 1))
                act.activation(rounded(kk[n % 2][0][:, h, :]), whole[h % KW][:, :], ACT.Copy
                               ).then_inc(kh_ready, 1)

            def images(i, last):
                for n in range(CH):
                    for ct in range(KT):
                        act.wait_ge(gv_done, i * (CH * KT) + (KT * n + 1))
                        act.wait_ge(r_ready, i * (CH * KT) + (KT * n + ct + 1))
                        act.activation(sg[n % 2][:, ct, :], h_ps[ct][0:CT, 0:TC], ACT.Sigmoid
                                       ).then_inc(g_ready, 1)
                    act.wait_ge(v_ready, i * (CH * KT) + KT * (n + 1))
                    for h in range(HT):
                        act.wait_ge(relu_done, i * (CH * HT) + (HT * (n + 1) + h + 1 + 2))
                        act.activation(whole[h % KW][:, :], whole[h % KW][:, :], ACT.Square).then_inc(kk_ready, 1)
                        high_of_hidden(i, n, h)
                    if n + 1 < CH or not last:
                        mix(i, n + 1)

            mix(0, 0)
            with act.Fori(0, B // 2 - 1) as i:
                images(i, False)
            images(B // 2 - 1, True)

        @block.gpsimd
        def _(pool):
            for t in (*X, *T):
                pool.memset(t[:, :, :], 0.0).then_inc(gaps, 1)
            for n, (w, parts) in enumerate(((wk, wk_parts), (wr, wr_parts), (wv, wv_parts))):
                pool.wait_ge(w_high, n + 1)
                pool.tensor_tensor(rounded(parts[1][:, :, :]), w[:, :, :], parts[0][:, :, :], ALU.subtract
                                   ).then_inc(w_split, 1)
            pool.sem_inc(kl_ready, KW)

            def images(i, last):
                for n in range(CH):
                    for h in range(HT):
                        pool.wait_ge(kh_ready, i * (CH * HT) + (HT * n + h + 1))
                        pool.tensor_tensor(rounded(kk[n % 2][1][:, h, :]), whole[h % KW][:, :],
                                           kk[n % 2][0][:, h, :], ALU.subtract).then_inc(kl_ready, 1)

            with pool.Fori(0, B // 2 - 1) as i:
                images(i, False)
            images(B // 2 - 1, True)

        @block.vector
        def _(dve):
            dve.wait_ge(w_loaded, 64)
            for h in range(HT):
                dve.tensor_mul(wv[:, h, :], wv[:, h, :], gam[:, :]).then_inc(w_folded, 1)
            dve.sem_inc(relu_done, HT + 2)
            dve.sem_inc(gv_done, KT)
            dve.sem_inc(res_done, KT)
            dve.sem_inc(xl_ready, KT)
            for u in range(2):
                dve.sem_inc(stored[u], 16)

            def rest_of_mix(i, n):
                for ct in range(KT):
                    dve.wait_ge(xh_ready, i * (CH * KT) + (KT * n + ct + 1))
                    dve.tensor_tensor(rounded(by_pixel(xT[n % 2][1][:, ct, :])), transposed(z_ps[ct], reverse=True),
                                      by_pixel(xT[n % 2][0][:, ct, :]), ALU.subtract).then_inc(xl_ready, 1)

            def images(i, last):
                for n in range(CH):
                    for h in range(HT):
                        dve.wait_ge(kl_ready, i * (CH * HT) + (HT * n + h + 1))
                        dve.wait_ge(h_ready, i * (CH * HT) + (HT * (n + 2) + h + 1))
                        bank = h_ps[h % 2][:, 0:TC]
                        dve.tensor_scalar_max(whole[h % KW][:, :], bank, 0.0).then_inc(relu_done, 1)
                    if n + 1 < CH or not last:
                        rest_of_mix(i, n + 1)
                    for ct in range(KT):
                        dve.wait_ge(v_ready, i * (CH * KT) + (KT * (n + 2) + ct + 1))
                        dve.wait_ge(g_ready, i * (CH * KT) + (KT * n + ct + 1))
                        dve.tensor_mul(gv[:, ct, :], v_ps[ct][0:CT, 0:TC], sg[n % 2][:, ct, :]
                                       ).then_inc(gv_done, 1)
                    for ct in range(KT):
                        if ct == 0:
                            dve.wait_ge(stored[n % 2], i * (16 * NCH) + 16 * (n // 2 + 1))
                        dve.wait_ge(gv_done, i * (CH * KT) + (KT * (n + 1) + ct + 1))
                        dve.wait_ge(tt_ready, i * (CH * KT) + (KT * n + ct + 1))
                        dve.tensor_tensor(by_pixel(res[n % 2][:, ct, :]), by_pixel(gv[:, ct, :]),
                                          transposed(t_ps[ct]), ALU.add).then_inc(res_done, 1)

            rest_of_mix(0, 0)
            with dve.Fori(0, B // 2 - 1) as i:
                images(i, False)
            images(B // 2 - 1, True)

        @block.sync
        def _(sp):
            for dst, src in [(wk, ins["ffn_wkt"].rearrange("(k p) n -> p k n", p=CT)),
                             (wv, ins["ffn_wvt"].rearrange("(k p) n -> p k n", p=128)),
                             (wr, ins["ffn_wrt"].rearrange("(k p) n -> p k n", p=CT))]:
                sp.dma_start(dst[:, :, :], src).then_inc(w_loaded, 16)
            sp.dma_start(gam[:, :], dram(ins["vecs"], V["gamma2"] * C, [[0, 128], [1, C]])).then_inc(w_loaded, 16)

            def load(b, u):
                copy_pairs(sp, by_group(X[u]), pair_batch(mix_d, B, b), x_loaded[u])
                copy_pairs(sp, by_group(T[u]), pair_batch(tok_d, B, b), t_loaded[u])

            def images(i, reload):
                for n in range(CH):
                    u, t = n // NCH, n % NCH
                    at = i * (2 * C * HW) + (u * C * HW + t * TC)
                    if reload:
                        at = sp.snap(at)
                    sp.wait_ge(res_done, i * (CH * KT) + (KT * (n + 2)))
                    sp.dma_start(dram(out, at, [[HW, CT], [CT * HW, KT], [1, TC]]), res[n % 2][:, :, :]
                                 ).then_inc(stored[n % 2], 16)
                    if t == NCH - 1 and reload:
                        load(i * 2 + (u + 2), u)

            sp.wait_ge(gaps, 4)
            load(0, 0)
            load(1, 1)
            with sp.Fori(0, B // 2 - 1) as i:
                images(i, True)
            images(B // 2 - 1, False)
            for u in range(2):
                sp.wait_ge(stored[u], 16 * (NCH * (B // 2) + 1))


class Kept:

    def __init__(self, m):
        self.ident = m.sb("identity", [PXP, PXP])
        self.wkvr = m.sb("kvr_weights", [CT, KT, 3, C])
        self.wo = m.sb("attention_out_weights", [CT, KT, C])
        self.decay = m.sb("wkv_decay", [CT, KT, 2])
        self.bonus = m.sb("wkv_bonus", [CT, KT, 2])


def build(nc, B, ins, out, debug=None):
    scratch = lambda name, shape: (debug or {}).get(name) or nc.dram_tensor(name, shape, F32).ap()
    pair_shape = [NG, PXC, B, G * PJ]
    xpw_d = scratch("x_pointwise", pair_shape)
    y_d = scratch("y_gelu", pair_shape)
    mixa_d = scratch("att_mix", pair_shape)
    tok_d = scratch("tok", pair_shape)
    mixf_d = scratch("ffn_mix", pair_shape)
    f13_d = scratch("flat13", [C, band(K13)[2]])
    f5a_d = scratch("flat5_att", [C, band(K5)[2]])
    f5f_d = scratch("flat5_ffn", [C, band(K5)[2]])
    bias_d = scratch("dw_bias", [1, C])
    s1_d = scratch("tok_sums", [PXC, B * PJ])
    s2_d = scratch("tok_square_sums", [PXC, B * PJ])
    with ExitStack() as ctx:
        m = Mem(nc, ctx)
        keep = Kept(m)
        with ExitStack() as inner:
            mi = Mem(nc, inner)
            wpw, shift_pw = mi.sb("pointwise_weights", [CT, KT, C]), mi.sb("pointwise_shift", [128, C])
            prepare(nc, ins, keep, wpw, shift_pw, f13_d, f5a_d, f5f_d, bias_d)
            pointwise(nc, B, ins["x"], wpw, shift_pw, xpw_d)
        with ExitStack() as inner:
            mi = Mem(nc, inner)
            s1, s2 = mi.sb("y_sum", [PXP, B * PJ]), mi.sb("y_square_sum", [PXP, B * PJ])
            depthwise(nc, B, "dw13", xpw_d, PXC, K13, f13_d, y_d, "gelu", bias_d=bias_d, stats=(s1, s2),
                      flipped=True)
            norm_scales(nc, "ln1", s1, s2)
            depthwise(nc, B, "omni1", y_d, PXP, K5, f5a_d, mixa_d, "copy", norm="ln1_g",
                      vecs=ins["vecs"], stats=(s2, s1))
        attention(nc, B, keep, mixa_d, y_d, tok_d, s1_d, s2_d)
        with ExitStack() as inner:
            mi = Mem(nc, inner)
            s1, s2 = mi.sb("t_sum", [PXP, B * PJ]), mi.sb("t_square_sum", [PXP, B * PJ])
            norm_scales(nc, "ln2", s1, s2, s1_d, s2_d)
            depthwise(nc, B, "omni2", tok_d, PXP, K5, f5f_d, mixf_d, "copy", norm="ln2_g",
                      vecs=ins["vecs"], stats=(s2, s1))
        feed_forward(nc, B, ins, keep, mixf_d, tok_d, out)


def layout(inputs):
    import numpy as np

    i = {k: np.asarray(v) for k, v in inputs.items()}
    l0, l1 = (lambda n: i["L0_conv_" + n]), (lambda n: i["L1_conv_" + n])
    vec = {n: l0(n) for n in VEC if n.startswith(("pw_", "dwk_", "dw1_"))}
    vec.update({n: l1(n) for n in VEC if n.startswith(("ln", "gamma"))})
    for n in range(2):
        vec[f"dec{n}"], vec[f"first{n}"] = l1("sp_decay")[n], l1("sp_first")[n]
    vecs = np.stack([vec[n] for n in VEC])
    plain = lambda w: np.ascontiguousarray(w[:, 0]).reshape(C, -1)
    flip = lambda w: np.ascontiguousarray(w[:, 0, ::-1, ::-1]).reshape(C, -1)
    x = i["x"]
    pairs = x.reshape(*x.shape[:2], PJ, 2, W)[:, :, :, ::-1, ::-1]
    cols = lambda a: np.ascontiguousarray(a.reshape(KT, CT).T)
    t = lambda a: np.ascontiguousarray(a.T)
    return {
        "x": np.ascontiguousarray(pairs).reshape(x.shape),
        "vecs": vecs,
        "vec_cols": np.ascontiguousarray(vecs.reshape(NV, KT, CT).transpose(2, 1, 0)),
        "alphas": np.concatenate([l1("att_alpha"), l1("ffn_alpha")]),
        "ident": np.eye(PXP, dtype=np.float32),
        "pw_wt": t(l0("pw_w")),
        "dwk_w": flip(l0("dwk_w")),
        "att_w5": plain(l1("att_w5")), "att_w3": plain(l1("att_w3")), "att_w1": cols(l1("att_w1")),
        "ffn_w5": plain(l1("ffn_w5")), "ffn_w3": plain(l1("ffn_w3")), "ffn_w1": cols(l1("ffn_w1")),
        "att_wt": np.stack([t(l1("att_wk")), t(l1("att_wv")), t(l1("att_wr"))]),
        "att_wot": t(l1("att_wo")),
        "ffn_wkt": t(l1("ffn_wk")), "ffn_wvt": t(l1("ffn_wv")), "ffn_wrt": t(l1("ffn_wr")),
    }


def kernel(**inputs):
    import concourse.bacc as bacc
    from concourse.bass_utils import run_bass_kernel_spmd

    arrays = layout(inputs)
    B = arrays["x"].shape[0]
    nc = bacc.Bacc("TRN2", target_bir_lowering=False, num_devices=1)
    ins = {n: nc.dram_tensor(n, a.shape, mybir.dt.from_np(a.dtype), kind="ExternalInput").ap()
           for n, a in arrays.items()}
    out = nc.dram_tensor("out", [B, C, W, W], F32, kind="ExternalOutput").ap()
    build(nc, B, ins, out)
    return run_bass_kernel_spmd(nc, [arrays], core_ids=[0]).results[0]["out"]
```
